# Optimizing a Trainium2 kernel written in Bass

```python
import numpy as np
import jax
import jax.numpy as jnp

def _softmax(x, axis=-1):
    return jax.nn.softmax(x, axis=axis)

def _gelu(x):
    return jax.nn.gelu(x, approximate=True)

def _silu(x):
    return jax.nn.silu(x)

def _sigmoid(x):
    return jax.nn.sigmoid(x)

def _layernorm(x, axis=-1, eps=1e-05):
    m = jnp.mean(x, axis=axis, keepdims=True)
    v = jnp.var(x, axis=axis, keepdims=True)
    return (x - m) / jnp.sqrt(v + eps)

def _scatter_add(tgt, idx, src, axis=0):
    return tgt.at[idx].add(src)

def _segment_sum(src, seg, n):
    return jax.ops.segment_sum(src, seg, n)
kernel_name = 'mk_vit_tower_d1_tok_img768_r4_fa77d7'

def setup_inputs(seed: int=0):
    np.random.seed(seed)
    _w = jnp.asarray

    def _rec_inputs():
        import jax
        import jax.numpy as jnp
        _rk = jax.random.key(seed)
        x = -0.000356955 + 1 * jax.random.normal(jax.random.fold_in(_rk, 1), (128, 3, 224, 224), jnp.float32)
        return x
    x = _rec_inputs()

    def _L0_tok_setup():
        import jax, jax.numpy as jnp
        import numpy as np
        N_PATCHES = 14
        HIDDEN_D = 192
        N_HEADS = 12
        D_HEAD = HIDDEN_D // N_HEADS
        SEQ = N_PATCHES ** 2 + 1
        INPUT_D = 3 * 16 * 16
        LN_EPS = 1e-05

        def positional_embeddings(seq_len, d):
            i = jnp.arange(seq_len, dtype=jnp.float32)[:, None]
            j = jnp.arange(d, dtype=jnp.float32)[None, :]
            even = (jnp.arange(d) % 2 == 0)[None, :]
            denom_even = jnp.power(10000.0, j / d)
            denom_odd = jnp.power(10000.0, (j - 1.0) / d)
            return jnp.where(even, jnp.sin(i / denom_even), jnp.cos(i / denom_odd))

        def _forward(images, W_map, b_map, class_token, ln_w, ln_b, Wq, bq, Wk, bk, Wv, bv):
            n = images.shape[0]
            patches = images.reshape(n, N_PATCHES ** 2, INPUT_D)
            tokens = jnp.einsum('npi,di->npd', patches, W_map) + b_map
            cls = jnp.broadcast_to(class_token[None], (n, 1, HIDDEN_D))
            tokens = jnp.concatenate([cls, tokens], axis=1)
            tokens = tokens + positional_embeddings(SEQ, HIDDEN_D)[None]
            mean = jnp.mean(tokens, axis=(-2, -1), keepdims=True)
            var = jnp.var(tokens, axis=(-2, -1), keepdims=True)
            x = (tokens - mean) / jnp.sqrt(var + LN_EPS) * ln_w + ln_b
            xh = x.reshape(n, SEQ, N_HEADS, D_HEAD)
            q = jnp.einsum('bshd,hed->bshe', xh, Wq) + bq[None, None]
            k = jnp.einsum('bshd,hed->bshe', xh, Wk) + bk[None, None]
            v = jnp.einsum('bshd,hed->bshe', xh, Wv) + bv[None, None]
            att = jax.nn.softmax(jnp.einsum('bshd,bthd->bhst', q, k) / jnp.sqrt(jnp.float32(D_HEAD)), axis=-1)
            msa = jnp.einsum('bhst,bthd->bshd', att, v).reshape(n, SEQ, HIDDEN_D)
            return tokens + msa
        key = jax.random.key(seed)
        ks = jax.random.split(key, 12)
        s = 0.02
        return {'images': jax.random.normal(ks[0], (128, 3, 224, 224), dtype=jnp.float32), 'W_map': jax.random.normal(ks[1], (HIDDEN_D, INPUT_D), dtype=jnp.float32) * s, 'b_map': jax.random.normal(ks[2], (HIDDEN_D,), dtype=jnp.float32) * s, 'class_token': jax.random.uniform(ks[3], (1, HIDDEN_D), dtype=jnp.float32), 'ln_w': jnp.ones((SEQ, HIDDEN_D), dtype=jnp.float32), 'ln_b': jnp.zeros((SEQ, HIDDEN_D), dtype=jnp.float32), 'Wq': jax.random.normal(ks[4], (N_HEADS, D_HEAD, D_HEAD), dtype=jnp.float32) * s, 'bq': jax.random.normal(ks[5], (N_HEADS, D_HEAD), dtype=jnp.float32) * s, 'Wk': jax.random.normal(ks[6], (N_HEADS, D_HEAD, D_HEAD), dtype=jnp.float32) * s, 'bk': jax.random.normal(ks[7], (N_HEADS, D_HEAD), dtype=jnp.float32) * s, 'Wv': jax.random.normal(ks[8], (N_HEADS, D_HEAD, D_HEAD), dtype=jnp.float32) * s, 'bv': jax.random.normal(ks[9], (N_HEADS, D_HEAD), dtype=jnp.float32) * s}
    _L0_tok_all = _L0_tok_setup()
    _L0_tok_in = {k: v for k, v in _L0_tok_all.items() if k in ('W_map', 'b_map', 'class_token', 'ln_w', 'ln_b', 'Wq', 'bq', 'Wk', 'bk', 'Wv', 'bv')}
    del _L0_tok_all

    def _L0_attn_setup():
        import jax, jax.numpy as jnp
        import numpy as np
        B, N, C = (16, 1024, 192)
        H = 12
        D = C // H
        SCALE = D ** (-0.5)
        key = jax.random.key(seed)
        k1, k2, k3, k4 = jax.random.split(key, 4)
        x = jax.random.normal(k1, (B, N, C), dtype=jnp.float32)
        w_qkv = jax.random.normal(k2, (C, 3 * C), dtype=jnp.float32) * 0.02
        w_proj = jax.random.normal(k3, (C, C), dtype=jnp.float32) * 0.02
        b_proj = jax.random.normal(k4, (C,), dtype=jnp.float32) * 0.02
        return {'x': x, 'w_qkv': w_qkv, 'w_proj': w_proj, 'b_proj': b_proj}
    _L0_attn_all = _L0_attn_setup()
    _L0_attn_in = {k: v for k, v in _L0_attn_all.items() if k in ('w_qkv', 'w_proj', 'b_proj')}
    del _L0_attn_all

    def _L0_ffn_setup():
        import jax, jax.numpy as jnp
        import numpy as np
        H = 192
        I = 96
        E = 16
        G = 4
        TOPK_GROUP = 2
        TOP_K = 4
        SCALE = 2.5
        N_SHARED = 2
        IS = I * N_SHARED
        B, S = (1, 512)

        def _route(x, router_w, router_b, corr_bias):
            logits = x.astype(jnp.float32) @ router_w.T + router_b
            scores = jax.nn.sigmoid(logits)
            sfc = scores + corr_bias[None, :]
            grp = sfc.reshape(-1, G, E // G)
            group_scores = jax.lax.top_k(grp, 2)[0].sum(-1)
            _, gidx = jax.lax.top_k(group_scores, TOPK_GROUP)
            gmask = jax.nn.one_hot(gidx, G, dtype=sfc.dtype).sum(axis=1)
            score_mask = jnp.repeat(gmask, E // G, axis=-1)
            sfc = jnp.where(score_mask > 0, sfc, 0.0)
            _, idx = jax.lax.top_k(sfc, TOP_K)
            w = jnp.take_along_axis(scores, idx, axis=1)
            w = w / (w.sum(-1, keepdims=True) + 1e-20)
            return (idx, w * SCALE)

        def _forward(x3, router_w, router_b, corr_bias, gWg, gbg, gWu, gbu, gWd, gbd, sWg, sbg, sWu, sbu, sWd, sbd):
            orig_shape = x3.shape
            x = x3.reshape(-1, H)
            idx, w = _route(x, router_w, router_b, corr_bias)
            c = (jax.nn.one_hot(idx, E, dtype=w.dtype) * w[..., None]).sum(1)
            h = jax.nn.silu(jnp.einsum('th,ehi->tei', x, gWg) + gbg) * (jnp.einsum('th,ehi->tei', x, gWu) + gbu)
            out_e = jnp.einsum('tei,eih->teh', h, gWd) + gbd
            moe_out = jnp.einsum('te,teh->th', c, out_e)
            hs = jax.nn.silu(x @ sWg + sbg) * (x @ sWu + sbu)
            shared = hs @ sWd + sbd
            return (moe_out + shared).reshape(orig_shape)
        key = jax.random.key(seed)
        ks = jax.random.split(key, 16)
        s = lambda k, shape, fan: jax.random.normal(k, shape, jnp.float32) * fan ** (-0.5)
        return {'hidden_states': jax.random.normal(ks[0], (B, S, H), jnp.float32), 'router_w': s(ks[1], (E, H), H), 'router_b': jnp.zeros((E,), jnp.float32), 'corr_bias': jnp.zeros((E,), jnp.float32), 'gWg': s(ks[2], (E, H, I), H), 'gbg': jnp.zeros((E, I), jnp.float32), 'gWu': s(ks[3], (E, H, I), H), 'gbu': jnp.zeros((E, I), jnp.float32), 'gWd': s(ks[4], (E, I, H), I), 'gbd': jnp.zeros((E, H), jnp.float32), 'sWg': s(ks[5], (H, IS), H), 'sbg': jnp.zeros((IS,), jnp.float32), 'sWu': s(ks[6], (H, IS), H), 'sbu': jnp.zeros((IS,), jnp.float32), 'sWd': s(ks[7], (IS, H), IS), 'sbd': jnp.zeros((H,), jnp.float32)}
    _L0_ffn_all = _L0_ffn_setup()
    _L0_ffn_in = {k: v for k, v in _L0_ffn_all.items() if k in ('router_w', 'router_b', 'corr_bias', 'gWg', 'gbg', 'gWu', 'gbu', 'gWd', 'gbd', 'sWg', 'sbg', 'sWu', 'sbu', 'sWd', 'sbd')}
    del _L0_ffn_all
    return {'x': x, 'L0_tok_W_map': _L0_tok_in['W_map'], 'L0_tok_b_map': _L0_tok_in['b_map'], 'L0_tok_class_token': _L0_tok_in['class_token'], 'L0_tok_ln_w': _L0_tok_in['ln_w'], 'L0_tok_ln_b': _L0_tok_in['ln_b'], 'L0_tok_Wq': _L0_tok_in['Wq'], 'L0_tok_bq': _L0_tok_in['bq'], 'L0_tok_Wk': _L0_tok_in['Wk'], 'L0_tok_bk': _L0_tok_in['bk'], 'L0_tok_Wv': _L0_tok_in['Wv'], 'L0_tok_bv': _L0_tok_in['bv'], 'L0_attn_w_qkv': _L0_attn_in['w_qkv'], 'L0_attn_w_proj': _L0_attn_in['w_proj'], 'L0_attn_b_proj': _L0_attn_in['b_proj'], 'L0_ffn_router_w': _L0_ffn_in['router_w'], 'L0_ffn_router_b': _L0_ffn_in['router_b'], 'L0_ffn_corr_bias': _L0_ffn_in['corr_bias'], 'L0_ffn_gWg': _L0_ffn_in['gWg'], 'L0_ffn_gbg': _L0_ffn_in['gbg'], 'L0_ffn_gWu': _L0_ffn_in['gWu'], 'L0_ffn_gbu': _L0_ffn_in['gbu'], 'L0_ffn_gWd': _L0_ffn_in['gWd'], 'L0_ffn_gbd': _L0_ffn_in['gbd'], 'L0_ffn_sWg': _L0_ffn_in['sWg'], 'L0_ffn_sbg': _L0_ffn_in['sbg'], 'L0_ffn_sWu': _L0_ffn_in['sWu'], 'L0_ffn_sbu': _L0_ffn_in['sbu'], 'L0_ffn_sWd': _L0_ffn_in['sWd'], 'L0_ffn_sbd': _L0_ffn_in['sbd']}

def reference(x, L0_tok_W_map, L0_tok_b_map, L0_tok_class_token, L0_tok_ln_w, L0_tok_ln_b, L0_tok_Wq, L0_tok_bq, L0_tok_Wk, L0_tok_bk, L0_tok_Wv, L0_tok_bv, L0_attn_w_qkv, L0_attn_w_proj, L0_attn_b_proj, L0_ffn_router_w, L0_ffn_router_b, L0_ffn_corr_bias, L0_ffn_gWg, L0_ffn_gbg, L0_ffn_gWu, L0_ffn_gbu, L0_ffn_gWd, L0_ffn_gbd, L0_ffn_sWg, L0_ffn_sbg, L0_ffn_sWu, L0_ffn_sbu, L0_ffn_sWd, L0_ffn_sbd):
    import jax
    import jax.numpy as jnp

    def _L0_tok_ref(images, W_map, b_map, class_token, ln_w, ln_b, Wq, bq, Wk, bk, Wv, bv):
        import jax, jax.numpy as jnp
        import numpy as np
        N_PATCHES = 14
        HIDDEN_D = 192
        N_HEADS = 12
        D_HEAD = HIDDEN_D // N_HEADS
        SEQ = N_PATCHES ** 2 + 1
        INPUT_D = 3 * 16 * 16
        LN_EPS = 1e-05

        def positional_embeddings(seq_len, d):
            i = jnp.arange(seq_len, dtype=jnp.float32)[:, None]
            j = jnp.arange(d, dtype=jnp.float32)[None, :]
            even = (jnp.arange(d) % 2 == 0)[None, :]
            denom_even = jnp.power(10000.0, j / d)
            denom_odd = jnp.power(10000.0, (j - 1.0) / d)
            return jnp.where(even, jnp.sin(i / denom_even), jnp.cos(i / denom_odd))

        def _forward(images, W_map, b_map, class_token, ln_w, ln_b, Wq, bq, Wk, bk, Wv, bv):
            n = images.shape[0]
            patches = images.reshape(n, N_PATCHES ** 2, INPUT_D)
            tokens = jnp.einsum('npi,di->npd', patches, W_map) + b_map
            cls = jnp.broadcast_to(class_token[None], (n, 1, HIDDEN_D))
            tokens = jnp.concatenate([cls, tokens], axis=1)
            tokens = tokens + positional_embeddings(SEQ, HIDDEN_D)[None]
            mean = jnp.mean(tokens, axis=(-2, -1), keepdims=True)
            var = jnp.var(tokens, axis=(-2, -1), keepdims=True)
            x = (tokens - mean) / jnp.sqrt(var + LN_EPS) * ln_w + ln_b
            xh = x.reshape(n, SEQ, N_HEADS, D_HEAD)
            q = jnp.einsum('bshd,hed->bshe', xh, Wq) + bq[None, None]
            k = jnp.einsum('bshd,hed->bshe', xh, Wk) + bk[None, None]
            v = jnp.einsum('bshd,hed->bshe', xh, Wv) + bv[None, None]
            att = jax.nn.softmax(jnp.einsum('bshd,bthd->bhst', q, k) / jnp.sqrt(jnp.float32(D_HEAD)), axis=-1)
            msa = jnp.einsum('bhst,bthd->bshd', att, v).reshape(n, SEQ, HIDDEN_D)
            return tokens + msa
        return _forward(images, W_map, b_map, class_token, ln_w, ln_b, Wq, bq, Wk, bk, Wv, bv)

    def _L0_attn_ref(x, w_qkv, w_proj, b_proj):
        import jax, jax.numpy as jnp
        import numpy as np
        B, N, C = (16, 1024, 192)
        H = 12
        D = C // H
        SCALE = D ** (-0.5)
        b, n, c = x.shape
        qkv = (x @ w_qkv).reshape(b, n, 3, H, D).transpose(2, 0, 3, 1, 4)
        q, k, v = (qkv[0], qkv[1], qkv[2])
        kv = jnp.einsum('bhnd,bhne->bhde', k, v) * SCALE
        gq = jax.nn.gelu(q, approximate=False)
        gkv = jax.nn.gelu(kv, approximate=False)
        out = jnp.einsum('bhtd,bhde->bhte', gq, gkv)
        out = out.transpose(0, 2, 1, 3).reshape(b, n, c)
        return out @ w_proj + b_proj

    def _L0_ffn_ref(hidden_states, router_w, router_b, corr_bias, gWg, gbg, gWu, gbu, gWd, gbd, sWg, sbg, sWu, sbu, sWd, sbd):
        import jax, jax.numpy as jnp
        import numpy as np
        H = 192
        I = 96
        E = 16
        G = 4
        TOPK_GROUP = 2
        TOP_K = 4
        SCALE = 2.5
        N_SHARED = 2
        IS = I * N_SHARED
        B, S = (1, 512)

        def _route(x, router_w, router_b, corr_bias):
            logits = x.astype(jnp.float32) @ router_w.T + router_b
            scores = jax.nn.sigmoid(logits)
            sfc = scores + corr_bias[None, :]
            grp = sfc.reshape(-1, G, E // G)
            group_scores = jax.lax.top_k(grp, 2)[0].sum(-1)
            _, gidx = jax.lax.top_k(group_scores, TOPK_GROUP)
            gmask = jax.nn.one_hot(gidx, G, dtype=sfc.dtype).sum(axis=1)
            score_mask = jnp.repeat(gmask, E // G, axis=-1)
            sfc = jnp.where(score_mask > 0, sfc, 0.0)
            _, idx = jax.lax.top_k(sfc, TOP_K)
            w = jnp.take_along_axis(scores, idx, axis=1)
            w = w / (w.sum(-1, keepdims=True) + 1e-20)
            return (idx, w * SCALE)

        def _forward(x3, router_w, router_b, corr_bias, gWg, gbg, gWu, gbu, gWd, gbd, sWg, sbg, sWu, sbu, sWd, sbd):
            orig_shape = x3.shape
            x = x3.reshape(-1, H)
            idx, w = _route(x, router_w, router_b, corr_bias)
            c = (jax.nn.one_hot(idx, E, dtype=w.dtype) * w[..., None]).sum(1)
            h = jax.nn.silu(jnp.einsum('th,ehi->tei', x, gWg) + gbg) * (jnp.einsum('th,ehi->tei', x, gWu) + gbu)
            out_e = jnp.einsum('tei,eih->teh', h, gWd) + gbd
            moe_out = jnp.einsum('te,teh->th', c, out_e)
            hs = jax.nn.silu(x @ sWg + sbg) * (x @ sWu + sbu)
            shared = hs @ sWd + sbd
            return (moe_out + shared).reshape(orig_shape)
        return _forward(hidden_states, router_w, router_b, corr_bias, gWg, gbg, gWu, gbu, gWd, gbd, sWg, sbg, sWu, sbu, sWd, sbd)
    h = _L0_tok_ref(x, L0_tok_W_map, L0_tok_b_map, L0_tok_class_token, L0_tok_ln_w, L0_tok_ln_b, L0_tok_Wq, L0_tok_bq, L0_tok_Wk, L0_tok_bk, L0_tok_Wv, L0_tok_bv)
    h = h + _L0_attn_ref(_layernorm(h, axis=-1), L0_attn_w_qkv, L0_attn_w_proj, L0_attn_b_proj)
    h = h + _L0_ffn_ref(_layernorm(h, axis=-1), L0_ffn_router_w, L0_ffn_router_b, L0_ffn_corr_bias, L0_ffn_gWg, L0_ffn_gbg, L0_ffn_gWu, L0_ffn_gbu, L0_ffn_gWd, L0_ffn_gbd, L0_ffn_sWg, L0_ffn_sbg, L0_ffn_sWu, L0_ffn_sbu, L0_ffn_sWd, L0_ffn_sbd)
    return h

_drawn_inputs = setup_inputs


def setup_inputs(seed=0):
    import zlib

    import numpy as np

    out = dict(_drawn_inputs(seed))
    spreads = {'L0_tok_ln_w': (1.0, 0.2),
     'L0_tok_ln_b': (0.0, 0.447),
     'L0_ffn_router_b': (0.0, 0.1),
     'L0_ffn_corr_bias': (0.0, 0.1),
     'L0_ffn_gbg': (0.0, 0.1),
     'L0_ffn_gbu': (0.0, 0.1),
     'L0_ffn_gbd': (0.0, 0.1),
     'L0_ffn_sbg': (0.0, 0.1),
     'L0_ffn_sbu': (0.0, 0.1),
     'L0_ffn_sbd': (0.0, 0.1)}
    factors = {'L0_tok_Wq': 8.0, 'L0_tok_bq': 8.0, 'L0_tok_Wk': 7.264, 'L0_tok_bk': 8.0}
    for name, (base, spread) in spreads.items():
        noise = np.random.default_rng([zlib.crc32(name.encode()), seed]).standard_normal(out[name].shape)
        drawn = base * np.exp(spread * noise) if base else spread * noise
        out[name] = jnp.asarray(drawn.astype(out[name].dtype))
    for name, factor in factors.items():
        out[name] = (out[name] * factor).astype(out[name].dtype)
    return out
```

```python
from contextlib import ExitStack

import concourse.bass as bass
from concourse import mybir

F32 = mybir.dt.float32
F16 = mybir.dt.float16
I32 = mybir.dt.int32
ALU = mybir.AluOpType
ACT = mybir.ActivationFunctionType
AX = mybir.AxisListType

IMAGES, PATCHES, PATCH_IN = 128, 196, 768
C, HEADS, DH = 192, 12, 16
SEQ = PATCHES + 1
TR = 100
TC = 2 * TR
PT = 2 * TC
LIVE = (TR, SEQ - TR)
EXPERTS, INNER, GROUPS = 16, 96, 4
UNITS = 14
ROUTED = EXPERTS * INNER // 128
UNIT_ROWS = [128] * 13 + [64]
HID = EXPERTS * INNER + 2 * INNER
CIN = PATCH_IN // 128
EPS = 1e-5
ROUTER_STEPS = 35
RSQRT_STEPS, RSQRT_ROUNDS, RSQRT_GUESS = 14, 3, float(0x5F3759DF)
SENTINEL, TAKEN = -1.0e30, -3.0e38

UP0, AT0 = 0, 2 * HID
QW, KW, VW = AT0, AT0 + 576, AT0 + 1152
SPLIT_A = AT0 + 1344
UP1 = SPLIT_A
L0 = UP1 + 2 * HID
L1 = L0 + 3 * C
R0 = L1 + 3 * C
R1 = R0 + EXPERTS
SPLIT = R1 + EXPERTS

PE_STAGES = dict(EM=1, MEAN=1, VAR=1, XT=1, Q=3, K=3, V=1, S1=12, MT=1, S2=12, PV=3, OT=2,
                 XT2=1, KV=2, LQ=1, KVT=1, GW=1, Y=1, XT3=1)
MADE = dict(variance=1, ln2_rstd=RSQRT_STEPS, ln3_rstd=RSQRT_STEPS, tokens=1, row_sums=1, neg_mean=1, squares=2, rstd=RSQRT_STEPS, centred=1, normed=1, x_high=1,
            x_low=1, x_turned=1, q_full=3, q_high=3, q_low=3, k_full=3, k_high=3, k_low=3,
            k_masked=6, v_made=1, row_max=12, max_turned=1, probs=12, heads_out=3, recip=2,
            heads=2, h1=2, h1_biased=1, ln2=6, ln2_high=2, ln2_low=2, x2_turned=1, kv=2,
            gelu_q=2, gelu_kv=2, gelu_kv_masked=2, kv_proj=2, h2=1, h2_biased=1, ln3=6,
            ln3_high=2, ln3_low=2, x3_turned=1)
PAIR = dict(RT=1, CT=1, router=ROUTER_STEPS, router_exp=1, gates_turned=1, CB=12, G=14, U=14, DN=4,
            gate_copied=12, tanh=14, gated=14, upped=14, hidden=14, result=2, stored=1, loaded=1)
READ_BY = dict(EM="tokens", MEAN="neg_mean", VAR="variance", XT="x_turned", Q="q_full", K="k_full",
               V="v_made", S1="row_max", MT="max_turned", S2="probs", PV="heads_out", OT="heads",
               XT2="x2_turned", KV="kv", LQ="gelu_q", KVT="gelu_kv", GW="kv_proj", Y="h2",
               XT3="x3_turned", RT="router", CT="gates_turned")
LAST_READ = dict(LQ=1, KVT=1, GW=1)


def schedule():
    out = []
    fill = [(s, m) for m in range(UNITS) for s in ("G", "U")] + [("DN", q) for q in range(4)]

    def filler(n):
        for _ in range(n):
            if fill:
                out.append(fill.pop(0))

    def both(*stages, n=1):
        for s in stages:
            for a in range(2):
                for k in range(PE_STAGES[s]):
                    out.append((s, a, k))
            filler(n)

    both("EM", "MEAN", "VAR", "XT", n=2)
    both("Q", "K", "V", n=2)
    for a in range(2):
        for k in range(12):
            out.append(("S1", a, k))
            if k % 4 == 3:
                filler(1)
    both("MT", n=1)
    for a in range(2):
        for k in range(12):
            out.append(("S2", a, k))
            if k % 4 == 3:
                out.append(("PV", a, k // 4))
                filler(1)
    both("OT", n=2)
    both("XT2", "KV", n=2)
    both("LQ", "KVT", n=0)
    filler(100)
    both("GW", "Y", "XT3", n=0)
    out += [("RT", None, 0), ("CT", None, 0)]
    return out


def vit_tower(nc, x, w_patch, pos, tok_add, ln_w, ln_b, w_split, bq, bk, bv, w_proj, b_proj,
              router_b, corr_b, w_down, down_b, shared_b, gate_bias, up_bias, select,
              consts32, consts16, out):
    pairs = x.shape[0]
    steps = schedule()
    ring = [s for s in steps if s[0] in PE_STAGES or s[0] in ("RT", "CT")]
    assert len(ring) % 4 == 0
    place = {s: n for n, s in enumerate(ring)}

    ctx = ExitStack()
    with ctx:
        def sb(name, shape, dt=F32):
            return ctx.enter_context(nc.sbuf_tensor(name, shape, dt))

        def two(name, shape, dt=F32):
            return [sb(f"{name}{a}", shape, dt) for a in range(2)]

        w_high, w_low = sb("w_high", [128, SPLIT], F16), sb("w_low", [128, SPLIT], F16)
        wp_sb = sb("wp_sb", [128, CIN, C])
        wd_sb = sb("wd_sb", [128, UNITS, C])
        wproj_sb = sb("wproj_sb", [128, 2, C])
        table = sb("table", [TR, 2, C])
        lnw_sb, lnb_sb = sb("lnw_sb", [TR, 2, C]), sb("lnb_sb", [TR, 2, C])
        bq_sb, bk_sb = sb("bq_sb", [96, 6]), sb("bk_sb", [96, 6])
        bv_sb, bproj_sb, sbd_sb = sb("bv_sb", [TR, C]), sb("bproj_sb", [TR, C]), sb("sbd_sb", [TR, C])
        rb_sb, corr_sb = sb("rb_sb", [TR, EXPERTS]), sb("corr_sb", [TR, EXPERTS])
        gbd_sb = sb("gbd_sb", [32, C])
        gbd_high, gbd_low = sb("gbd_high", [32, C], F16), sb("gbd_low", [32, C], F16)
        gbias, ubias, half_gbias = sb("gbias", [128, UNITS]), sb("ubias", [128, UNITS]), sb("half_gbias", [128, UNITS])
        select_sb = sb("select_sb", [32, ROUTED, 128], F16)
        c32 = sb("c32", [128, consts32.shape[1]])
        ident32, bd_mask = c32[:, 0:128], c32[:, 128:320]
        head_mask, mean_w, before = c32[:, 320:322], c32[:, 322:422], c32[:, 422:438]
        c16 = sb("c16", [128, 128], F16)
        ident16 = c16[:, :]

        xin = sb("xin", [128, CIN, 2, TC])
        tok, h1 = two("tok", [TR, 2, C]), two("h1", [TR, 2, C])
        xa, xb = two("xa", [TR, 2, C]), two("xb", [TR, 2, C])
        tok_add_sb = h1[0]
        ms, h1b, h2 = xa, xa, tok
        rsum, nmean, sq, rstd, var = two("rsum", [TR, 2]), two("nmean", [TR, 1]), two("sq", [TR, 2]), two("rstd", [TR, 1]), two("var", [TR, 1])
        x3 = two("x3", [TR, 2, 6, 64], F16)
        xt = two("xt", [128, 3, TC], F16)
        qf = two("qf", [128, 6, TC])
        kf = qf
        qs, kh = two("qs", [128, 6, TC], F16), two("kh", [96, 6, TC], F16)
        ks = two("ks", [128, HEADS, TC], F16)
        vp = two("vp", [TR, 2, HEADS, 32])
        mx = two("mx", [TR, 2, HEADS], F16)
        probs = sb("probs", [128, HEADS, 2, TC])
        ots = [b[:, 0:3, :] for b in qf]
        rec = two("rec", [TR, 2, HEADS])
        bns, bna, rs2 = two("bns", [TR, 2, 6]), two("bna", [TR, 2, 2]), two("rs2", [TR, 2])
        xn = xb
        xs = [b[:, :, :, :].rearrange("p t j c -> p t (j c)") for b in x3]
        xt2 = xt
        eps = sb("eps", [TR, 2])
        work = two("work", [TR, 2, 2])
        kv, gkv, gw = two("kv", [TR, 2, 2 * C]), two("gkv", [128, C]), two("gw", [128, 2, C])
        gq, gkvm = [b[:, 3:5, :] for b in qf], gkv

        xp = sb("xp", [128, 3, PT], F16)
        ct = sb("ct", [32, PT], F16)
        hs = sb("hs", [TR, 2, 2, C])
        res = sb("res", [TR, 2, 2, C])
        z, ez, s1, score, sf = (sb(n, [TR, 4, EXPERTS]) for n in ("z", "ez", "s1", "score", "sf"))
        psum2 = sb("psum2", [TR, 16, 6])
        gs, rank, keep = (sb(n, [TR, 16]) for n in ("gs", "rank", "keep"))
        gt, eq, eql, beats = (sb(n, [TR, 4, 4, 4]) for n in ("gt", "eq", "eql", "beats"))
        sm, mr = sb("sm", [TR, 4, 20]), sb("mr", [TR, 4, 20])
        top8 = sb("top8", [TR, 4, 8])
        wsel, gates = sb("wsel", [TR, 4, EXPERTS]), sb("gates", [TR, 4, EXPERTS])
        den, den1, rden = (sb(n, [TR, 4]) for n in ("den", "den1", "rden"))
        gates_hl = sb("gates_hl", [TR, 4, 32], F16)
        cs, th, ga = (two(n, [128, PT]) for n in ("cs", "th", "ga"))
        ub = ga
        hid = sb("hid", [128, UNITS, PT])

        bank = [ctx.enter_context(nc.psum_tensor(f"ring{n}", [128, 512], F32)) for n in range(4)]
        bank_g, bank_u, bank_c, bank_d = (ctx.enter_context(nc.psum_tensor(n, [128, 512], F32))
                                          for n in ("bank_g", "bank_u", "bank_c", "bank_d"))

        sem = {n: [ctx.enter_context(nc.semaphore(f"{n}_{a}")) for a in range(2)]
              for n in (*PE_STAGES, *MADE)}
        pair_sem = {n: ctx.enter_context(nc.semaphore(n)) for n in PAIR}
        per = {**PE_STAGES, **MADE, **PAIR}
        consts_in = ctx.enter_context(nc.semaphore("consts_in"))
        stage_in = [ctx.enter_context(nc.semaphore(f"stage_in{n}")) for n in range(2)]
        init_done = ctx.enter_context(nc.semaphore("init_done"))
        pool_init = ctx.enter_context(nc.semaphore("pool_init"))
        init_chain = ctx.enter_context(nc.semaphore("init_chain"))

        def nth(name, i, k=0):
            return per[name] * i + k + 1

        def later(i):
            return not isinstance(i, int) or i > 0

        def ring_bank(step):
            return bank[place[step] % 4]

        def last_tenant(step):
            n = place[step] - 4
            return ring[n % len(ring)], n < 0

        def ring_used(step, i):
            return later(i) or not last_tenant(step)[1]

        def ring_reader(step):
            (stage, a, _), _ = last_tenant(step)
            return pair_sem[READ_BY[stage]] if a is None else sem[READ_BY[stage]][a]

        def ring_count(step, i):
            (stage, _, k), pair_before = last_tenant(step)
            return nth(READ_BY[stage], i - 1 if pair_before else i, LAST_READ.get(stage, k))

        def run(body):
            def whole(eng):
                body(0, None)
                body(1, 0)
                with eng.Fori(2, pairs) as i:
                    body(i, i - 1)
                body(None, pairs - 1)
            return whole

        def walk(image_steps, ffn_steps, tail=None):
            def body(i, j):
                for step in steps:
                    if step[0] in ("G", "U", "DN"):
                        if j is not None and step[0] in ffn_steps:
                            ffn_steps[step[0]](j, step[1])
                    elif i is not None and step[0] in image_steps:
                        image_steps[step[0]](i, *step[1:])
            return body

        staged = [probs[:, :, :, :].rearrange("p h t n -> p (h t n)")[:, 0:SPLIT_A],
                  hid[:, :, :].rearrange("p m n -> p (m n)")[:, 0:SPLIT - SPLIT_A]]
        block = ctx.enter_context(nc.Block())

        @block.sync
        def _(sp):
            sp.dma_start(staged[0],
                         w_split[:, 0:SPLIT_A]).then_inc(stage_in[0], 16)
            sp.dma_start(staged[1],
                         w_split[:, SPLIT_A:SPLIT]).then_inc(stage_in[1], 16)
            sp.dma_start(xin[:, :, :, :], x[0]).then_inc(pair_sem["loaded"], 16)
            for dst, src in ((wp_sb[:, :, :], w_patch), (wd_sb[:, :, :], w_down), (wproj_sb[:, :, :], w_proj),
                             (table[:, :, :], pos), (tok_add_sb[:, :, :], tok_add), (lnw_sb[:, :, :], ln_w),
                             (lnb_sb[:, :, :], ln_b), (bq_sb[:, :], bq), (bk_sb[:, :], bk), (bv_sb[:, :], bv),
                             (bproj_sb[:, :], b_proj), (sbd_sb[:, :], shared_b), (rb_sb[:, :], router_b),
                             (corr_sb[:, :], corr_b), (gbd_sb[:, :], down_b), (gbias[:, :], gate_bias),
                             (ubias[:, :], up_bias), (select_sb[:, :, :], select), (c32[:, :], consts32),
                             (c16[:, :], consts16[:, 0:128]),
                             ):
                sp.dma_start(dst, src).then_inc(consts_in, 16)
            sp.wait_ge(pool_init, 4)
            for a in range(2):
                sp.dma_start(ks[a][96:128, :, :],
                             consts16[96:128, 128:128 + HEADS * TC].rearrange("p (h n) -> p h n", h=HEADS)
                             ).then_inc(consts_in, 16)

            def body(i, j):
                if i is not None:
                    last = isinstance(i, int) and i == pairs - 1
                    if not last:
                        sp.wait_ge(sem["EM"][1], nth("EM", i))
                        sp.wait_ge(sem["EM"][0], nth("EM", i))
                        nxt = i + 1
                        sp.dma_start(xin[:, :, :, :], x[nxt] if isinstance(nxt, int)
                                     else x[bass.ds(nxt, 1)].rearrange("o p c a n -> p (o c) a n")
                                     ).then_inc(pair_sem["loaded"], 16)
                if j is not None:
                    sp.wait_ge(pair_sem["result"], nth("result", j, 1))
                    dst = out[j] if isinstance(j, int) else out[bass.ds(j, 1)].rearrange("o p a t c -> p (o a) t c")
                    sp.dma_start(dst, res[:, :, :, :]).then_inc(pair_sem["stored"], 16)
            body(0, None)
            body(1, 0)
            with sp.Fori(2, pairs - 1) as i:
                body(i, i - 1)
            body(pairs - 1, pairs - 2)
            body(None, pairs - 1)
            sp.wait_ge(pair_sem["stored"], 16 * pairs)

        CONSTS = 16 * 22

        @block.gpsimd
        def _(pool):
            for a in range(2):
                pool.memset(vp[a][:, :, :, 16:32], 1.0).then_inc(pool_init, 1)
                pool.wait_ge(pool_init, 2 * a + 1)
                pool.memset(qs[a][96:128, :, :], 0.0).then_inc(pool_init, 1)
                pool.wait_ge(pool_init, 2 * a + 2)
            pool.memset(sm[:, :, 16:20], SENTINEL).then_inc(pool_init, 1)
            pool.memset(eps[:, :], EPS).then_inc(pool_init, 1)
            pool.wait_ge(pool_init, 6)
            pool.wait_ge(consts_in, CONSTS)
            pool.wait_ge(init_done, 1)

            def rsqrt(i, a, y, variance, tmp, name):
                v, t = tmp[:, 0, :], tmp[:, 1, :]
                steps_done = [0]

                def step(ins):
                    ins.then_inc(sem[name][a], 1)
                    pool.drain()
                    steps_done[0] += 1

                step(nc.gpsimd.tensor_tensor(v, variance, eps[:, 0:variance.shape[1]], ALU.add))
                step(nc.gpsimd.tensor_scalar(y[:, :].bitcast(I32), v.bitcast(I32), -0.5, RSQRT_GUESS, ALU.mult, ALU.add))
                for _ in range(RSQRT_ROUNDS):
                    step(nc.gpsimd.tensor_tensor(t, y[:, :], y[:, :], ALU.mult))
                    step(nc.gpsimd.tensor_tensor(t, t, v, ALU.mult))
                    step(nc.gpsimd.tensor_scalar(t, t, -0.5, 1.5, ALU.mult, ALU.add))
                    step(nc.gpsimd.tensor_tensor(y[:, :], y[:, :], t, ALU.mult))
                assert steps_done[0] == RSQRT_STEPS

            def low_of_x(i, a, k):
                pool.wait_ge(sem["variance"][a], nth("variance", i))
                rsqrt(i, a, rstd[a], var[a][:, :], work[a][:, :, 0:1], "rstd")
                pool.wait_ge(sem["x_high"][a], nth("x_high", i))
                pool.wait_ge(sem["normed"][a], nth("normed", i))
                nc.gpsimd.tensor_tensor(x3[a][:, :, :, 32:64], xb[a][:, :, :].rearrange("p t (j c) -> p t j c", c=32),
                                        x3[a][:, :, :, 0:32], ALU.subtract).then_inc(sem["x_low"][a], 1)

            def low_of_q(i, a, k):
                pool.wait_ge(sem["q_high"][a], nth("q_high", i, k))
                pool.wait_ge(sem["q_full"][a], nth("q_full", i, k))
                nc.gpsimd.tensor_tensor(qs[a][32:64, 2 * k:2 * k + 2, :], qf[a][32:64, 2 * k:2 * k + 2, :],
                                        qs[a][32:64, 2 * k:2 * k + 2, :], ALU.subtract).then_inc(sem["q_low"][a], 1)

            def low_of_k(i, a, k):
                pool.wait_ge(sem["k_high"][a], nth("k_high", i, k))
                pool.wait_ge(sem["k_full"][a], nth("k_full", i, k))
                nc.gpsimd.tensor_tensor(kh[a][64:96, 2 * k:2 * k + 2, :], kf[a][64:96, 2 * k:2 * k + 2, :],
                                        kh[a][64:96, 2 * k:2 * k + 2, :], ALU.subtract).then_inc(sem["k_low"][a], 1)

            def residual(i, a, t):
                pool.wait_ge(sem["heads"][a], nth("heads", i, t))
                pool.wait_ge(sem["tokens"][a], nth("tokens", i))
                nc.gpsimd.tensor_tensor(h1[a][:, t, :], tok[a][:, t, :], ms[a][:, t, :], ALU.add
                                        ).then_inc(sem["h1"][a], 1)

            def lows_of_norm(i, a, name):
                pool.wait_ge(sem[name][a], nth(name, i, 3))
                rsqrt(i, a, rs2[a], bna[a][:, :, 1], work[a], name + "_rstd")
                pool.wait_ge(sem[name + "_high"][a], nth(name + "_high", i, 1))
                pool.wait_ge(sem[name][a], nth(name, i, 5))
                nc.gpsimd.tensor_tensor(xs[a][:, :, 128:256], xn[a][:, :, 0:128], xs[a][:, :, 0:128],
                                        ALU.subtract).then_inc(sem[name + "_low"][a], 1)
                nc.gpsimd.tensor_tensor(xs[a][:, :, 320:384], xn[a][:, :, 128:192], xs[a][:, :, 256:320],
                                        ALU.subtract).then_inc(sem[name + "_low"][a], 1)

            def norm2(i, a, k):
                lows_of_norm(i, a, "ln2")
                nc.gpsimd.tensor_tensor(h1b[a][:, :, :], h1[a][:, :, :],
                                        bproj_sb[:, :].unsqueeze(1).to_broadcast([TR, 2, C]), ALU.add
                                        ).then_inc(sem["h1_biased"][a], 1)

            def mask_kv(i, a, k):
                pool.wait_ge(sem["gelu_kv"][a], nth("gelu_kv", i, 1))
                nc.gpsimd.tensor_tensor(gkvm[a][:, 0:128], gkv[a][:, 0:128], bd_mask[:, 0:128], ALU.mult
                                        ).then_inc(sem["gelu_kv_masked"][a], 1)
                nc.gpsimd.tensor_tensor(gkvm[a][0:64, 128:192], gkv[a][0:64, 128:192], bd_mask[0:64, 128:192],
                                        ALU.mult).then_inc(sem["gelu_kv_masked"][a], 1)

            def norm3(i, a, k):
                lows_of_norm(i, a, "ln3")
                if later(i):
                    pool.wait_ge(pair_sem["result"], nth("result", i - 1, 1))
                nc.gpsimd.tensor_tensor(hs[:, a, :, :], h2[a][:, :, :],
                                        sbd_sb[:, :].unsqueeze(1).to_broadcast([TR, 2, C]), ALU.add
                                        ).then_inc(sem["h2_biased"][a], 1)

            run(walk(dict(VAR=low_of_x, Q=low_of_q, K=low_of_k, OT=residual, XT2=norm2, KVT=mask_kv,
                          XT3=norm3), {}))(pool)

        @block.scalar
        def _(act):
            act.wait_ge(init_done, 1)
            act.wait_ge(consts_in, CONSTS)

            def moments(i, a, k):
                act.wait_ge(sem["MEAN"][a], nth("MEAN", i))
                nc.scalar.activation(nmean[a][:, :], ring_bank(("MEAN", a, 0))[0:TR, 0:1], ACT.Copy, scale=-1.0
                                     ).then_inc(sem["neg_mean"][a], 1)
                act.wait_ge(sem["neg_mean"][a], nth("neg_mean", i))
                for t in range(2):
                    n = LIVE[t]
                    nc.scalar.activation(xa[a][0:n, t, :], tok[a][0:n, t, :], ACT.Square,
                                         bias=nmean[a][0:n, :], accum_out=sq[a][0:n, t:t + 1]
                                         ).then_inc(sem["squares"][a], 1)

            def high_of_x(i, a, k):
                act.wait_ge(sem["normed"][a], nth("normed", i))
                nc.scalar.activation(x3[a][:, :, :, 0:32], xb[a][:, :, :].rearrange("p t (j c) -> p t j c", c=32),
                                     ACT.Copy).then_inc(sem["x_high"][a], 1)

            def x_out(i, a, k):
                act.wait_ge(sem["XT"][a], nth("XT", i))
                nc.scalar.activation(xt[a][:, :, :], turned(("XT", a, 0)), ACT.Copy).then_inc(sem["x_turned"][a], 1)

            def turned(step):
                return ring_bank(step)[:, 0:300].bitcast(F16).rearrange("p (b n) -> p b n", b=3)

            def high_of_q(i, a, k):
                act.wait_ge(sem["q_full"][a], nth("q_full", i, k))
                nc.scalar.activation(qs[a][0:96, 2 * k:2 * k + 2, :], qf[a][0:96, 2 * k:2 * k + 2, :], ACT.Copy
                                     ).then_inc(sem["q_high"][a], 1)

            def high_of_k(i, a, k):
                act.wait_ge(sem["k_full"][a], nth("k_full", i, k))
                nc.scalar.activation(kh[a][:, 2 * k:2 * k + 2, :], kf[a][0:96, 2 * k:2 * k + 2, :], ACT.Copy
                                     ).then_inc(sem["k_high"][a], 1)

            def exponents(i, a, h):
                act.wait_ge(sem["S2"][a], nth("S2", i, h))
                if a == 1:
                    act.wait_ge(sem["PV"][0], nth("PV", i, h // 4))
                else:
                    if later(i):
                        act.wait_ge(sem["PV"][1], nth("PV", i - 1, h // 4))
                nc.scalar.activation(probs[0:TR, h, :, :],
                                     ring_bank(("S2", a, h))[0:TR, 0:2 * TC].rearrange("p (t n) -> p t n", t=2),
                                     ACT.Exp, scale=DH ** -0.5).then_inc(sem["probs"][a], 1)

            def heads_out(i, a, g):
                act.wait_ge(sem["PV"][a], nth("PV", i, g))
                nc.scalar.activation(ots[a][:, g, :], ring_bank(("PV", a, g))[:, 0:TC], ACT.Copy
                                     ).then_inc(sem["heads_out"][a], 1)

            def highs_of_norm(i, a, name):
                act.wait_ge(sem[name][a], nth(name, i, 5))
                nc.scalar.activation(xs[a][:, :, 0:128], xn[a][:, :, 0:128], ACT.Copy
                                     ).then_inc(sem[name + "_high"][a], 1)
                nc.scalar.activation(xs[a][:, :, 256:320], xn[a][:, :, 128:192], ACT.Copy
                                     ).then_inc(sem[name + "_high"][a], 1)

            def norm2(i, a, k):
                highs_of_norm(i, a, "ln2")
                act.wait_ge(sem["XT2"][a], nth("XT2", i))
                nc.scalar.activation(xt2[a][:, :, :], turned(("XT2", a, 0)), ACT.Copy
                                     ).then_inc(sem["x2_turned"][a], 1)

            def kv_out(i, a, t):
                act.wait_ge(sem["KV"][a], nth("KV", i, t))
                nc.scalar.activation(kv[a][:, t, :], ring_bank(("KV", a, t))[0:TR, 0:2 * C], ACT.Copy
                                     ).then_inc(sem["kv"][a], 1)

            def gelu_q(i, a, k):
                b = ring_bank(("LQ", a, 0))
                act.wait_ge(sem["LQ"][a], nth("LQ", i))
                nc.scalar.activation(gq[a][:, 0, :], b[:, 0:TC], ACT.Gelu).then_inc(sem["gelu_q"][a], 1)
                nc.scalar.activation(gq[a][0:64, 1, :], b[0:64, TC:2 * TC], ACT.Gelu).then_inc(sem["gelu_q"][a], 1)

            def gelu_kv(i, a, k):
                b = ring_bank(("KVT", a, 0))
                act.wait_ge(sem["KVT"][a], nth("KVT", i))
                nc.scalar.activation(gkv[a][:, 0:128], b[:, 0:128], ACT.Gelu, scale=DH ** -0.5
                                     ).then_inc(sem["gelu_kv"][a], 1)
                nc.scalar.activation(gkv[a][0:64, 128:192], b[0:64, 128:192], ACT.Gelu, scale=DH ** -0.5
                                     ).then_inc(sem["gelu_kv"][a], 1)

            def norm3(i, a, k):
                highs_of_norm(i, a, "ln3")
                act.wait_ge(sem["XT3"][a], nth("XT3", i))
                if later(i):
                    act.wait_ge(pair_sem["U"], nth("U", i - 1, UNITS - 1))
                nc.scalar.activation(xp[:, :, a * TC:(a + 1) * TC], turned(("XT3", a, 0)), ACT.Copy
                                     ).then_inc(sem["x3_turned"][a], 1)

            def router_exp(i, a, k):
                act.wait_ge(pair_sem["router"], nth("router", i, 0))
                nc.scalar.activation(ez[:, :, :], z[:, :, :], ACT.Exp, scale=-1.0).then_inc(pair_sem["router_exp"], 1)

            def gate(j, m):
                n = UNIT_ROWS[m]
                if m < ROUTED:
                    act.wait_ge(pair_sem["CB"], nth("CB", j, m))
                    if m >= 2:
                        act.wait_ge(pair_sem["gated"], nth("gated", j, m - 2))
                    nc.scalar.activation(cs[m % 2][:, :], bank_c[:, 0:PT], ACT.Copy, scale=0.5
                                         ).then_inc(pair_sem["gate_copied"], 1)
                act.wait_ge(pair_sem["G"], nth("G", j, m))
                if m >= 2:
                    act.wait_ge(pair_sem["hidden"], nth("hidden", j, m - 2))
                nc.scalar.activation(th[m % 2][0:n, :], bank_g[0:n, 0:PT], ACT.Tanh, scale=0.5,
                                     bias=half_gbias[0:n, m:m + 1]).then_inc(pair_sem["tanh"], 1)

            run(walk(dict(MEAN=moments, VAR=high_of_x, XT=x_out, Q=high_of_q, K=high_of_k, S2=exponents,
                          PV=heads_out, XT2=norm2, KV=kv_out, LQ=gelu_q, KVT=gelu_kv, XT3=norm3,
                          RT=router_exp), dict(G=gate)))(act)

        @block.vector
        def _(dve):
            chain = [0]

            def link(ins):
                chain[0] += 1
                ins.then_inc(init_chain, 1)
                dve.wait_ge(init_chain, chain[0])

            for n, (lo, hi) in enumerate(((0, SPLIT_A), (SPLIT_A, SPLIT))):
                full = staged[n]
                dve.wait_ge(stage_in[n], 16)
                link(nc.vector.tensor_copy(w_high[:, lo:hi], full))
                link(nc.vector.tensor_tensor(w_low[:, lo:hi], full, w_high[:, lo:hi], ALU.subtract))
            dve.wait_ge(consts_in, CONSTS)
            dve.wait_ge(pool_init, 5)
            link(nc.vector.tensor_copy(gbd_high[:, :], gbd_sb[:, :]))
            link(nc.vector.tensor_tensor(gbd_low[:, :], gbd_sb[:, :], gbd_high[:, :], ALU.subtract))
            link(nc.vector.tensor_scalar(half_gbias[:, :], gbias[:, :], 0.5, None, ALU.mult))
            nc.vector.tensor_tensor(table[:, :, :], table[:, :, :], tok_add_sb[:, :, :], ALU.add
                                    ).then_inc(init_done, 1)
            dve.wait_ge(init_done, 1)

            def tokens(i, a, k):
                dve.wait_ge(sem["EM"][a], nth("EM", i))
                if later(i):
                    dve.wait_ge(sem["h2_biased"][a], nth("h2_biased", i - 1))
                nc.vector.tensor_tensor(tok[a][:, :, :], ring_bank(("EM", a, 0))[0:TR, 0:2 * C].rearrange(
                    "p (t c) -> p t c", t=2), table[:, :, :], ALU.add).then_inc(sem["tokens"][a], 1)
                dve.wait_ge(sem["tokens"][a], nth("tokens", i))
                nc.vector.tensor_reduce(rsum[a][:, :], tok[a][:, :, :], AX.X, ALU.add
                                        ).then_inc(sem["row_sums"][a], 1)

            def normalise(i, a, k):
                dve.wait_ge(sem["VAR"][a], nth("VAR", i))
                nc.vector.tensor_copy(var[a][:, :], ring_bank(("VAR", a, 0))[0:TR, 0:1]).then_inc(sem["variance"][a], 1)
                dve.wait_ge(sem["neg_mean"][a], nth("neg_mean", i))
                nc.vector.scalar_tensor_tensor(out=xa[a][:, :, :], in0=tok[a][:, :, :], scalar=nmean[a][:, 0:1],
                                               in1=lnw_sb[:, :, :], op0=ALU.add, op1=ALU.mult
                                               ).then_inc(sem["centred"][a], 1)
                dve.wait_ge(sem["centred"][a], nth("centred", i))
                dve.wait_ge(sem["rstd"][a], nth("rstd", i, RSQRT_STEPS - 1))
                nc.vector.scalar_tensor_tensor(out=xb[a][:, :, :], in0=xa[a][:, :, :], scalar=rstd[a][:, 0:1],
                                               in1=lnb_sb[:, :, :], op0=ALU.mult, op1=ALU.add
                                               ).then_inc(sem["normed"][a], 1)

            def biased(full, bias, stage, name):
                def part(i, a, k):
                    dve.wait_ge(sem[stage][a], nth(stage, i, k))
                    nc.vector.tensor_tensor(full[a][0:96, 2 * k:2 * k + 2, :],
                                            ring_bank((stage, a, k))[0:96, 0:2 * TC].rearrange("p (j n) -> p j n", j=2),
                                            bias[:, 2 * k:2 * k + 2].unsqueeze(2).to_broadcast([96, 2, TC]), ALU.add
                                            ).then_inc(sem[name][a], 1)
                return part

            def keys(i, a, k):
                dve.wait_ge(sem["q_low"][a], nth("q_low", i, k))
                dve.wait_ge(sem["q_high"][a], nth("q_high", i, k))
                biased(kf, bk_sb, "K", "k_full")(i, a, k)
                if k >= 1:
                    mask_keys(i, a, k - 1)

            def mask_keys(i, a, k):
                dve.wait_ge(sem["k_low"][a], nth("k_low", i, k))
                dve.wait_ge(sem["k_high"][a], nth("k_high", i, k))
                for odd in range(2):
                    nc.vector.tensor_scalar(ks[a][0:96, 4 * k + odd:4 * k + 4:2, :], kh[a][:, 2 * k:2 * k + 2, :],
                                            head_mask[0:96, odd:odd + 1], None, ALU.mult
                                            ).then_inc(sem["k_masked"][a], 1)

            def values(i, a, k):
                mask_keys(i, a, 2)
                dve.wait_ge(sem["V"][a], nth("V", i))
                nc.vector.tensor_tensor(vp[a][:, :, :, 0:16],
                                        ring_bank(("V", a, 0))[0:TR, 0:2 * C].rearrange("p (t h d) -> p t h d", t=2, d=DH),
                                        bv_sb[:, :].rearrange("p (h d) -> p h d", d=DH).unsqueeze(1)
                                        .to_broadcast([TR, 2, HEADS, DH]), ALU.add).then_inc(sem["v_made"][a], 1)

            def row_max(i, a, k):
                t, hp = divmod(k, 6)
                dve.wait_ge(sem["S1"][a], nth("S1", i, k))
                nc.vector.tensor_reduce(mx[a][:, t, 2 * hp:2 * hp + 2],
                                        ring_bank(("S1", a, k))[0:TR, 0:2 * TC].rearrange("p (x n) -> p x n", x=2)[:, :, 0:SEQ],
                                        AX.X, ALU.max).then_inc(sem["row_max"][a], 1)

            def max_out(i, a, k):
                dve.wait_ge(sem["MT"][a], nth("MT", i))
                nc.vector.tensor_copy(qs[a][96:96 + HEADS, :, :],
                                      ring_bank(("MT", a, 0))[0:HEADS, 0:TR].bitcast(F16).unsqueeze(1)
                                      .to_broadcast([HEADS, 6, TC])).then_inc(sem["max_turned"][a], 1)

            def divide(i, a, t):
                b = ring_bank(("OT", a, t))[0:TR, 0:384].rearrange("p (h d) -> p h d", d=32)
                dve.wait_ge(sem["OT"][a], nth("OT", i, t))
                nc.vector.reciprocal(rec[a][:, t, :], b[:, :, 16]).then_inc(sem["recip"][a], 1)
                dve.wait_ge(sem["recip"][a], nth("recip", i, t))
                nc.vector.tensor_tensor(ms[a][:, t, :].rearrange("p (h d) -> p h d", d=DH), b[:, :, 0:16],
                                        rec[a][:, t, :].unsqueeze(2).to_broadcast([TR, HEADS, DH]), ALU.mult
                                        ).then_inc(sem["heads"][a], 1)

            def layernorm(i, a, src, name):
                for t in range(2):
                    nc.vector.bn_stats(bns[a][:, t, :], src[a][:, t, :]).then_inc(sem[name][a], 1)
                for t in range(2):
                    if t == 0:
                        dve.drain()
                    nc.vector.bn_aggr(bna[a][:, t, :], bns[a][:, t, :]).then_inc(sem[name][a], 1)
                dve.wait_ge(sem[name + "_rstd"][a], nth(name + "_rstd", i, RSQRT_STEPS - 1))
                for t in range(2):
                    nc.vector.tensor_scalar(xn[a][:, t, :], src[a][:, t, :], bna[a][:, t, 0:1], rs2[a][:, t:t + 1],
                                            ALU.subtract, ALU.mult).then_inc(sem[name][a], 1)

            def norm2(i, a, k):
                dve.wait_ge(sem["h1"][a], nth("h1", i, 1))
                layernorm(i, a, h1, "ln2")

            def proj_out(i, a, k):
                b = ring_bank(("GW", a, 0))
                dve.wait_ge(sem["GW"][a], nth("GW", i))
                nc.vector.tensor_copy(gw[a][:, 0, :], b[:, 0:C]).then_inc(sem["kv_proj"][a], 1)
                nc.vector.tensor_copy(gw[a][0:64, 1, :], b[0:64, C:2 * C]).then_inc(sem["kv_proj"][a], 1)

            def y_out(i, a, k):
                dve.wait_ge(sem["Y"][a], nth("Y", i))
                dve.wait_ge(sem["h1_biased"][a], nth("h1_biased", i))
                nc.vector.tensor_tensor(h2[a][:, :, :], ring_bank(("Y", a, 0))[0:TR, 0:2 * C].rearrange(
                    "p (t c) -> p t c", t=2), h1b[a][:, :, :], ALU.add).then_inc(sem["h2"][a], 1)

            def norm3(i, a, k):
                dve.wait_ge(sem["h2"][a], nth("h2", i))
                layernorm(i, a, h2, "ln3")

            def route(i, a, k):
                done = [0]

                def step(ins):
                    ins.then_inc(pair_sem["router"], 1)
                    dve.drain()
                    done[0] += 1

                def all4(ap):
                    return ap.unsqueeze(1).to_broadcast([TR, 4, EXPERTS])

                dve.wait_ge(pair_sem["RT"], nth("RT", i))
                step(nc.vector.tensor_tensor(z[:, :, :], ring_bank(("RT", None, 0))[0:TR, 0:4 * EXPERTS].rearrange(
                    "p (q e) -> p q e", q=4), all4(rb_sb[:, :]), ALU.add))
                dve.wait_ge(pair_sem["router_exp"], nth("router_exp", i))
                step(nc.vector.tensor_scalar(s1[:, :, :], ez[:, :, :], 1.0, None, ALU.add))
                step(nc.vector.reciprocal(score[:, :, :], s1[:, :, :]))
                step(nc.vector.tensor_tensor(sf[:, :, :], score[:, :, :], all4(corr_sb[:, :]), ALU.add))
                g4 = sf[:, :, :].rearrange("p q (g e) -> p (q g) e", e=4)
                step(nc.vector.tensor_tensor(psum2[:, :, 0:3], g4[:, :, 0:3], g4[:, :, 1:4], ALU.add))
                step(nc.vector.tensor_tensor(psum2[:, :, 3:5], g4[:, :, 0:2], g4[:, :, 2:4], ALU.add))
                step(nc.vector.tensor_tensor(psum2[:, :, 5:6], g4[:, :, 0:1], g4[:, :, 3:4], ALU.add))
                step(nc.vector.tensor_reduce(gs[:, :], psum2[:, :, :], AX.X, ALU.max))
                other = gs[:, :].rearrange("p (q g) -> p q g", g=4).unsqueeze(2).to_broadcast([TR, 4, 4, 4])
                own = gs[:, :].rearrange("p (q g) -> p q g", g=4).unsqueeze(3).to_broadcast([TR, 4, 4, 4])
                step(nc.vector.tensor_tensor(gt[:, :, :, :], other, own, ALU.is_gt))
                step(nc.vector.tensor_tensor(eq[:, :, :, :], other, own, ALU.is_equal))
                step(nc.vector.tensor_tensor(eql[:, :, :, :].rearrange("p q g h -> p q (g h)"),
                                             eq[:, :, :, :].rearrange("p q g h -> p q (g h)"),
                                             all4(before[0:TR, :]), ALU.mult))
                step(nc.vector.tensor_tensor(beats[:, :, :, :], gt[:, :, :, :], eql[:, :, :, :], ALU.add))
                step(nc.vector.tensor_reduce(rank[:, :], beats[:, :, :, :].rearrange("p q g h -> p (q g) h"),
                                             AX.X, ALU.add))
                step(nc.vector.tensor_scalar(keep[:, :], rank[:, :], 1.5, None, ALU.is_lt))
                step(nc.vector.tensor_tensor(sm[:, :, 0:16].rearrange("p q (g e) -> p q g e", e=4),
                                             sf[:, :, :].rearrange("p q (g e) -> p q g e", e=4),
                                             keep[:, :].rearrange("p (q g) -> p q g", g=4).unsqueeze(3)
                                             .to_broadcast([TR, 4, 4, 4]), ALU.mult))
                for q in range(4):
                    step(nc.vector.max(top8[:, q, :], sm[:, q, :]))
                step(nc.vector.memset(top8[:, :, 4:8], SENTINEL))
                for q in range(4):
                    step(nc.vector.match_replace(mr[:, q, :], top8[:, q, :], sm[:, q, :], TAKEN))
                step(nc.vector.scalar_tensor_tensor(out=wsel[:, :, :], in0=mr[:, :, 0:16], scalar=-2.0e38,
                                                    in1=score[:, :, :], op0=ALU.is_lt, op1=ALU.mult))
                step(nc.vector.tensor_reduce(den[:, :], wsel[:, :, :], AX.X, ALU.add))
                step(nc.vector.tensor_scalar(den1[:, :], den[:, :], 1e-20, None, ALU.add))
                step(nc.vector.reciprocal(rden[:, :], den1[:, :]))
                step(nc.vector.tensor_tensor(gates[:, :, :], wsel[:, :, :],
                                             rden[:, :].unsqueeze(2).to_broadcast([TR, 4, EXPERTS]), ALU.mult))
                step(nc.vector.tensor_scalar(gates_hl[:, :, 0:16], gates[:, :, :], 2.5, None, ALU.mult))
                step(nc.vector.scalar_tensor_tensor(out=gates_hl[:, :, 16:32], in0=gates[:, :, :], scalar=2.5,
                                                    in1=gates_hl[:, :, 0:16], op0=ALU.mult, op1=ALU.subtract))
                while done[0] < ROUTER_STEPS:
                    step(nc.vector.tensor_copy(den1[:, 0:1], den[:, 0:1]))

            def gates_out(i, a, k):
                dve.wait_ge(pair_sem["CT"], nth("CT", i))
                if later(i):
                    dve.wait_ge(pair_sem["DN"], nth("DN", i - 1, 3))
                nc.vector.tensor_copy(ct[:, :], ring_bank(("CT", None, 0))[0:32, 0:TC].bitcast(F16)
                                      ).then_inc(pair_sem["gates_turned"], 1)

            def gated(j, m):
                n = UNIT_ROWS[m]
                dve.wait_ge(pair_sem["tanh"], nth("tanh", j, m))
                if m < ROUTED:
                    dve.wait_ge(pair_sem["gate_copied"], nth("gate_copied", j, m))
                    nc.vector.scalar_tensor_tensor(out=ga[m % 2][0:n, :], in0=bank_g[0:n, 0:PT],
                                                   scalar=gbias[0:n, m:m + 1], in1=cs[m % 2][0:n, :],
                                                   op0=ALU.add, op1=ALU.mult).then_inc(pair_sem["gated"], 1)
                else:
                    nc.vector.tensor_scalar(ga[m % 2][0:n, :], bank_g[0:n, 0:PT], gbias[0:n, m:m + 1], 0.5,
                                            ALU.add, ALU.mult).then_inc(pair_sem["gated"], 1)

            def hidden(j, m):
                n = UNIT_ROWS[m]
                dve.wait_ge(pair_sem["U"], nth("U", j, m))
                dve.wait_ge(pair_sem["gated"], nth("gated", j, m))
                nc.vector.scalar_tensor_tensor(out=ub[m % 2][0:n, :], in0=bank_u[0:n, 0:PT],
                                               scalar=ubias[0:n, m:m + 1], in1=ga[m % 2][0:n, :],
                                               op0=ALU.add, op1=ALU.mult).then_inc(pair_sem["upped"], 1)
                dve.wait_ge(pair_sem["upped"], nth("upped", j, m))
                if later(j):
                    dve.wait_ge(pair_sem["DN"], nth("DN", j - 1, 3))
                nc.vector.scalar_tensor_tensor(out=hid[0:n, m, :], in0=th[m % 2][0:n, :], scalar=1.0,
                                               in1=ub[m % 2][0:n, :], op0=ALU.add, op1=ALU.mult
                                               ).then_inc(pair_sem["hidden"], 1)

            def result(j, q):
                a, t = divmod(q, 2)
                if t == 0:
                    return
                dve.wait_ge(pair_sem["DN"], nth("DN", j, q))
                if a == 0 and later(j):
                    dve.wait_ge(pair_sem["stored"], 16 * j)
                dve.wait_ge(sem["h2_biased"][a], nth("h2_biased", j))
                nc.vector.tensor_tensor(res[:, a, :, :], bank_d[0:TR, 0:2 * C].rearrange("p (t c) -> p t c", t=2),
                                        hs[:, a, :, :], ALU.add).then_inc(pair_sem["result"], 1)

            run(walk(dict(EM=tokens, VAR=normalise, Q=biased(qf, bq_sb, "Q", "q_full"), K=keys, V=values,
                          S1=row_max, MT=max_out, OT=divide, XT2=norm2, GW=proj_out, Y=y_out, XT3=norm3,
                          RT=route, CT=gates_out), dict(G=gated, U=hidden, DN=result)))(dve)

        @block.tensor
        def _(pe):
            mm = nc.tensor.matmul
            pe.wait_ge(init_done, 1)
            pe.wait_ge(consts_in, CONSTS)

            def dense(dst, stationary, moving, columns=None):
                for n, (blk, w, row) in enumerate(((0, w_high, 0), (1, w_high, 0), (0, w_low, 0),
                                                   (2, w_high, 1), (2, w_low, 1))):
                    last = mm(dst, stationary(blk, w, row), moving(blk, w, row), start=n == 0, stop=n == 4)
                return last

            def embed(i, a, k):
                step = ("EM", a, 0)
                pe.wait_ge(pair_sem["loaded"], 16 * (i + 1))
                if ring_used(step, i):
                    pe.wait_ge(ring_reader(step), ring_count(step, i))
                for t in range(2):
                    for c in range(CIN):
                        last = mm(ring_bank(step)[0:TR, t * C:(t + 1) * C], xin[:, c, a, t * TR:(t + 1) * TR],
                                  wp_sb[:, c, :], start=c == 0, stop=c == CIN - 1)
                last.then_inc(sem["EM"][a], 1)

            def moment(stage, source, made, k_made):
                def part(i, a, k):
                    step = (stage, a, 0)
                    pe.wait_ge(sem[made][a], nth(made, i, k_made))
                    if ring_used(step, i):
                        pe.wait_ge(ring_reader(step), ring_count(step, i))
                    for t in range(2):
                        n = LIVE[t]
                        last = mm(ring_bank(step)[0:TR, 0:1], mean_w[0:n, :], source[a][0:n, t:t + 1],
                                  start=t == 0, stop=t == 1)
                    last.then_inc(sem[stage][a], 1)
                return part

            def turn(dst, src, n_blocks):
                for t in range(2):
                    for b in range(n_blocks):
                        last = nc.tensor.transpose(dst[:, b, t * TR:(t + 1) * TR], src(t, b), ident16[0:TR, 0:TR])
                return last

            def turned(step):
                return ring_bank(step)[:, 0:300].bitcast(F16).rearrange("p (b n) -> p b n", b=3)

            def turn_x(i, a, k):
                pe.wait_ge(sem["x_low"][a], nth("x_low", i))
                if ring_used(("XT", a, 0), i):
                    pe.wait_ge(ring_reader(("XT", a, 0)), ring_count(("XT", a, 0), i))
                turn(turned(("XT", a, 0)),
                     lambda t, b: x3[a][:, t, 2 * b:2 * b + 2, :].rearrange("p j c -> p (j c)"), 3
                     ).then_inc(sem["XT"][a], 1)

            def project(stage, col):
                def part(i, a, k):
                    step = (stage, a, k)
                    pe.wait_ge(sem["x_turned"][a], nth("x_turned", i))
                    if ring_used(step, i):
                        pe.wait_ge(ring_reader(step), ring_count(step, i))
                    for y in range(2):
                        j = 2 * k + y
                        for n, w in enumerate((w_high, w_low)):
                            last = mm(ring_bank(step)[0:96, y * TC:(y + 1) * TC],
                                      w[:, col + 96 * j:col + 96 * j + 96], xt[a][:, j // 2, :],
                                      start=n == 0, stop=n == 1)
                    last.then_inc(sem[stage][a], 1)
                return part

            def project_v(i, a, k):
                step = ("V", a, 0)
                pe.wait_ge(sem["x_turned"][a], nth("x_turned", i))
                if ring_used(step, i):
                    pe.wait_ge(ring_reader(step), ring_count(step, i))
                for t in range(2):
                    for b in range(3):
                        for n, w in enumerate((w_high, w_low)):
                            last = mm(ring_bank(step)[0:TR, t * C + 64 * b:t * C + 64 * b + 64],
                                      xt[a][:, b, t * TR:(t + 1) * TR], w[:, VW + 64 * b:VW + 64 * b + 64],
                                      start=n == 0, stop=n == 1)
                last.then_inc(sem["V"][a], 1)

            def scores(i, a, k):
                step = ("S1", a, k)
                t, hp = divmod(k, 6)
                pe.wait_ge(sem["q_low"][a], nth("q_low", i, hp // 2))
                pe.wait_ge(sem["q_high"][a], nth("q_high", i, hp // 2))
                pe.wait_ge(sem["k_masked"][a], nth("k_masked", i, 2 * (hp // 2) + 1))
                if ring_used(step, i):
                    pe.wait_ge(ring_reader(step), ring_count(step, i))
                for odd in range(2):
                    last = mm(ring_bank(step)[0:TR, odd * TC:odd * TC + SEQ], qs[a][0:96, hp, t * TR:(t + 1) * TR],
                              ks[a][0:96, 2 * hp + odd, 0:SEQ], start=True, stop=True)
                last.then_inc(sem["S1"][a], 1)

            def turn_max(i, a, k):
                step = ("MT", a, 0)
                pe.wait_ge(sem["row_max"][a], nth("row_max", i, 11))
                if ring_used(step, i):
                    pe.wait_ge(ring_reader(step), ring_count(step, i))
                for t in range(2):
                    last = nc.tensor.transpose(ring_bank(step)[0:HEADS, 0:TR].bitcast(F16)[:, t * TR:(t + 1) * TR],
                                               mx[a][:, t, :], ident16[0:TR, 0:TR])
                last.then_inc(sem["MT"][a], 1)

            def scores_less_max(i, a, h):
                step = ("S2", a, h)
                pe.wait_ge(sem["max_turned"][a], nth("max_turned", i))
                if ring_used(step, i):
                    pe.wait_ge(ring_reader(step), ring_count(step, i))
                for t in range(2):
                    last = mm(ring_bank(step)[0:TR, t * TC:(t + 1) * TC], ks[a][:, h, t * TR:(t + 1) * TR],
                              qs[a][:, h // 2, :], start=True, stop=True)
                last.then_inc(sem["S2"][a], 1)

            def attend(i, a, g):
                step = ("PV", a, g)
                pe.wait_ge(sem["v_made"][a], nth("v_made", i))
                assert ring[place[step] - 4] == ("S2", a, 4 * g)
                pe.wait_ge(sem["probs"][a], nth("probs", i, 4 * g + 3))
                for t in range(2):
                    n = LIVE[t]
                    for y in range(4):
                        h = 4 * g + y
                        last = mm(ring_bank(step)[32 * y:32 * y + 32, 0:TC], vp[a][0:n, t, h, :],
                                  probs[0:n, h, t, :], start=t == 0, stop=t == 1,
                                  tile_position=(0, 32 * y))
                last.then_inc(sem["PV"][a], 1)

            def turn_heads(i, a, t):
                step = ("OT", a, t)
                pe.wait_ge(sem["heads_out"][a], nth("heads_out", i, 2))
                if ring_used(step, i):
                    pe.wait_ge(ring_reader(step), ring_count(step, i))
                for g in range(3):
                    last = nc.tensor.transpose(ring_bank(step)[0:TR, 128 * g:128 * g + 128],
                                               ots[a][:, g, t * TR:(t + 1) * TR], ident32)
                last.then_inc(sem["OT"][a], 1)

            def turn_norm(stage, name):
                def part(i, a, k):
                    pe.wait_ge(sem[name + "_low"][a], nth(name + "_low", i, 1))
                    if ring_used((stage, a, 0), i):
                        pe.wait_ge(ring_reader((stage, a, 0)), ring_count((stage, a, 0), i))
                    turn(turned((stage, a, 0)), lambda t, b: xs[a][:, t, 128 * b:128 * b + 128], 3
                         ).then_inc(sem[stage][a], 1)
                return part

            def linear_kv(i, a, t):
                step = ("KV", a, t)
                pe.wait_ge(sem["x2_turned"][a], nth("x2_turned", i))
                if ring_used(step, i):
                    pe.wait_ge(ring_reader(step), ring_count(step, i))
                dense(ring_bank(step)[0:TR, 0:2 * C],
                      lambda blk, w, row: xt2[a][:, blk, t * TR:(t + 1) * TR],
                      lambda blk, w, row: w[:, (L0, L1)[row] + C:(L0, L1)[row] + 3 * C]
                      ).then_inc(sem["KV"][a], 1)

            def linear_q(i, a, k):
                step = ("LQ", a, 0)
                pe.wait_ge(sem["x2_turned"][a], nth("x2_turned", i))
                if ring_used(step, i):
                    pe.wait_ge(ring_reader(step), ring_count(step, i))
                for n, (lo, m) in enumerate(((0, 128), (128, 64))):
                    last = dense(ring_bank(step)[0:m, n * TC:(n + 1) * TC],
                                 lambda blk, w, row: w[:, (L0, L1)[row] + lo:(L0, L1)[row] + lo + m],
                                 lambda blk, w, row: xt2[a][:, blk, :])
                last.then_inc(sem["LQ"][a], 1)

            def linear_kv_product(i, a, k):
                step = ("KVT", a, 0)
                pe.wait_ge(sem["kv"][a], nth("kv", i, 1))
                if ring_used(step, i):
                    pe.wait_ge(ring_reader(step), ring_count(step, i))
                for lo, m in ((0, 128), (128, 64)):
                    for t in range(2):
                        n = LIVE[t]
                        last = mm(ring_bank(step)[0:m, lo:lo + m], kv[a][0:n, t, C + lo:C + lo + m],
                                  kv[a][0:n, t, lo:lo + m], start=t == 0, stop=t == 1)
                last.then_inc(sem["KVT"][a], 1)

            def fold_projection(i, a, k):
                step = ("GW", a, 0)
                pe.wait_ge(sem["gelu_kv_masked"][a], nth("gelu_kv_masked", i, 1))
                if ring_used(step, i):
                    pe.wait_ge(ring_reader(step), ring_count(step, i))
                mm(ring_bank(step)[0:128, 0:C], gkvm[a][:, 0:128], wproj_sb[:, 0, :], start=True, stop=True)
                mm(ring_bank(step)[0:64, C:2 * C], gkvm[a][0:64, 128:192], wproj_sb[0:64, 1, :],
                   start=True, stop=True).then_inc(sem["GW"][a], 1)

            def linear_out(i, a, k):
                step = ("Y", a, 0)
                pe.wait_ge(sem["kv_proj"][a], nth("kv_proj", i, 1))
                pe.wait_ge(sem["gelu_q"][a], nth("gelu_q", i, 1))
                if ring_used(step, i):
                    pe.wait_ge(ring_reader(step), ring_count(step, i))
                for t in range(2):
                    mm(ring_bank(step)[0:TR, t * C:(t + 1) * C], gq[a][:, 0, t * TR:(t + 1) * TR], gw[a][:, 0, :],
                       start=True, stop=False)
                    last = mm(ring_bank(step)[0:TR, t * C:(t + 1) * C], gq[a][0:64, 1, t * TR:(t + 1) * TR],
                              gw[a][0:64, 1, :], start=False, stop=True)
                last.then_inc(sem["Y"][a], 1)

            def router(i, a, k):
                step = ("RT", None, 0)
                pe.wait_ge(sem["x3_turned"][0], nth("x3_turned", i))
                pe.wait_ge(sem["x3_turned"][1], nth("x3_turned", i))
                if ring_used(step, i):
                    pe.wait_ge(ring_reader(step), ring_count(step, i))
                for q in range(4):
                    last = dense(ring_bank(step)[0:TR, EXPERTS * q:EXPERTS * (q + 1)],
                                 lambda blk, w, row: xp[:, blk, q * TR:(q + 1) * TR],
                                 lambda blk, w, row: w[:, (R0, R1)[row]:(R0, R1)[row] + EXPERTS])
                last.then_inc(pair_sem["RT"], 1)

            def turn_gates(i, a, k):
                step = ("CT", None, 0)
                pe.wait_ge(pair_sem["router"], nth("router", i, ROUTER_STEPS - 1))
                if ring_used(step, i):
                    pe.wait_ge(ring_reader(step), ring_count(step, i))
                for q in range(4):
                    last = nc.tensor.transpose(ring_bank(step)[0:32, 0:TC].bitcast(F16)[:, q * TR:(q + 1) * TR],
                                               gates_hl[:, q, :], ident16[0:TR, 0:TR])
                last.then_inc(pair_sem["CT"], 1)

            def ffn_up(dst, m, col):
                n = UNIT_ROWS[m]
                lo = col + 128 * m
                return dense(dst[0:n, 0:PT],
                             lambda blk, w, row: w[:, (UP0, UP1)[row] + lo:(UP0, UP1)[row] + lo + n],
                             lambda blk, w, row: xp[:, blk, :])

            def ffn_gate(j, m):
                if m == 0:
                    pe.wait_ge(sem["x3_turned"][0], nth("x3_turned", j))
                    pe.wait_ge(sem["x3_turned"][1], nth("x3_turned", j))
                    pe.wait_ge(pair_sem["gates_turned"], nth("gates_turned", j))
                if m < ROUTED:
                    if m >= 1:
                        pe.wait_ge(pair_sem["gate_copied"], nth("gate_copied", j, m - 1))
                    mm(bank_c[:, 0:PT], select_sb[:, m, :], ct[:, :], start=True, stop=True).then_inc(pair_sem["CB"], 1)
                if m >= 1:
                    pe.wait_ge(pair_sem["gated"], nth("gated", j, m - 1))
                ffn_up(bank_g, m, 0).then_inc(pair_sem["G"], 1)

            def ffn_value(j, m):
                if m >= 1:
                    pe.wait_ge(pair_sem["upped"], nth("upped", j, m - 1))
                ffn_up(bank_u, m, HID).then_inc(pair_sem["U"], 1)

            def ffn_down(j, q):
                a, t = divmod(q, 2)
                pe.wait_ge(pair_sem["hidden"], nth("hidden", j, UNITS - 1))
                if a == 1:
                    pe.wait_ge(pair_sem["result"], nth("result", j, 0))
                else:
                    if later(j):
                        pe.wait_ge(pair_sem["result"], nth("result", j - 1, 1))
                dst = bank_d[0:TR, t * C:(t + 1) * C]
                mm(dst, ct[:, q * TR:(q + 1) * TR], gbd_high[:, :], start=True, stop=False)
                mm(dst, ct[:, q * TR:(q + 1) * TR], gbd_low[:, :], start=False, stop=False)
                for m in range(UNITS):
                    n = UNIT_ROWS[m]
                    last = mm(dst, hid[0:n, m, q * TR:(q + 1) * TR], wd_sb[0:n, m, :], start=False,
                              stop=m == UNITS - 1)
                last.then_inc(pair_sem["DN"], 1)

            run(walk(dict(EM=embed, MEAN=moment("MEAN", rsum, "row_sums", 0), VAR=moment("VAR", sq, "squares", 1),
                          XT=turn_x, Q=project("Q", QW), K=project("K", KW), V=project_v, S1=scores, MT=turn_max,
                          S2=scores_less_max, PV=attend, OT=turn_heads, XT2=turn_norm("XT2", "ln2"),
                          KV=linear_kv, LQ=linear_q, KVT=linear_kv_product, GW=fold_projection, Y=linear_out,
                          XT3=turn_norm("XT3", "ln3"), RT=router, CT=turn_gates),
                     dict(G=ffn_gate, U=ffn_value, DN=ffn_down)))(pe)


def layout(np, pairs, x, L0_tok_W_map, L0_tok_b_map, L0_tok_class_token, L0_tok_ln_w, L0_tok_ln_b, L0_tok_Wq, L0_tok_bq,
           L0_tok_Wk, L0_tok_bk, L0_tok_Wv, L0_tok_bv, L0_attn_w_qkv, L0_attn_w_proj, L0_attn_b_proj,
           L0_ffn_router_w, L0_ffn_router_b, L0_ffn_corr_bias, L0_ffn_gWg, L0_ffn_gbg, L0_ffn_gWu, L0_ffn_gbu,
           L0_ffn_gWd, L0_ffn_gbd, L0_ffn_sWg, L0_ffn_sbg, L0_ffn_sWu, L0_ffn_sbu, L0_ffn_sWd, L0_ffn_sbd):
    f = np.float32
    A = {}
    xt = np.zeros((pairs, 128, CIN, 2, TC), f)
    xt[..., 0:PATCHES] = x.reshape(pairs, 2, PATCHES, CIN, 128).transpose(0, 4, 3, 1, 2)
    A["x"] = xt
    A["w_patch"] = L0_tok_W_map.T.reshape(CIN, 128, C).transpose(1, 0, 2)

    def tokens(rows_of_patches, row_of_class):
        t = np.zeros((TC, C), f)
        t[0:PATCHES] = rows_of_patches
        t[PATCHES] = row_of_class
        return t.reshape(2, TR, C).transpose(1, 0, 2)

    s = np.arange(SEQ, dtype=f)[:, None]
    d = np.arange(C, dtype=f)[None, :]
    even = (np.arange(C) % 2 == 0)[None, :]
    pos = np.where(even, np.sin(s / np.power(f(10000.0), d / f(C))),
                   np.cos(s / np.power(f(10000.0), (d - f(1.0)) / f(C)))).astype(f)
    A["pos"] = tokens(pos[1:], pos[0])
    A["tok_add"] = tokens(L0_tok_b_map, L0_tok_class_token[0])
    A["ln_w"] = tokens(L0_tok_ln_w[1:], L0_tok_ln_w[0])
    A["ln_b"] = tokens(L0_tok_ln_b[1:], L0_tok_ln_b[0])

    W = np.zeros((128, SPLIT), f)

    def twice(w):
        return np.concatenate([w[128:C], w[128:C]], 0)

    def hidden_columns(of_experts, shared):
        return np.concatenate([of_experts.transpose(1, 0, 2).reshape(C, EXPERTS * INNER), shared], 1)

    up = np.concatenate([hidden_columns(L0_ffn_gWg, L0_ffn_sWg), hidden_columns(L0_ffn_gWu, L0_ffn_sWu)], 1)
    W[:, UP0:UP0 + 2 * HID] = up[0:128]
    W[:, UP1:UP1 + 2 * HID] = twice(up)
    for col, w in ((QW, L0_tok_Wq), (KW, L0_tok_Wk)):
        for j in range(6):
            r = 64 * (j % 2)
            for y in range(2):
                for copy in range(3):
                    c0 = col + 96 * j + 32 * copy + 16 * y
                    for half in range(2):
                        r0 = r + 32 * half + 16 * y
                        W[r0:r0 + 16, c0:c0 + 16] = w[2 * j + y].T
    for b in range(3):
        for y in range(4):
            for half in range(2):
                r0 = 64 * (y // 2) + 32 * half + 16 * (y % 2)
                c0 = VW + 64 * b + 16 * y
                W[r0:r0 + 16, c0:c0 + 16] = L0_tok_Wv[4 * b + y].T
    W[:, L0:L0 + 3 * C] = L0_attn_w_qkv[0:128]
    W[:, L1:L1 + 3 * C] = twice(L0_attn_w_qkv)
    W[:, R0:R0 + EXPERTS] = L0_ffn_router_w.T[0:128]
    W[:, R1:R1 + EXPERTS] = twice(L0_ffn_router_w.T)
    A["w_split"] = W
    for name, b in (("bq", L0_tok_bq), ("bk", L0_tok_bk)):
        A[name] = np.concatenate([b.reshape(6, 32).T] * 3, 0)

    def rows(v, n=TR):
        return np.broadcast_to(v.reshape(1, -1), (n, v.size))

    A["bv"] = rows(L0_tok_bv)
    wproj = np.zeros((128, 2, C), f)
    wproj[:, 0] = L0_attn_w_proj[0:128]
    wproj[0:64, 1] = L0_attn_w_proj[128:C]
    A["w_proj"] = wproj
    A["b_proj"] = rows(L0_attn_b_proj)
    A["router_b"] = rows(L0_ffn_router_b)
    A["corr_b"] = rows(L0_ffn_corr_bias)
    wd = np.zeros((UNITS * 128, C), f)
    wd[0:HID] = np.concatenate([L0_ffn_gWd.reshape(EXPERTS * INNER, C), L0_ffn_sWd], 0)
    A["w_down"] = wd.reshape(UNITS, 128, C).transpose(1, 0, 2)
    A["down_b"] = np.concatenate([L0_ffn_gbd, L0_ffn_gbd], 0)
    A["shared_b"] = rows(L0_ffn_sbd)
    for name, of_experts, shared in (("gate_bias", L0_ffn_gbg, L0_ffn_sbg), ("up_bias", L0_ffn_gbu, L0_ffn_sbu)):
        b = np.zeros((UNITS * 128,), f)
        b[0:HID] = np.concatenate([of_experts.reshape(-1), shared], 0)
        A[name] = b.reshape(UNITS, 128).T
    expert = np.arange(ROUTED * 128) // INNER
    sel = (np.arange(EXPERTS)[:, None] == expert[None, :]).astype(np.float16)
    A["select"] = np.concatenate([sel, sel], 0).reshape(32, ROUTED, 128)
    c32 = np.zeros((128, 438), f)
    c32[:, 0:128] = np.eye(128, dtype=f)
    p = np.arange(128)
    c32[:, 128:256] = p[:, None] // DH == p[None, :] // DH
    c32[:, 256:320] = p[:, None] // DH == p[None, 0:64] // DH
    for odd in range(2):
        c32[:, 320 + odd] = (p // DH) % 2 == odd
    c32[:, 322:422] = 1.0 / (SEQ * C)
    g = np.arange(GROUPS)
    c32[:, 422:438] = (g[None, :] < g[:, None]).astype(f).reshape(1, 16)
    A["consts32"] = c32
    c16 = np.zeros((128, 128 + HEADS * TC), np.float16)
    c16[:, 0:128] = np.eye(128, dtype=np.float16)
    for h in range(HEADS):
        c16[96 + h, 128 + TC * h:128 + TC * (h + 1)] = -1.0
    A["consts16"] = c16
    return A


NAMES = ["x", "w_patch", "pos", "tok_add", "ln_w", "ln_b", "w_split", "bq", "bk", "bv", "w_proj", "b_proj",
         "router_b", "corr_b", "w_down", "down_b", "shared_b", "gate_bias", "up_bias", "select",
         "consts32", "consts16"]


def kernel(**inputs):
    import numpy as np
    import concourse.bacc as bacc
    from concourse.bass_utils import run_bass_kernel_spmd

    pairs = inputs["x"].shape[0] // 2
    arrays = {k: np.ascontiguousarray(v) for k, v in
              layout(np, pairs, **{k: np.asarray(v) for k, v in inputs.items()}).items()}
    nc = bacc.Bacc("TRN2", target_bir_lowering=False, num_devices=1)
    args = [nc.dram_tensor(f"in_{n}", arrays[n].shape, mybir.dt.from_np(arrays[n].dtype), kind="ExternalInput").ap()
            for n in NAMES]
    args.append(nc.dram_tensor("out_0", (pairs, TR, 2, 2, C), F32, kind="ExternalOutput").ap())
    vit_tower(nc, *args)
    r = run_bass_kernel_spmd(nc, [{f"in_{n}": arrays[n] for n in NAMES}], core_ids=[0])
    got = np.asarray(r.results[0]["out_0"]).transpose(0, 2, 3, 1, 4).reshape(2 * pairs, TC, C)
    return np.concatenate([got[:, PATCHES:SEQ], got[:, 0:PATCHES]], 1)
```

```python
from contextlib import ExitStack

import concourse.bass as bass
from concourse import mybir

F32 = mybir.dt.float32
F16 = mybir.dt.float16
I32 = mybir.dt.int32
ALU = mybir.AluOpType
ACT = mybir.ActivationFunctionType
AX = mybir.AxisListType

IMAGES, PATCHES, PATCH_IN = 128, 196, 768
C, HEADS, DH = 192, 12, 16
SEQ = PATCHES + 1
TR = 100
TC = 2 * TR
PT = 2 * TC
LIVE = (TR, SEQ - TR)
EXPERTS, INNER, GROUPS = 16, 96, 4
UNITS = 14
ROUTED = EXPERTS * INNER // 128
UNIT_ROWS = [128] * 13 + [64]
HID = EXPERTS * INNER + 2 * INNER
CIN = PATCH_IN // 128
EPS = 1e-5
ROUTER_STEPS = 31
RSQRT_STEPS, RSQRT_ROUNDS, RSQRT_GUESS = 14, 3, float(0x5F3759DF)
SENTINEL, TAKEN = -1.0e30, -3.0e38

UP0, AT0 = 0, 2 * HID
QW, KW, VW = AT0, AT0 + 576, AT0 + 1152
SPLIT_A = AT0 + 1344
UP1 = SPLIT_A
L0 = UP1 + 2 * HID
L1 = L0 + 3 * C
R0 = L1 + 3 * C
R1 = R0 + EXPERTS
SPLIT = R1 + EXPERTS

PE_STAGES = dict(EM=1, MEAN=1, VAR=1, XT=1, Q=3, K=3, V=1, S1=12, MT=1, S2=12, PV=3, OT=2,
                 XT2=1, KV=2, LQ=1, KVT=1, GW=1, Y=1, XT3=1)
MADE = dict(variance=1, ln2_rstd=RSQRT_STEPS, ln3_rstd=RSQRT_STEPS, tokens=1, row_sums=1, neg_mean=1, squares=2, rstd=RSQRT_STEPS, centred=1, normed=1, x_high=1,
            x_low=1, x_turned=1, q_full=3, q_high=3, q_low=3, k_full=3, k_high=3, k_low=3,
            k_masked=6, v_made=1, row_max=12, max_turned=1, probs=12, heads_out=3, recip=2,
            heads=2, h1=2, h1_biased=1, ln2=6, ln2_high=2, ln2_low=2, x2_turned=1, kv=2,
            gelu_q=2, gelu_kv=2, gelu_kv_masked=2, kv_proj=2, h2=1, h2_biased=1, ln3=6,
            ln3_high=2, ln3_low=2, x3_turned=1)
PAIR = dict(RT=1, CT=1, router=ROUTER_STEPS, router_exp=1, gates_turned=1, CB=12, G=14, U=14, DN=4,
            gate_copied=12, tanh=14, gated=14, upped=14, hidden=14, result=2, stored=1, loaded=1)
READ_BY = dict(EM="tokens", MEAN="neg_mean", VAR="variance", XT="x_turned", Q="q_full", K="k_full",
               V="v_made", S1="row_max", MT="max_turned", S2="probs", PV="heads_out", OT="heads",
               XT2="x2_turned", KV="kv", LQ="gelu_q", KVT="gelu_kv", GW="kv_proj", Y="h2",
               XT3="x3_turned", RT="router", CT="gates_turned")
LAST_READ = dict(LQ=1, KVT=1, GW=1)


BACK = dict(HS=1, LN3A=1, XT3=1, RT=1, ROUTE=1, CT=1, G=1, U=1, DN=1, DN_LAST=2)
MOST_BACK = 2


def schedule():
    ups = [(s, m, 0) for m in range(UNITS) for s in ("G", "U")]
    downs = [("DN", q, half) for q in range(3) for half in range(2)]
    out = []

    def fill(of, n=1):
        for _ in range(min(n, len(of))):
            out.append(of.pop(0))

    def add(a, *stages):
        for s in stages:
            out.extend((s, a, k) for k in range(PE_STAGES.get(s, 1)))

    add(0, "LN3A", "EM", "EM_END")
    add(1, "LN3A")
    add(0, "XT3")
    add(1, "EM")
    add(0, "MEAN")
    add(1, "XT3", "EM_END")
    add(0, "VAR")
    add(None, "RT")
    out.append(("DN_LAST", 3, 0))
    add(1, "MEAN")
    add(0, "N1")
    add(1, "VAR")
    add(None, "ROUTE")
    out.append(("DN_LAST", 3, 1))
    add(0, "XT")
    add(1, "N1")
    add(0, "Q")
    add(1, "XT")
    add(0, "K")
    add(None, "CT")
    add(0, "V", "HS")
    add(1, "Q", "HS")
    fill(ups)
    add(1, "K")
    fill(ups)
    add(1, "V")
    for k in range(12):
        out.append(("S1", 0, k))
        if k % 2:
            fill(ups)
    fill(ups)
    add(0, "MT")
    fill(ups)
    for k in range(12):
        out.append(("S1", 1, k))
        out.append(("S2", 0, k))
        if k in (5, 9):
            out.append(("PV", 0, k // 4 - 1))
        if k % 6 != 5:
            fill(ups)
    fill(ups)
    out.append(("PV", 0, 2))
    add(1, "MT")
    fill(ups)
    add(0, "OT", "LN2S")
    for k in range(12):
        out.append(("S2", 1, k))
        if k in (5, 9):
            out.append(("PV", 1, k // 4 - 1))
        if k == 3:
            add(0, "LN2A")
        if k == 7:
            add(0, "XT2")
        if k == 9:
            add(0, "KV")
        fill(ups)
    fill(ups, len(ups))
    fill(downs)
    out.append(("PV", 1, 2))
    add(0, "LQ", "KVT")
    add(1, "OT", "LN2S")
    fill(downs)
    add(0, "GW")
    fill(downs)
    add(1, "LN2A")
    add(0, "Y")
    add(1, "XT2")
    add(0, "LN3S")
    add(1, "KV", "LQ")
    fill(downs)
    add(1, "KVT")
    fill(downs)
    add(1, "GW")
    fill(downs)
    add(1, "Y", "LN3S")
    return out


def vit_tower(nc, x, w_patch, pos, tok_add, ln_w, ln_b, w_split, bq, bk, bv, w_proj, b_proj,
              router_b, corr_b, w_down, down_b, shared_b, gate_bias, up_bias, select,
              consts32, consts16, out):
    pairs = x.shape[0]
    steps = schedule()
    ring = [s for s in steps if s[0] in PE_STAGES or s[0] in ("RT", "CT")]
    assert len(ring) % 4 == 0
    place = {s: n for n, s in enumerate(ring)}

    ctx = ExitStack()
    with ctx:
        def sb(name, shape, dt=F32):
            return ctx.enter_context(nc.sbuf_tensor(name, shape, dt))

        def two(name, shape, dt=F32):
            return [sb(f"{name}{a}", shape, dt) for a in range(2)]

        w_high, w_low = sb("w_high", [128, SPLIT], F16), sb("w_low", [128, SPLIT], F16)
        wp_sb = sb("wp_sb", [128, CIN, C])
        wd_sb = sb("wd_sb", [128, UNITS, C])
        wproj_sb = sb("wproj_sb", [128, 2, C])
        table = sb("table", [TR, 2, C])
        lnw_sb, lnb_sb = sb("lnw_sb", [TR, 2, C]), sb("lnb_sb", [TR, 2, C])
        bq_sb, bk_sb = sb("bq_sb", [96, 6]), sb("bk_sb", [96, 6])
        bv_sb, bproj_sb, sbd_sb = sb("bv_sb", [TR, C]), sb("bproj_sb", [TR, C]), sb("sbd_sb", [TR, C])
        rb_sb, corr_sb = sb("rb_sb", [TR, EXPERTS]), sb("corr_sb", [TR, EXPERTS])
        gbd_sb = sb("gbd_sb", [32, C])
        gbd_high, gbd_low = sb("gbd_high", [32, C], F16), sb("gbd_low", [32, C], F16)
        gbias, ubias, half_gbias = sb("gbias", [128, UNITS]), sb("ubias", [128, UNITS]), sb("half_gbias", [128, UNITS])
        select_sb = sb("select_sb", [32, ROUTED, 128], F16)
        c32 = sb("c32", [128, consts32.shape[1]])
        ident32, bd_mask = c32[:, 0:128], c32[:, 128:320]
        head_mask, mean_w, before = c32[:, 320:322], c32[:, 322:422], c32[:, 422:438]
        c16 = sb("c16", [128, 128], F16)
        ident16 = c16[:, :]

        xin = sb("xin", [128, CIN, 2, TC])
        tok, h1 = two("tok", [TR, 2, C]), two("h1", [TR, 2, C])
        xa, xb = two("xa", [TR, 2, C]), two("xb", [TR, 2, C])
        tok_add_sb = h1[0]
        ms, h1b = xa, xa
        rsum, nmean, sq, rstd, var = two("rsum", [TR, 2]), two("nmean", [TR, 1]), two("sq", [TR, 2]), two("rstd", [TR, 1]), two("var", [TR, 1])
        x3 = two("x3", [TR, 2, 6, 64], F16)
        xt = two("xt", [128, 3, TC], F16)
        qf = two("qf", [128, 6, TC])
        kf = qf
        qs, kh = two("qs", [128, 6, TC], F16), two("kh", [96, 6, TC], F16)
        ks = two("ks", [128, HEADS, TC], F16)
        vp = two("vp", [TR, 2, HEADS, 32])
        mx = two("mx", [TR, 2, HEADS], F16)
        probs = sb("probs", [128, HEADS, 2, TC])
        ots = [b[:, 0:3, :] for b in qf]
        rec = two("rec", [TR, 2, HEADS])
        bns, bna, rs2 = two("bns", [TR, 2, 6]), two("bna", [TR, 2, 2]), two("rs2", [TR, 2])
        xn = xb
        xs = [b[:, :, :, :].rearrange("p t j c -> p t (j c)") for b in x3]
        xt2 = xt
        eps = sb("eps", [TR, 2])
        work = two("work", [TR, 2, 2])
        kv, gkv, gw = two("kv", [TR, 2, 2 * C]), two("gkv", [128, C]), two("gw", [128, 2, C])
        h2 = [b[:, :, 0:C] for b in kv]
        gq, gkvm = [b[:, 3:5, :] for b in qf], gkv

        xp = sb("xp", [128, 3, PT], F16)
        ct = sb("ct", [32, PT], F16)
        hs = sb("hs", [TR, 2, 2, C])
        res = sb("res", [TR, 2, 2, C])
        z, ez, s1, score, sf = (sb(n, [TR, 4, EXPERTS]) for n in ("z", "ez", "s1", "score", "sf"))
        psum2 = sb("psum2", [TR, 16, 6])
        gs, rank, keep = (sb(n, [TR, 16]) for n in ("gs", "rank", "keep"))
        gt, eq, eql, beats = (sb(n, [TR, 4, 4, 4]) for n in ("gt", "eq", "eql", "beats"))
        sm, mr = sb("sm", [TR, 4, 20]), sb("mr", [TR, 4, 20])
        top8 = sb("top8", [TR, 4, 8])
        wsel, gates = sb("wsel", [TR, 4, EXPERTS]), sb("gates", [TR, 4, EXPERTS])
        den, den1, rden = (sb(n, [TR, 4]) for n in ("den", "den1", "rden"))
        gates_hl = sb("gates_hl", [TR, 4, 32], F16)
        cs, th, ga = (two(n, [128, PT]) for n in ("cs", "th", "ga"))
        ub = ga
        hid = sb("hid", [128, UNITS, PT])

        bank = [ctx.enter_context(nc.psum_tensor(f"ring{n}", [128, 512], F32)) for n in range(4)]
        bank_g, bank_u, bank_c, bank_d = (ctx.enter_context(nc.psum_tensor(n, [128, 512], F32))
                                          for n in ("bank_g", "bank_u", "bank_c", "bank_d"))

        sem = {n: [ctx.enter_context(nc.semaphore(f"{n}_{a}")) for a in range(2)]
              for n in (*PE_STAGES, *MADE)}
        pair_sem = {n: ctx.enter_context(nc.semaphore(n)) for n in PAIR}
        per = {**PE_STAGES, **MADE, **PAIR}
        consts_in = ctx.enter_context(nc.semaphore("consts_in"))
        stage_in = [ctx.enter_context(nc.semaphore(f"stage_in{n}")) for n in range(2)]
        init_done = ctx.enter_context(nc.semaphore("init_done"))
        pool_init = ctx.enter_context(nc.semaphore("pool_init"))
        init_chain = ctx.enter_context(nc.semaphore("init_chain"))

        def nth(name, i, k=0):
            return per[name] * i + k + 1

        def later(i):
            return not isinstance(i, int) or i > 0

        def ring_bank(step):
            return bank[place[step] % 4]

        def last_tenant(step, i):
            n, it = place[step] - 4, i + BACK.get(step[0], 0)
            while True:
                if n < 0:
                    n, it = n + len(ring), it - 1
                pair = it - BACK.get(ring[n][0], 0)
                if not isinstance(it, int) or 0 <= pair < pairs:
                    return ring[n], pair
                if it < 0:
                    return ring[n], None
                n -= 4

        def ring_used(step, i):
            return last_tenant(step, i)[1] is not None

        def ring_reader(step, i):
            (stage, a, _), _ = last_tenant(step, i)
            return pair_sem[READ_BY[stage]] if a is None else sem[READ_BY[stage]][a]

        def ring_count(step, i):
            (stage, _, k), pair = last_tenant(step, i)
            return nth(READ_BY[stage], pair, LAST_READ.get(stage, k))

        def walk(eng, parts, stop=pairs):
            def iteration(it):
                for step in steps:
                    pair = it - BACK.get(step[0], 0)
                    if step[0] in parts and (not isinstance(it, int) or 0 <= pair < pairs):
                        parts[step[0]](pair, *step[1:])
            for it in range(MOST_BACK + 1):
                iteration(it)
            with eng.Fori(MOST_BACK + 1, stop) as it:
                iteration(it)
            for it in range(stop, pairs + MOST_BACK):
                iteration(it)

        staged = [probs[:, :, :, :].rearrange("p h t n -> p (h t n)")[:, 0:SPLIT_A],
                  hid[:, :, :].rearrange("p m n -> p (m n)")[:, 0:SPLIT - SPLIT_A]]
        block = ctx.enter_context(nc.Block())

        @block.sync
        def _(sp):
            sp.dma_start(staged[0],
                         w_split[:, 0:SPLIT_A]).then_inc(stage_in[0], 16)
            sp.dma_start(staged[1],
                         w_split[:, SPLIT_A:SPLIT]).then_inc(stage_in[1], 16)
            sp.dma_start(xin[:, :, :, :], x[0]).then_inc(pair_sem["loaded"], 16)
            for dst, src in ((wp_sb[:, :, :], w_patch), (wd_sb[:, :, :], w_down), (wproj_sb[:, :, :], w_proj),
                             (table[:, :, :], pos), (tok_add_sb[:, :, :], tok_add), (lnw_sb[:, :, :], ln_w),
                             (lnb_sb[:, :, :], ln_b), (bq_sb[:, :], bq), (bk_sb[:, :], bk), (bv_sb[:, :], bv),
                             (bproj_sb[:, :], b_proj), (sbd_sb[:, :], shared_b), (rb_sb[:, :], router_b),
                             (corr_sb[:, :], corr_b), (gbd_sb[:, :], down_b), (gbias[:, :], gate_bias),
                             (ubias[:, :], up_bias), (select_sb[:, :, :], select), (c32[:, :], consts32),
                             (c16[:, :], consts16[:, 0:128]),
                             ):
                sp.dma_start(dst, src).then_inc(consts_in, 16)
            sp.wait_ge(pool_init, 4)
            for a in range(2):
                sp.dma_start(ks[a][96:128, :, :],
                             consts16[96:128, 128:128 + HEADS * TC].rearrange("p (h n) -> p h n", h=HEADS)
                             ).then_inc(consts_in, 16)

            def load_next(i, a, k):
                if a == 0 or (isinstance(i, int) and i == pairs - 1):
                    return
                sp.wait_ge(sem["EM"][0], nth("EM", i))
                sp.wait_ge(sem["EM"][1], nth("EM", i))
                if isinstance(i, int):
                    src = x[i + 1]
                else:
                    src = x[bass.ds(i + 1, 1)].rearrange("o p c a n -> p (o c) a n")
                sp.dma_start(xin[:, :, :, :], src).then_inc(pair_sem["loaded"], 16)

            def store(j, q, half):
                if half == 0:
                    return
                sp.wait_ge(pair_sem["result"], nth("result", j, 1))
                if isinstance(j, int):
                    dst = out[j]
                else:
                    dst = out[bass.ds(j, 1)].rearrange("o p a t c -> p (o a) t c")
                sp.dma_start(dst, res[:, :, :, :]).then_inc(pair_sem["stored"], 16)

            walk(sp, dict(EM_END=load_next, DN_LAST=store), stop=pairs - 1)
            sp.wait_ge(pair_sem["stored"], 16 * pairs)

        CONSTS = 16 * 22

        @block.gpsimd
        def _(pool):
            for a in range(2):
                pool.memset(vp[a][:, :, :, 16:32], 1.0).then_inc(pool_init, 1)
                pool.wait_ge(pool_init, 2 * a + 1)
                pool.memset(qs[a][96:128, :, :], 0.0).then_inc(pool_init, 1)
                pool.wait_ge(pool_init, 2 * a + 2)
            pool.memset(sm[:, :, 16:20], SENTINEL).then_inc(pool_init, 1)
            pool.memset(eps[:, :], EPS).then_inc(pool_init, 1)
            pool.wait_ge(pool_init, 6)
            pool.wait_ge(consts_in, CONSTS)
            pool.wait_ge(init_done, 1)

            def rsqrt(i, a, y, variance, tmp, name):
                v, t = tmp[:, 0, :], tmp[:, 1, :]
                steps_done = [0]

                def step(ins):
                    ins.then_inc(sem[name][a], 1)
                    pool.drain()
                    steps_done[0] += 1

                step(nc.gpsimd.tensor_tensor(v, variance, eps[:, 0:variance.shape[1]], ALU.add))
                step(nc.gpsimd.tensor_scalar(y[:, :].bitcast(I32), v.bitcast(I32), -0.5, RSQRT_GUESS, ALU.mult, ALU.add))
                for _ in range(RSQRT_ROUNDS):
                    step(nc.gpsimd.tensor_tensor(t, y[:, :], y[:, :], ALU.mult))
                    step(nc.gpsimd.tensor_tensor(t, t, v, ALU.mult))
                    step(nc.gpsimd.tensor_scalar(t, t, -0.5, 1.5, ALU.mult, ALU.add))
                    step(nc.gpsimd.tensor_tensor(y[:, :], y[:, :], t, ALU.mult))
                assert steps_done[0] == RSQRT_STEPS

            def rsqrt_x(i, a, k):
                pool.drain()
                pool.wait_ge(sem["variance"][a], nth("variance", i))
                rsqrt(i, a, rstd[a], var[a][:, :], work[a][:, :, 0:1], "rstd")

            def low_of_x(i, a, k):
                pool.drain()
                pool.wait_ge(sem["x_high"][a], nth("x_high", i))
                pool.wait_ge(sem["normed"][a], nth("normed", i))
                nc.gpsimd.tensor_tensor(x3[a][:, :, :, 32:64], xb[a][:, :, :].rearrange("p t (j c) -> p t j c", c=32),
                                        x3[a][:, :, :, 0:32], ALU.subtract).then_inc(sem["x_low"][a], 1)

            def low_of_q(i, a, k):
                pool.drain()
                pool.wait_ge(sem["q_high"][a], nth("q_high", i, k))
                pool.wait_ge(sem["q_full"][a], nth("q_full", i, k))
                nc.gpsimd.tensor_tensor(qs[a][32:64, 2 * k:2 * k + 2, :], qf[a][32:64, 2 * k:2 * k + 2, :],
                                        qs[a][32:64, 2 * k:2 * k + 2, :], ALU.subtract).then_inc(sem["q_low"][a], 1)

            def low_of_k(i, a, k):
                pool.drain()
                pool.wait_ge(sem["k_high"][a], nth("k_high", i, k))
                pool.wait_ge(sem["k_full"][a], nth("k_full", i, k))
                nc.gpsimd.tensor_tensor(kh[a][64:96, 2 * k:2 * k + 2, :], kf[a][64:96, 2 * k:2 * k + 2, :],
                                        kh[a][64:96, 2 * k:2 * k + 2, :], ALU.subtract).then_inc(sem["k_low"][a], 1)

            def residual(i, a, t):
                pool.drain()
                pool.wait_ge(sem["heads"][a], nth("heads", i, t))
                pool.wait_ge(sem["tokens"][a], nth("tokens", i))
                nc.gpsimd.tensor_tensor(h1[a][:, t, :], tok[a][:, t, :], ms[a][:, t, :], ALU.add
                                        ).then_inc(sem["h1"][a], 1)

            def rsqrt_norm(i, a, name):
                pool.drain()
                pool.wait_ge(sem[name][a], nth(name, i, 3))
                rsqrt(i, a, rs2[a], bna[a][:, :, 1], work[a], name + "_rstd")

            def lows_of_norm(i, a, name):
                pool.drain()
                pool.wait_ge(sem[name + "_high"][a], nth(name + "_high", i, 1))
                pool.wait_ge(sem[name][a], nth(name, i, 5))
                nc.gpsimd.tensor_tensor(xs[a][:, :, 128:256], xn[a][:, :, 0:128], xs[a][:, :, 0:128],
                                        ALU.subtract).then_inc(sem[name + "_low"][a], 1)
                nc.gpsimd.tensor_tensor(xs[a][:, :, 320:384], xn[a][:, :, 128:192], xs[a][:, :, 256:320],
                                        ALU.subtract).then_inc(sem[name + "_low"][a], 1)

            def norm2(i, a, k):
                lows_of_norm(i, a, "ln2")
                nc.gpsimd.tensor_tensor(h1b[a][:, :, :], h1[a][:, :, :],
                                        bproj_sb[:, :].unsqueeze(1).to_broadcast([TR, 2, C]), ALU.add
                                        ).then_inc(sem["h1_biased"][a], 1)

            def mask_kv(i, a, k):
                pool.drain()
                pool.wait_ge(sem["gelu_kv"][a], nth("gelu_kv", i, 1))
                nc.gpsimd.tensor_tensor(gkvm[a][:, 0:128], gkv[a][:, 0:128], bd_mask[:, 0:128], ALU.mult
                                        ).then_inc(sem["gelu_kv_masked"][a], 1)
                nc.gpsimd.tensor_tensor(gkvm[a][0:64, 128:192], gkv[a][0:64, 128:192], bd_mask[0:64, 128:192],
                                        ALU.mult).then_inc(sem["gelu_kv_masked"][a], 1)

            def residual2(i, a, k):
                pool.drain()
                if later(i):
                    pool.wait_ge(pair_sem["result"], nth("result", i - 1, 1))
                nc.gpsimd.tensor_tensor(hs[:, a, :, :], h2[a][:, :, :],
                                        sbd_sb[:, :].unsqueeze(1).to_broadcast([TR, 2, C]), ALU.add
                                        ).then_inc(sem["h2_biased"][a], 1)

            walk(pool, dict(VAR=rsqrt_x, N1=low_of_x, Q=low_of_q, K=low_of_k, OT=residual,
                          LN2S=lambda i, a, k: rsqrt_norm(i, a, "ln2"), LN2A=norm2, KVT=mask_kv,
                          LN3S=lambda i, a, k: rsqrt_norm(i, a, "ln3"),
                          LN3A=lambda i, a, k: lows_of_norm(i, a, "ln3"), HS=residual2))

        @block.scalar
        def _(act):
            act.wait_ge(init_done, 1)
            act.wait_ge(consts_in, CONSTS)

            def moments(i, a, k):
                act.wait_ge(sem["MEAN"][a], nth("MEAN", i))
                nc.scalar.activation(nmean[a][:, :], ring_bank(("MEAN", a, 0))[0:TR, 0:1], ACT.Copy, scale=-1.0
                                     ).then_inc(sem["neg_mean"][a], 1)
                act.wait_ge(sem["neg_mean"][a], nth("neg_mean", i))
                for t in range(2):
                    n = LIVE[t]
                    nc.scalar.activation(xa[a][0:n, t, :], tok[a][0:n, t, :], ACT.Square,
                                         bias=nmean[a][0:n, :], accum_out=sq[a][0:n, t:t + 1]
                                         ).then_inc(sem["squares"][a], 1)

            def high_of_x(i, a, k):
                act.wait_ge(sem["normed"][a], nth("normed", i))
                nc.scalar.activation(x3[a][:, :, :, 0:32], xb[a][:, :, :].rearrange("p t (j c) -> p t j c", c=32),
                                     ACT.Copy).then_inc(sem["x_high"][a], 1)

            def x_out(i, a, k):
                act.wait_ge(sem["XT"][a], nth("XT", i))
                nc.scalar.activation(xt[a][:, :, :], turned(("XT", a, 0)), ACT.Copy).then_inc(sem["x_turned"][a], 1)

            def turned(step):
                return ring_bank(step)[:, 0:300].bitcast(F16).rearrange("p (b n) -> p b n", b=3)

            def high_of_q(i, a, k):
                act.wait_ge(sem["q_full"][a], nth("q_full", i, k))
                nc.scalar.activation(qs[a][0:96, 2 * k:2 * k + 2, :], qf[a][0:96, 2 * k:2 * k + 2, :], ACT.Copy
                                     ).then_inc(sem["q_high"][a], 1)

            def high_of_k(i, a, k):
                act.wait_ge(sem["k_full"][a], nth("k_full", i, k))
                nc.scalar.activation(kh[a][:, 2 * k:2 * k + 2, :], kf[a][0:96, 2 * k:2 * k + 2, :], ACT.Copy
                                     ).then_inc(sem["k_high"][a], 1)

            def exponents(i, a, h):
                act.wait_ge(sem["S2"][a], nth("S2", i, h))
                if a == 1:
                    act.wait_ge(sem["PV"][0], nth("PV", i, h // 4))
                else:
                    if later(i):
                        act.wait_ge(sem["PV"][1], nth("PV", i - 1, h // 4))
                nc.scalar.activation(probs[0:TR, h, :, :],
                                     ring_bank(("S2", a, h))[0:TR, 0:2 * TC].rearrange("p (t n) -> p t n", t=2),
                                     ACT.Exp, scale=DH ** -0.5).then_inc(sem["probs"][a], 1)

            def heads_out(i, a, g):
                act.wait_ge(sem["PV"][a], nth("PV", i, g))
                nc.scalar.activation(ots[a][:, g, :], ring_bank(("PV", a, g))[:, 0:TC], ACT.Copy
                                     ).then_inc(sem["heads_out"][a], 1)

            def highs_of_norm(i, a, name):
                act.wait_ge(sem[name][a], nth(name, i, 5))
                nc.scalar.activation(xs[a][:, :, 0:128], xn[a][:, :, 0:128], ACT.Copy
                                     ).then_inc(sem[name + "_high"][a], 1)
                nc.scalar.activation(xs[a][:, :, 256:320], xn[a][:, :, 128:192], ACT.Copy
                                     ).then_inc(sem[name + "_high"][a], 1)

            def x2_out(i, a, k):
                act.wait_ge(sem["XT2"][a], nth("XT2", i))
                nc.scalar.activation(xt2[a][:, :, :], turned(("XT2", a, 0)), ACT.Copy
                                     ).then_inc(sem["x2_turned"][a], 1)

            def kv_out(i, a, t):
                act.wait_ge(sem["KV"][a], nth("KV", i, t))
                nc.scalar.activation(kv[a][:, t, :], ring_bank(("KV", a, t))[0:TR, 0:2 * C], ACT.Copy
                                     ).then_inc(sem["kv"][a], 1)

            def gelu_q(i, a, k):
                b = ring_bank(("LQ", a, 0))
                act.wait_ge(sem["LQ"][a], nth("LQ", i))
                nc.scalar.activation(gq[a][:, 0, :], b[:, 0:TC], ACT.Gelu).then_inc(sem["gelu_q"][a], 1)
                nc.scalar.activation(gq[a][0:64, 1, :], b[0:64, TC:2 * TC], ACT.Gelu).then_inc(sem["gelu_q"][a], 1)

            def gelu_kv(i, a, k):
                b = ring_bank(("KVT", a, 0))
                act.wait_ge(sem["KVT"][a], nth("KVT", i))
                nc.scalar.activation(gkv[a][:, 0:128], b[:, 0:128], ACT.Gelu, scale=DH ** -0.5
                                     ).then_inc(sem["gelu_kv"][a], 1)
                nc.scalar.activation(gkv[a][0:64, 128:192], b[0:64, 128:192], ACT.Gelu, scale=DH ** -0.5
                                     ).then_inc(sem["gelu_kv"][a], 1)

            def x3_out(i, a, k):
                act.wait_ge(sem["XT3"][a], nth("XT3", i))
                if later(i):
                    act.wait_ge(pair_sem["U"], nth("U", i - 1, UNITS - 1))
                nc.scalar.activation(xp[:, :, a * TC:(a + 1) * TC], turned(("XT3", a, 0)), ACT.Copy
                                     ).then_inc(sem["x3_turned"][a], 1)

            def router_exp(i, a, k):
                act.wait_ge(pair_sem["router"], nth("router", i, 0))
                nc.scalar.activation(ez[:, :, :], z[:, :, :], ACT.Exp, scale=-1.0).then_inc(pair_sem["router_exp"], 1)

            def gate(j, m, k):
                n = UNIT_ROWS[m]
                if m < ROUTED:
                    act.wait_ge(pair_sem["CB"], nth("CB", j, m))
                    if m >= 2:
                        act.wait_ge(pair_sem["gated"], nth("gated", j, m - 2))
                    nc.scalar.activation(cs[m % 2][:, :], bank_c[:, 0:PT], ACT.Copy, scale=0.5
                                         ).then_inc(pair_sem["gate_copied"], 1)
                act.wait_ge(pair_sem["G"], nth("G", j, m))
                if m >= 2:
                    act.wait_ge(pair_sem["hidden"], nth("hidden", j, m - 2))
                nc.scalar.activation(th[m % 2][0:n, :], bank_g[0:n, 0:PT], ACT.Tanh, scale=0.5,
                                     bias=half_gbias[0:n, m:m + 1]).then_inc(pair_sem["tanh"], 1)

            walk(act, dict(MEAN=moments, N1=high_of_x, XT=x_out, Q=high_of_q, K=high_of_k, S2=exponents,
                          PV=heads_out, LN2A=lambda i, a, k: highs_of_norm(i, a, "ln2"), XT2=x2_out,
                          KV=kv_out, LQ=gelu_q, KVT=gelu_kv, LN3A=lambda i, a, k: highs_of_norm(i, a, "ln3"),
                          XT3=x3_out, ROUTE=router_exp, G=gate))

        @block.vector
        def _(dve):
            chain = [0]

            def link(ins):
                chain[0] += 1
                ins.then_inc(init_chain, 1)
                dve.wait_ge(init_chain, chain[0])

            for n, (lo, hi) in enumerate(((0, SPLIT_A), (SPLIT_A, SPLIT))):
                full = staged[n]
                dve.wait_ge(stage_in[n], 16)
                link(nc.vector.tensor_copy(w_high[:, lo:hi], full))
                link(nc.vector.tensor_tensor(w_low[:, lo:hi], full, w_high[:, lo:hi], ALU.subtract))
            dve.wait_ge(consts_in, CONSTS)
            dve.wait_ge(pool_init, 5)
            link(nc.vector.tensor_copy(gbd_high[:, :], gbd_sb[:, :]))
            link(nc.vector.tensor_tensor(gbd_low[:, :], gbd_sb[:, :], gbd_high[:, :], ALU.subtract))
            link(nc.vector.tensor_scalar(half_gbias[:, :], gbias[:, :], 0.5, None, ALU.mult))
            nc.vector.tensor_tensor(table[:, :, :], table[:, :, :], tok_add_sb[:, :, :], ALU.add
                                    ).then_inc(init_done, 1)
            dve.wait_ge(init_done, 1)

            def tokens(i, a, k):
                dve.wait_ge(sem["EM"][a], nth("EM", i))
                nc.vector.tensor_tensor(tok[a][:, :, :], ring_bank(("EM", a, 0))[0:TR, 0:2 * C].rearrange(
                    "p (t c) -> p t c", t=2), table[:, :, :], ALU.add).then_inc(sem["tokens"][a], 1)
                dve.wait_ge(sem["tokens"][a], nth("tokens", i))
                nc.vector.tensor_reduce(rsum[a][:, :], tok[a][:, :, :], AX.X, ALU.add
                                        ).then_inc(sem["row_sums"][a], 1)

            def centre(i, a, k):
                dve.wait_ge(sem["VAR"][a], nth("VAR", i))
                nc.vector.tensor_copy(var[a][:, :], ring_bank(("VAR", a, 0))[0:TR, 0:1]).then_inc(sem["variance"][a], 1)
                dve.wait_ge(sem["neg_mean"][a], nth("neg_mean", i))
                nc.vector.scalar_tensor_tensor(out=xa[a][:, :, :], in0=tok[a][:, :, :], scalar=nmean[a][:, 0:1],
                                               in1=lnw_sb[:, :, :], op0=ALU.add, op1=ALU.mult
                                               ).then_inc(sem["centred"][a], 1)

            def normalise(i, a, k):
                dve.wait_ge(sem["centred"][a], nth("centred", i))
                dve.wait_ge(sem["rstd"][a], nth("rstd", i, RSQRT_STEPS - 1))
                nc.vector.scalar_tensor_tensor(out=xb[a][:, :, :], in0=xa[a][:, :, :], scalar=rstd[a][:, 0:1],
                                               in1=lnb_sb[:, :, :], op0=ALU.mult, op1=ALU.add
                                               ).then_inc(sem["normed"][a], 1)

            def biased(full, bias, stage, name):
                def part(i, a, k):
                    dve.wait_ge(sem[stage][a], nth(stage, i, k))
                    nc.vector.tensor_tensor(full[a][0:96, 2 * k:2 * k + 2, :],
                                            ring_bank((stage, a, k))[0:96, 0:2 * TC].rearrange("p (j n) -> p j n", j=2),
                                            bias[:, 2 * k:2 * k + 2].unsqueeze(2).to_broadcast([96, 2, TC]), ALU.add
                                            ).then_inc(sem[name][a], 1)
                return part

            def keys(i, a, k):
                dve.wait_ge(sem["q_low"][a], nth("q_low", i, k))
                dve.wait_ge(sem["q_high"][a], nth("q_high", i, k))
                biased(kf, bk_sb, "K", "k_full")(i, a, k)
                if k >= 1:
                    mask_keys(i, a, k - 1)

            def mask_keys(i, a, k):
                dve.wait_ge(sem["k_low"][a], nth("k_low", i, k))
                dve.wait_ge(sem["k_high"][a], nth("k_high", i, k))
                for odd in range(2):
                    nc.vector.tensor_scalar(ks[a][0:96, 4 * k + odd:4 * k + 4:2, :], kh[a][:, 2 * k:2 * k + 2, :],
                                            head_mask[0:96, odd:odd + 1], None, ALU.mult
                                            ).then_inc(sem["k_masked"][a], 1)

            def values(i, a, k):
                mask_keys(i, a, 2)
                dve.wait_ge(sem["V"][a], nth("V", i))
                nc.vector.tensor_tensor(vp[a][:, :, :, 0:16],
                                        ring_bank(("V", a, 0))[0:TR, 0:2 * C].rearrange("p (t h d) -> p t h d", t=2, d=DH),
                                        bv_sb[:, :].rearrange("p (h d) -> p h d", d=DH).unsqueeze(1)
                                        .to_broadcast([TR, 2, HEADS, DH]), ALU.add).then_inc(sem["v_made"][a], 1)

            def row_max(i, a, k):
                t, hp = divmod(k, 6)
                dve.wait_ge(sem["S1"][a], nth("S1", i, k))
                nc.vector.tensor_reduce(mx[a][:, t, 2 * hp:2 * hp + 2],
                                        ring_bank(("S1", a, k))[0:TR, 0:2 * TC].rearrange("p (x n) -> p x n", x=2)[:, :, 0:SEQ],
                                        AX.X, ALU.max).then_inc(sem["row_max"][a], 1)

            def max_out(i, a, k):
                dve.wait_ge(sem["MT"][a], nth("MT", i))
                nc.vector.tensor_copy(qs[a][96:96 + HEADS, :, :],
                                      ring_bank(("MT", a, 0))[0:HEADS, 0:TR].bitcast(F16).unsqueeze(1)
                                      .to_broadcast([HEADS, 6, TC])).then_inc(sem["max_turned"][a], 1)

            def divide(i, a, t):
                b = ring_bank(("OT", a, t))[0:TR, 0:384].rearrange("p (h d) -> p h d", d=32)
                dve.wait_ge(sem["OT"][a], nth("OT", i, t))
                nc.vector.reciprocal(rec[a][:, t, :], b[:, :, 16]).then_inc(sem["recip"][a], 1)
                dve.wait_ge(sem["recip"][a], nth("recip", i, t))
                nc.vector.tensor_tensor(ms[a][:, t, :].rearrange("p (h d) -> p h d", d=DH), b[:, :, 0:16],
                                        rec[a][:, t, :].unsqueeze(2).to_broadcast([TR, HEADS, DH]), ALU.mult
                                        ).then_inc(sem["heads"][a], 1)

            def statistics(i, a, src, name):
                for t in range(2):
                    nc.vector.bn_stats(bns[a][:, t, :], src[a][:, t, :]).then_inc(sem[name][a], 1)
                dve.drain()
                for t in range(2):
                    nc.vector.bn_aggr(bna[a][:, t, :], bns[a][:, t, :]).then_inc(sem[name][a], 1)

            def standardise(i, a, src, name):
                dve.wait_ge(sem[name + "_rstd"][a], nth(name + "_rstd", i, RSQRT_STEPS - 1))
                for t in range(2):
                    nc.vector.tensor_scalar(xn[a][:, t, :], src[a][:, t, :], bna[a][:, t, 0:1], rs2[a][:, t:t + 1],
                                            ALU.subtract, ALU.mult).then_inc(sem[name][a], 1)

            def statistics2(i, a, k):
                dve.wait_ge(sem["h1"][a], nth("h1", i, 1))
                statistics(i, a, h1, "ln2")

            def standardise2(i, a, k):
                standardise(i, a, h1, "ln2")

            def proj_out(i, a, k):
                b = ring_bank(("GW", a, 0))
                dve.wait_ge(sem["GW"][a], nth("GW", i))
                nc.vector.tensor_copy(gw[a][:, 0, :], b[:, 0:C]).then_inc(sem["kv_proj"][a], 1)
                nc.vector.tensor_copy(gw[a][0:64, 1, :], b[0:64, C:2 * C]).then_inc(sem["kv_proj"][a], 1)

            def y_out(i, a, k):
                dve.wait_ge(sem["Y"][a], nth("Y", i))
                dve.wait_ge(sem["h1_biased"][a], nth("h1_biased", i))
                nc.vector.tensor_tensor(h2[a][:, :, :], ring_bank(("Y", a, 0))[0:TR, 0:2 * C].rearrange(
                    "p (t c) -> p t c", t=2), h1b[a][:, :, :], ALU.add).then_inc(sem["h2"][a], 1)

            def statistics3(i, a, k):
                dve.wait_ge(sem["h2"][a], nth("h2", i))
                statistics(i, a, h2, "ln3")

            def standardise3(i, a, k):
                standardise(i, a, h2, "ln3")

            def all4(ap):
                return ap.unsqueeze(1).to_broadcast([TR, 4, EXPERTS])

            def router_logits(i, a, k):
                dve.wait_ge(pair_sem["RT"], nth("RT", i))
                nc.vector.tensor_tensor(z[:, :, :], ring_bank(("RT", None, 0))[0:TR, 0:4 * EXPERTS].rearrange(
                    "p (q e) -> p q e", q=4), all4(rb_sb[:, :]), ALU.add).then_inc(pair_sem["router"], 1)

            def route(i, a, k):
                done = [1]

                def step(ins):
                    ins.then_inc(pair_sem["router"], 1)
                    dve.drain()
                    done[0] += 1

                dve.wait_ge(pair_sem["router_exp"], nth("router_exp", i))
                step(nc.vector.tensor_scalar(s1[:, :, :], ez[:, :, :], 1.0, None, ALU.add))
                step(nc.vector.reciprocal(score[:, :, :], s1[:, :, :]))
                step(nc.vector.tensor_tensor(sf[:, :, :], score[:, :, :], all4(corr_sb[:, :]), ALU.add))
                g4 = sf[:, :, :].rearrange("p q (g e) -> p (q g) e", e=4)
                step(nc.vector.tensor_tensor(psum2[:, :, 0:3], g4[:, :, 0:3], g4[:, :, 1:4], ALU.add))
                step(nc.vector.tensor_tensor(psum2[:, :, 3:5], g4[:, :, 0:2], g4[:, :, 2:4], ALU.add))
                step(nc.vector.tensor_tensor(psum2[:, :, 5:6], g4[:, :, 0:1], g4[:, :, 3:4], ALU.add))
                step(nc.vector.tensor_reduce(gs[:, :], psum2[:, :, :], AX.X, ALU.max))
                other = gs[:, :].rearrange("p (q g) -> p q g", g=4).unsqueeze(2).to_broadcast([TR, 4, 4, 4])
                own = gs[:, :].rearrange("p (q g) -> p q g", g=4).unsqueeze(3).to_broadcast([TR, 4, 4, 4])
                step(nc.vector.tensor_tensor(gt[:, :, :, :], other, own, ALU.is_gt))
                step(nc.vector.tensor_tensor(eq[:, :, :, :], other, own, ALU.is_equal))
                step(nc.vector.tensor_tensor(eql[:, :, :, :].rearrange("p q g h -> p q (g h)"),
                                             eq[:, :, :, :].rearrange("p q g h -> p q (g h)"),
                                             all4(before[0:TR, :]), ALU.mult))
                step(nc.vector.tensor_tensor(beats[:, :, :, :], gt[:, :, :, :], eql[:, :, :, :], ALU.add))
                step(nc.vector.tensor_reduce(rank[:, :], beats[:, :, :, :].rearrange("p q g h -> p (q g) h"),
                                             AX.X, ALU.add))
                step(nc.vector.tensor_scalar(keep[:, :], rank[:, :], 1.5, None, ALU.is_lt))
                step(nc.vector.tensor_tensor(sm[:, :, 0:16].rearrange("p q (g e) -> p q g e", e=4),
                                             sf[:, :, :].rearrange("p q (g e) -> p q g e", e=4),
                                             keep[:, :].rearrange("p (q g) -> p q g", g=4).unsqueeze(3)
                                             .to_broadcast([TR, 4, 4, 4]), ALU.mult))
                for q in range(4):
                    step(nc.vector.max(top8[:, q, :], sm[:, q, :]))
                step(nc.vector.memset(top8[:, :, 4:8], SENTINEL))
                for q in range(4):
                    step(nc.vector.match_replace(mr[:, q, :], top8[:, q, :], sm[:, q, :], TAKEN))
                step(nc.vector.scalar_tensor_tensor(out=wsel[:, :, :], in0=mr[:, :, 0:16], scalar=-2.0e38,
                                                    in1=score[:, :, :], op0=ALU.is_lt, op1=ALU.mult))
                step(nc.vector.tensor_reduce(den[:, :], wsel[:, :, :], AX.X, ALU.add))
                step(nc.vector.tensor_scalar(den1[:, :], den[:, :], 1e-20, None, ALU.add))
                step(nc.vector.reciprocal(rden[:, :], den1[:, :]))
                step(nc.vector.tensor_tensor(gates[:, :, :], wsel[:, :, :],
                                             rden[:, :].unsqueeze(2).to_broadcast([TR, 4, EXPERTS]), ALU.mult))
                step(nc.vector.tensor_scalar(gates_hl[:, :, 0:16], gates[:, :, :], 2.5, None, ALU.mult))
                step(nc.vector.scalar_tensor_tensor(out=gates_hl[:, :, 16:32], in0=gates[:, :, :], scalar=2.5,
                                                    in1=gates_hl[:, :, 0:16], op0=ALU.mult, op1=ALU.subtract))
                assert done[0] == ROUTER_STEPS, done

            def gates_out(i, a, k):
                dve.wait_ge(pair_sem["CT"], nth("CT", i))
                if later(i):
                    dve.wait_ge(pair_sem["DN"], nth("DN", i - 1, 3))
                nc.vector.tensor_copy(ct[:, :], ring_bank(("CT", None, 0))[0:32, 0:TC].bitcast(F16)
                                      ).then_inc(pair_sem["gates_turned"], 1)

            def gated(j, m, k):
                n = UNIT_ROWS[m]
                dve.wait_ge(pair_sem["tanh"], nth("tanh", j, m))
                if m < ROUTED:
                    dve.wait_ge(pair_sem["gate_copied"], nth("gate_copied", j, m))
                    nc.vector.scalar_tensor_tensor(out=ga[m % 2][0:n, :], in0=bank_g[0:n, 0:PT],
                                                   scalar=gbias[0:n, m:m + 1], in1=cs[m % 2][0:n, :],
                                                   op0=ALU.add, op1=ALU.mult).then_inc(pair_sem["gated"], 1)
                else:
                    nc.vector.tensor_scalar(ga[m % 2][0:n, :], bank_g[0:n, 0:PT], gbias[0:n, m:m + 1], 0.5,
                                            ALU.add, ALU.mult).then_inc(pair_sem["gated"], 1)

            def hidden_before(j, m, k):
                if m >= 1:
                    hidden(j, m - 1)

            def hidden(j, m):
                n = UNIT_ROWS[m]
                dve.wait_ge(pair_sem["U"], nth("U", j, m))
                dve.wait_ge(pair_sem["gated"], nth("gated", j, m))
                nc.vector.scalar_tensor_tensor(out=ub[m % 2][0:n, :], in0=bank_u[0:n, 0:PT],
                                               scalar=ubias[0:n, m:m + 1], in1=ga[m % 2][0:n, :],
                                               op0=ALU.add, op1=ALU.mult).then_inc(pair_sem["upped"], 1)
                dve.wait_ge(pair_sem["upped"], nth("upped", j, m))
                if later(j):
                    dve.wait_ge(pair_sem["DN"], nth("DN", j - 1, 3))
                nc.vector.scalar_tensor_tensor(out=hid[0:n, m, :], in0=th[m % 2][0:n, :], scalar=1.0,
                                               in1=ub[m % 2][0:n, :], op0=ALU.add, op1=ALU.mult
                                               ).then_inc(pair_sem["hidden"], 1)

            def result(j, q, half):
                a, t = divmod(q, 2)
                if q == 0 and half == 0:
                    hidden(j, UNITS - 1)
                if t == 0 or half == 0:
                    return
                dve.wait_ge(pair_sem["DN"], nth("DN", j, q))
                if a == 0 and later(j):
                    dve.wait_ge(pair_sem["stored"], 16 * j)
                dve.wait_ge(sem["h2_biased"][a], nth("h2_biased", j))
                nc.vector.tensor_tensor(res[:, a, :, :], bank_d[0:TR, 0:2 * C].rearrange("p (t c) -> p t c", t=2),
                                        hs[:, a, :, :], ALU.add).then_inc(pair_sem["result"], 1)

            walk(dve, dict(EM_END=tokens, VAR=centre, N1=normalise, Q=biased(qf, bq_sb, "Q", "q_full"), K=keys, V=values,
                          S1=row_max, MT=max_out, OT=divide, LN2S=statistics2, LN2A=standardise2,
                          GW=proj_out, Y=y_out, LN3S=statistics3, LN3A=standardise3, RT=router_logits,
                          ROUTE=route, CT=gates_out, G=hidden_before, U=gated, DN=result, DN_LAST=result))

        @block.tensor
        def _(pe):
            mm = nc.tensor.matmul
            pe.wait_ge(init_done, 1)
            pe.wait_ge(consts_in, CONSTS)

            def dense(dst, stationary, moving, columns=None):
                for n, (blk, w, row) in enumerate(((0, w_high, 0), (1, w_high, 0), (0, w_low, 0),
                                                   (2, w_high, 1), (2, w_low, 1))):
                    last = mm(dst, stationary(blk, w, row), moving(blk, w, row), start=n == 0, stop=n == 4)
                return last

            def embed(i, a, t):
                step = ("EM", a, 0)
                if t == 0:
                    pe.wait_ge(pair_sem["loaded"], 16 * (i + 1))
                    if ring_used(step, i):
                        pe.wait_ge(ring_reader(step, i), ring_count(step, i))
                for c in range(CIN):
                    last = mm(ring_bank(step)[0:TR, t * C:(t + 1) * C], xin[:, c, a, t * TR:(t + 1) * TR],
                              wp_sb[:, c, :], start=c == 0, stop=c == CIN - 1)
                if t == 1:
                    last.then_inc(sem["EM"][a], 1)

            def moment(stage, source, made, k_made):
                def part(i, a, k):
                    step = (stage, a, 0)
                    pe.wait_ge(sem[made][a], nth(made, i, k_made))
                    if ring_used(step, i):
                        pe.wait_ge(ring_reader(step, i), ring_count(step, i))
                    for t in range(2):
                        n = LIVE[t]
                        last = mm(ring_bank(step)[0:TR, 0:1], mean_w[0:n, :], source[a][0:n, t:t + 1],
                                  start=t == 0, stop=t == 1)
                    last.then_inc(sem[stage][a], 1)
                return part

            def turn(dst, src, n_blocks):
                for t in range(2):
                    for b in range(n_blocks):
                        last = nc.tensor.transpose(dst[:, b, t * TR:(t + 1) * TR], src(t, b), ident16[0:TR, 0:TR])
                return last

            def turned(step):
                return ring_bank(step)[:, 0:300].bitcast(F16).rearrange("p (b n) -> p b n", b=3)

            def turn_x(i, a, k):
                pe.wait_ge(sem["x_low"][a], nth("x_low", i))
                if ring_used(("XT", a, 0), i):
                    pe.wait_ge(ring_reader(("XT", a, 0), i), ring_count(("XT", a, 0), i))
                turn(turned(("XT", a, 0)),
                     lambda t, b: x3[a][:, t, 2 * b:2 * b + 2, :].rearrange("p j c -> p (j c)"), 3
                     ).then_inc(sem["XT"][a], 1)

            def project(stage, col):
                def part(i, a, k):
                    step = (stage, a, k)
                    pe.wait_ge(sem["x_turned"][a], nth("x_turned", i))
                    if ring_used(step, i):
                        pe.wait_ge(ring_reader(step, i), ring_count(step, i))
                    for y in range(2):
                        j = 2 * k + y
                        for n, w in enumerate((w_high, w_low)):
                            last = mm(ring_bank(step)[0:96, y * TC:(y + 1) * TC],
                                      w[:, col + 96 * j:col + 96 * j + 96], xt[a][:, j // 2, :],
                                      start=n == 0, stop=n == 1)
                    last.then_inc(sem[stage][a], 1)
                return part

            def project_v(i, a, k):
                step = ("V", a, 0)
                pe.wait_ge(sem["x_turned"][a], nth("x_turned", i))
                if ring_used(step, i):
                    pe.wait_ge(ring_reader(step, i), ring_count(step, i))
                for t in range(2):
                    for b in range(3):
                        for n, w in enumerate((w_high, w_low)):
                            last = mm(ring_bank(step)[0:TR, t * C + 64 * b:t * C + 64 * b + 64],
                                      xt[a][:, b, t * TR:(t + 1) * TR], w[:, VW + 64 * b:VW + 64 * b + 64],
                                      start=n == 0, stop=n == 1)
                last.then_inc(sem["V"][a], 1)

            def scores(i, a, k):
                step = ("S1", a, k)
                t, hp = divmod(k, 6)
                pe.wait_ge(sem["q_low"][a], nth("q_low", i, hp // 2))
                pe.wait_ge(sem["q_high"][a], nth("q_high", i, hp // 2))
                pe.wait_ge(sem["k_masked"][a], nth("k_masked", i, 2 * (hp // 2) + 1))
                if ring_used(step, i):
                    pe.wait_ge(ring_reader(step, i), ring_count(step, i))
                for odd in range(2):
                    last = mm(ring_bank(step)[0:TR, odd * TC:odd * TC + SEQ], qs[a][0:96, hp, t * TR:(t + 1) * TR],
                              ks[a][0:96, 2 * hp + odd, 0:SEQ], start=True, stop=True)
                last.then_inc(sem["S1"][a], 1)

            def turn_max(i, a, k):
                step = ("MT", a, 0)
                pe.wait_ge(sem["row_max"][a], nth("row_max", i, 11))
                if ring_used(step, i):
                    pe.wait_ge(ring_reader(step, i), ring_count(step, i))
                for t in range(2):
                    last = nc.tensor.transpose(ring_bank(step)[0:HEADS, 0:TR].bitcast(F16)[:, t * TR:(t + 1) * TR],
                                               mx[a][:, t, :], ident16[0:TR, 0:TR])
                last.then_inc(sem["MT"][a], 1)

            def scores_less_max(i, a, h):
                step = ("S2", a, h)
                pe.wait_ge(sem["max_turned"][a], nth("max_turned", i))
                if ring_used(step, i):
                    pe.wait_ge(ring_reader(step, i), ring_count(step, i))
                for t in range(2):
                    last = mm(ring_bank(step)[0:TR, t * TC:(t + 1) * TC], ks[a][:, h, t * TR:(t + 1) * TR],
                              qs[a][:, h // 2, :], start=True, stop=True)
                last.then_inc(sem["S2"][a], 1)

            def attend(i, a, g):
                step = ("PV", a, g)
                pe.wait_ge(sem["v_made"][a], nth("v_made", i))
                if last_tenant(step, i)[0][0:2] != ("S2", a):
                    pe.wait_ge(ring_reader(step, i), ring_count(step, i))
                pe.wait_ge(sem["probs"][a], nth("probs", i, 4 * g + 3))
                for t in range(2):
                    n = LIVE[t]
                    for y in range(4):
                        h = 4 * g + y
                        last = mm(ring_bank(step)[32 * y:32 * y + 32, 0:TC], vp[a][0:n, t, h, :],
                                  probs[0:n, h, t, :], start=t == 0, stop=t == 1,
                                  tile_position=(0, 32 * y))
                last.then_inc(sem["PV"][a], 1)

            def turn_heads(i, a, t):
                step = ("OT", a, t)
                pe.wait_ge(sem["heads_out"][a], nth("heads_out", i, 2))
                if ring_used(step, i):
                    pe.wait_ge(ring_reader(step, i), ring_count(step, i))
                for g in range(3):
                    last = nc.tensor.transpose(ring_bank(step)[0:TR, 128 * g:128 * g + 128],
                                               ots[a][:, g, t * TR:(t + 1) * TR], ident32)
                last.then_inc(sem["OT"][a], 1)

            def turn_norm(stage, name):
                def part(i, a, k):
                    pe.wait_ge(sem[name + "_low"][a], nth(name + "_low", i, 1))
                    if ring_used((stage, a, 0), i):
                        pe.wait_ge(ring_reader((stage, a, 0), i), ring_count((stage, a, 0), i))
                    turn(turned((stage, a, 0)), lambda t, b: xs[a][:, t, 128 * b:128 * b + 128], 3
                         ).then_inc(sem[stage][a], 1)
                return part

            def linear_kv(i, a, t):
                step = ("KV", a, t)
                pe.wait_ge(sem["x2_turned"][a], nth("x2_turned", i))
                if ring_used(step, i):
                    pe.wait_ge(ring_reader(step, i), ring_count(step, i))
                dense(ring_bank(step)[0:TR, 0:2 * C],
                      lambda blk, w, row: xt2[a][:, blk, t * TR:(t + 1) * TR],
                      lambda blk, w, row: w[:, (L0, L1)[row] + C:(L0, L1)[row] + 3 * C]
                      ).then_inc(sem["KV"][a], 1)

            def linear_q(i, a, k):
                step = ("LQ", a, 0)
                pe.wait_ge(sem["x2_turned"][a], nth("x2_turned", i))
                if ring_used(step, i):
                    pe.wait_ge(ring_reader(step, i), ring_count(step, i))
                for n, (lo, m) in enumerate(((0, 128), (128, 64))):
                    last = dense(ring_bank(step)[0:m, n * TC:(n + 1) * TC],
                                 lambda blk, w, row: w[:, (L0, L1)[row] + lo:(L0, L1)[row] + lo + m],
                                 lambda blk, w, row: xt2[a][:, blk, :])
                last.then_inc(sem["LQ"][a], 1)

            def linear_kv_product(i, a, k):
                step = ("KVT", a, 0)
                pe.wait_ge(sem["kv"][a], nth("kv", i, 1))
                if ring_used(step, i):
                    pe.wait_ge(ring_reader(step, i), ring_count(step, i))
                for lo, m in ((0, 128), (128, 64)):
                    for t in range(2):
                        n = LIVE[t]
                        last = mm(ring_bank(step)[0:m, lo:lo + m], kv[a][0:n, t, C + lo:C + lo + m],
                                  kv[a][0:n, t, lo:lo + m], start=t == 0, stop=t == 1)
                last.then_inc(sem["KVT"][a], 1)

            def fold_projection(i, a, k):
                step = ("GW", a, 0)
                pe.wait_ge(sem["gelu_kv_masked"][a], nth("gelu_kv_masked", i, 1))
                if ring_used(step, i):
                    pe.wait_ge(ring_reader(step, i), ring_count(step, i))
                mm(ring_bank(step)[0:128, 0:C], gkvm[a][:, 0:128], wproj_sb[:, 0, :], start=True, stop=True)
                mm(ring_bank(step)[0:64, C:2 * C], gkvm[a][0:64, 128:192], wproj_sb[0:64, 1, :],
                   start=True, stop=True).then_inc(sem["GW"][a], 1)

            def linear_out(i, a, k):
                step = ("Y", a, 0)
                pe.wait_ge(sem["kv_proj"][a], nth("kv_proj", i, 1))
                pe.wait_ge(sem["gelu_q"][a], nth("gelu_q", i, 1))
                if ring_used(step, i):
                    pe.wait_ge(ring_reader(step, i), ring_count(step, i))
                for t in range(2):
                    mm(ring_bank(step)[0:TR, t * C:(t + 1) * C], gq[a][:, 0, t * TR:(t + 1) * TR], gw[a][:, 0, :],
                       start=True, stop=False)
                    last = mm(ring_bank(step)[0:TR, t * C:(t + 1) * C], gq[a][0:64, 1, t * TR:(t + 1) * TR],
                              gw[a][0:64, 1, :], start=False, stop=True)
                last.then_inc(sem["Y"][a], 1)

            def router(i, a, k):
                step = ("RT", None, 0)
                pe.wait_ge(sem["x3_turned"][0], nth("x3_turned", i))
                pe.wait_ge(sem["x3_turned"][1], nth("x3_turned", i))
                if ring_used(step, i):
                    pe.wait_ge(ring_reader(step, i), ring_count(step, i))
                for q in range(4):
                    last = dense(ring_bank(step)[0:TR, EXPERTS * q:EXPERTS * (q + 1)],
                                 lambda blk, w, row: xp[:, blk, q * TR:(q + 1) * TR],
                                 lambda blk, w, row: w[:, (R0, R1)[row]:(R0, R1)[row] + EXPERTS])
                last.then_inc(pair_sem["RT"], 1)

            def turn_gates(i, a, k):
                step = ("CT", None, 0)
                pe.wait_ge(pair_sem["router"], nth("router", i, ROUTER_STEPS - 1))
                if ring_used(step, i):
                    pe.wait_ge(ring_reader(step, i), ring_count(step, i))
                for q in range(4):
                    last = nc.tensor.transpose(ring_bank(step)[0:32, 0:TC].bitcast(F16)[:, q * TR:(q + 1) * TR],
                                               gates_hl[:, q, :], ident16[0:TR, 0:TR])
                last.then_inc(pair_sem["CT"], 1)

            def ffn_up(dst, m, col):
                n = UNIT_ROWS[m]
                lo = col + 128 * m
                return dense(dst[0:n, 0:PT],
                             lambda blk, w, row: w[:, (UP0, UP1)[row] + lo:(UP0, UP1)[row] + lo + n],
                             lambda blk, w, row: xp[:, blk, :])

            def ffn_gate(j, m, k):
                if m == 0:
                    pe.wait_ge(sem["x3_turned"][0], nth("x3_turned", j))
                    pe.wait_ge(sem["x3_turned"][1], nth("x3_turned", j))
                    pe.wait_ge(pair_sem["gates_turned"], nth("gates_turned", j))
                if m < ROUTED:
                    if m >= 1:
                        pe.wait_ge(pair_sem["gate_copied"], nth("gate_copied", j, m - 1))
                    mm(bank_c[:, 0:PT], select_sb[:, m, :], ct[:, :], start=True, stop=True).then_inc(pair_sem["CB"], 1)
                if m >= 1:
                    pe.wait_ge(pair_sem["gated"], nth("gated", j, m - 1))
                ffn_up(bank_g, m, 0).then_inc(pair_sem["G"], 1)

            def ffn_value(j, m, k):
                if m >= 1:
                    pe.wait_ge(pair_sem["upped"], nth("upped", j, m - 1))
                ffn_up(bank_u, m, HID).then_inc(pair_sem["U"], 1)

            def ffn_down(j, q, half):
                a, t = divmod(q, 2)
                dst = bank_d[0:TR, t * C:(t + 1) * C]
                if half == 0:
                    pe.wait_ge(pair_sem["hidden"], nth("hidden", j, UNITS - 1))
                    if a == 1:
                        pe.wait_ge(pair_sem["result"], nth("result", j, 0))
                    elif later(j):
                        pe.wait_ge(pair_sem["result"], nth("result", j - 1, 1))
                    mm(dst, ct[:, q * TR:(q + 1) * TR], gbd_high[:, :], start=True, stop=False)
                    mm(dst, ct[:, q * TR:(q + 1) * TR], gbd_low[:, :], start=False, stop=False)
                for m in range(7 * half, 7 * half + 7):
                    n = UNIT_ROWS[m]
                    last = mm(dst, hid[0:n, m, q * TR:(q + 1) * TR], wd_sb[0:n, m, :], start=False,
                              stop=m == UNITS - 1)
                if half == 1:
                    last.then_inc(pair_sem["DN"], 1)

            walk(pe, dict(EM=lambda i, a, k: embed(i, a, 0), EM_END=lambda i, a, k: embed(i, a, 1), MEAN=moment("MEAN", rsum, "row_sums", 0), VAR=moment("VAR", sq, "squares", 1),
                          XT=turn_x, Q=project("Q", QW), K=project("K", KW), V=project_v, S1=scores, MT=turn_max,
                          S2=scores_less_max, PV=attend, OT=turn_heads, XT2=turn_norm("XT2", "ln2"),
                          KV=linear_kv, LQ=linear_q, KVT=linear_kv_product, GW=fold_projection, Y=linear_out,
                          XT3=turn_norm("XT3", "ln3"), RT=router, CT=turn_gates,
                          G=ffn_gate, U=ffn_value, DN=ffn_down, DN_LAST=ffn_down))


def layout(np, pairs, x, L0_tok_W_map, L0_tok_b_map, L0_tok_class_token, L0_tok_ln_w, L0_tok_ln_b, L0_tok_Wq, L0_tok_bq,
           L0_tok_Wk, L0_tok_bk, L0_tok_Wv, L0_tok_bv, L0_attn_w_qkv, L0_attn_w_proj, L0_attn_b_proj,
           L0_ffn_router_w, L0_ffn_router_b, L0_ffn_corr_bias, L0_ffn_gWg, L0_ffn_gbg, L0_ffn_gWu, L0_ffn_gbu,
           L0_ffn_gWd, L0_ffn_gbd, L0_ffn_sWg, L0_ffn_sbg, L0_ffn_sWu, L0_ffn_sbu, L0_ffn_sWd, L0_ffn_sbd):
    f = np.float32
    A = {}
    xt = np.zeros((pairs, 128, CIN, 2, TC), f)
    xt[..., 0:PATCHES] = x.reshape(pairs, 2, PATCHES, CIN, 128).transpose(0, 4, 3, 1, 2)
    A["x"] = xt
    A["w_patch"] = L0_tok_W_map.T.reshape(CIN, 128, C).transpose(1, 0, 2)

    def tokens(rows_of_patches, row_of_class):
        t = np.zeros((TC, C), f)
        t[0:PATCHES] = rows_of_patches
        t[PATCHES] = row_of_class
        return t.reshape(2, TR, C).transpose(1, 0, 2)

    s = np.arange(SEQ, dtype=f)[:, None]
    d = np.arange(C, dtype=f)[None, :]
    even = (np.arange(C) % 2 == 0)[None, :]
    pos = np.where(even, np.sin(s / np.power(f(10000.0), d / f(C))),
                   np.cos(s / np.power(f(10000.0), (d - f(1.0)) / f(C)))).astype(f)
    A["pos"] = tokens(pos[1:], pos[0])
    A["tok_add"] = tokens(L0_tok_b_map, L0_tok_class_token[0])
    A["ln_w"] = tokens(L0_tok_ln_w[1:], L0_tok_ln_w[0])
    A["ln_b"] = tokens(L0_tok_ln_b[1:], L0_tok_ln_b[0])

    W = np.zeros((128, SPLIT), f)

    def twice(w):
        return np.concatenate([w[128:C], w[128:C]], 0)

    def hidden_columns(of_experts, shared):
        return np.concatenate([of_experts.transpose(1, 0, 2).reshape(C, EXPERTS * INNER), shared], 1)

    up = np.concatenate([hidden_columns(L0_ffn_gWg, L0_ffn_sWg), hidden_columns(L0_ffn_gWu, L0_ffn_sWu)], 1)
    W[:, UP0:UP0 + 2 * HID] = up[0:128]
    W[:, UP1:UP1 + 2 * HID] = twice(up)
    for col, w in ((QW, L0_tok_Wq), (KW, L0_tok_Wk)):
        for j in range(6):
            r = 64 * (j % 2)
            for y in range(2):
                for copy in range(3):
                    c0 = col + 96 * j + 32 * copy + 16 * y
                    for half in range(2):
                        r0 = r + 32 * half + 16 * y
                        W[r0:r0 + 16, c0:c0 + 16] = w[2 * j + y].T
    for b in range(3):
        for y in range(4):
            for half in range(2):
                r0 = 64 * (y // 2) + 32 * half + 16 * (y % 2)
                c0 = VW + 64 * b + 16 * y
                W[r0:r0 + 16, c0:c0 + 16] = L0_tok_Wv[4 * b + y].T
    W[:, L0:L0 + 3 * C] = L0_attn_w_qkv[0:128]
    W[:, L1:L1 + 3 * C] = twice(L0_attn_w_qkv)
    W[:, R0:R0 + EXPERTS] = L0_ffn_router_w.T[0:128]
    W[:, R1:R1 + EXPERTS] = twice(L0_ffn_router_w.T)
    A["w_split"] = W
    for name, b in (("bq", L0_tok_bq), ("bk", L0_tok_bk)):
        A[name] = np.concatenate([b.reshape(6, 32).T] * 3, 0)

    def rows(v, n=TR):
        return np.broadcast_to(v.reshape(1, -1), (n, v.size))

    A["bv"] = rows(L0_tok_bv)
    wproj = np.zeros((128, 2, C), f)
    wproj[:, 0] = L0_attn_w_proj[0:128]
    wproj[0:64, 1] = L0_attn_w_proj[128:C]
    A["w_proj"] = wproj
    A["b_proj"] = rows(L0_attn_b_proj)
    A["router_b"] = rows(L0_ffn_router_b)
    A["corr_b"] = rows(L0_ffn_corr_bias)
    wd = np.zeros((UNITS * 128, C), f)
    wd[0:HID] = np.concatenate([L0_ffn_gWd.reshape(EXPERTS * INNER, C), L0_ffn_sWd], 0)
    A["w_down"] = wd.reshape(UNITS, 128, C).transpose(1, 0, 2)
    A["down_b"] = np.concatenate([L0_ffn_gbd, L0_ffn_gbd], 0)
    A["shared_b"] = rows(L0_ffn_sbd)
    for name, of_experts, shared in (("gate_bias", L0_ffn_gbg, L0_ffn_sbg), ("up_bias", L0_ffn_gbu, L0_ffn_sbu)):
        b = np.zeros((UNITS * 128,), f)
        b[0:HID] = np.concatenate([of_experts.reshape(-1), shared], 0)
        A[name] = b.reshape(UNITS, 128).T
    expert = np.arange(ROUTED * 128) // INNER
    sel = (np.arange(EXPERTS)[:, None] == expert[None, :]).astype(np.float16)
    A["select"] = np.concatenate([sel, sel], 0).reshape(32, ROUTED, 128)
    c32 = np.zeros((128, 438), f)
    c32[:, 0:128] = np.eye(128, dtype=f)
    p = np.arange(128)
    c32[:, 128:256] = p[:, None] // DH == p[None, :] // DH
    c32[:, 256:320] = p[:, None] // DH == p[None, 0:64] // DH
    for odd in range(2):
        c32[:, 320 + odd] = (p // DH) % 2 == odd
    c32[:, 322:422] = 1.0 / (SEQ * C)
    g = np.arange(GROUPS)
    c32[:, 422:438] = (g[None, :] < g[:, None]).astype(f).reshape(1, 16)
    A["consts32"] = c32
    c16 = np.zeros((128, 128 + HEADS * TC), np.float16)
    c16[:, 0:128] = np.eye(128, dtype=np.float16)
    for h in range(HEADS):
        c16[96 + h, 128 + TC * h:128 + TC * (h + 1)] = -1.0
    A["consts16"] = c16
    return A


NAMES = ["x", "w_patch", "pos", "tok_add", "ln_w", "ln_b", "w_split", "bq", "bk", "bv", "w_proj", "b_proj",
         "router_b", "corr_b", "w_down", "down_b", "shared_b", "gate_bias", "up_bias", "select",
         "consts32", "consts16"]


def kernel(**inputs):
    import numpy as np
    import concourse.bacc as bacc
    from concourse.bass_utils import run_bass_kernel_spmd

    pairs = inputs["x"].shape[0] // 2
    arrays = {k: np.ascontiguousarray(v) for k, v in
              layout(np, pairs, **{k: np.asarray(v) for k, v in inputs.items()}).items()}
    nc = bacc.Bacc("TRN2", target_bir_lowering=False, num_devices=1)
    args = [nc.dram_tensor(f"in_{n}", arrays[n].shape, mybir.dt.from_np(arrays[n].dtype), kind="ExternalInput").ap()
            for n in NAMES]
    args.append(nc.dram_tensor("out_0", (pairs, TR, 2, 2, C), F32, kind="ExternalOutput").ap())
    vit_tower(nc, *args)
    r = run_bass_kernel_spmd(nc, [{f"in_{n}": arrays[n] for n in NAMES}], core_ids=[0])
    got = np.asarray(r.results[0]["out_0"]).transpose(0, 2, 3, 1, 4).reshape(2 * pairs, TC, C)
    return np.concatenate([got[:, PATCHES:SEQ], got[:, 0:PATCHES]], 1)
```

```python
from contextlib import ExitStack

import concourse.bass as bass
from concourse import mybir

F32 = mybir.dt.float32
F16 = mybir.dt.float16
I32 = mybir.dt.int32
ALU = mybir.AluOpType
ACT = mybir.ActivationFunctionType
AX = mybir.AxisListType

IMAGES, PATCHES, PATCH_IN = 128, 196, 768
C, HEADS, DH = 192, 12, 16
SEQ = PATCHES + 1
TR = 100
TC = 2 * TR
PT = 2 * TC
LIVE = (TR, SEQ - TR)
EXPERTS, INNER, GROUPS = 16, 96, 4
UNITS = 14
ROUTED = EXPERTS * INNER // 128
UNIT_ROWS = [128] * 13 + [64]
HID = EXPERTS * INNER + 2 * INNER
CIN = PATCH_IN // 128
EPS = 1e-5
ROUTER_STEPS = 31
RSQRT_STEPS, RSQRT_ROUNDS, RSQRT_GUESS = 14, 3, float(0x5F3759DF)
SENTINEL, TAKEN = -1.0e30, -3.0e38

UP0, AT0 = 0, 2 * HID
QW, KW, VW = AT0, AT0 + 576, AT0 + 1152
SPLIT_A = AT0 + 1344
UP1 = SPLIT_A
L0 = UP1 + 2 * HID
L1 = L0 + 3 * C
R0 = L1 + 3 * C
R1 = R0 + EXPERTS
SPLIT = R1 + EXPERTS

PE_STAGES = dict(EM=1, MEAN=1, VAR=1, XT=1, Q=3, K=3, V=1, S1=12, MT=1, S2=12, PV=3, OT=2,
                 XT2=1, KV=2, LQ=1, KVT=1, GW=1, Y=1, XT3=1)
MADE = dict(variance=1, ln2_rstd=RSQRT_STEPS, ln3_rstd=RSQRT_STEPS, tokens=1, row_sums=1, neg_mean=1, squares=2, rstd=RSQRT_STEPS, centred=1, normed=1, x_high=1,
            x_low=1, x_turned=1, q_full=3, q_high=3, q_low=3, k_full=3, k_high=3, k_low=3,
            k_masked=6, v_made=1, row_max=12, max_turned=1, probs=12, heads_out=3, recip=2,
            heads=2, h1=2, h1_biased=1, ln2=6, ln2_high=1, ln2_low=2, x2_turned=1, kv=2,
            gelu_q=2, gelu_kv=2, gelu_kv_masked=2, kv_proj=2, h2=1, h2_biased=1, ln3=6,
            ln3_high=1, ln3_low=2, x3_turned=1)
PAIR = dict(RT=1, CT=1, router=ROUTER_STEPS, router_exp=1, gates_turned=1, CB=12, G=14, U=14, DN=4,
            gate_copied=12, tanh=14, gated=14, upped=14, hidden=14, hidden_high=14, hidden_low=14, result=2, stored=1, loaded=1)
READ_BY = dict(EM="tokens", MEAN="neg_mean", VAR="variance", XT="x_turned", Q="q_full", K="k_full",
               V="v_made", S1="row_max", MT="max_turned", S2="probs", PV="heads_out", OT="heads",
               XT2="x2_turned", KV="kv", LQ="gelu_q", KVT="gelu_kv", GW="kv_proj", Y="h2",
               XT3="x3_turned", RT="router", CT="gates_turned")
LAST_READ = dict(LQ=1, KVT=1, GW=1)


ORDER = [12, 13, *range(ROUTED)]
SHARED_UNITS = UNITS - ROUTED
DOWN_PARTS = ((0, 4), (4, 8), (8, 11), (11, 14))
COVERED = dict(Q=("x_turned", 0), K=("x_turned", 0), V=("x_turned", 0), MT=("row_max", 11), S2=("max_turned", 0),
               OT=("heads_out", 2), KV=("x2_turned", 0), LQ=("x2_turned", 0), KVT=("kv", 1), Y=("kv_proj", 1),
               RT=("x3_turned", 0), CT=("router", ROUTER_STEPS - 1))


ORDER_OF_STEPS = """
    b.Y b.LN3S a.EM a.EM_END a.XT3 DN/1/2 b.LN3A DN/1/3 a.MEAN b.XT3 RT a.VAR ROUTE/0 b.EM a.N1 b.EM_END
    DN/2/0 ROUTE/1 a.XT G/0 a.Q/0 a.Q/1 a.Q/2 DN/2/1 b.MEAN DN/2/2 ROUTE/2 DN/2/3 b.VAR U/0 a.K/0
    ROUTE/3 DN/3/0 b.N1 a.K/1 G/1 a.K/2 DN/3/1 DN/3/2 DN/3/3 SPLIT/0 CT U/1 a.V a.S1/0 a.S1/1 G/2 a.S1/2
    b.XT b.Q/0 SPLIT/1 a.S1/3 U/2 a.S1/4 b.Q/1 G/3 a.S1/5 SPLIT/2 a.S1/6 U/3 a.S1/7 a.S1/8 a.S1/9 b.Q/2
    b.K/0 a.S1/10 G/4 a.S1/11 U/4 a.MT SPLIT/3 b.K/1 G/5 SPLIT/4 DN/0/0 a.S2/0 b.K/2 U/5 a.S2/1 a.S2/2
    a.S2/3 a.S2/4 G/6 b.V b.S1/0 SPLIT/5 b.S1/1 b.S1/2 U/6 a.PV/0 a.S2/5 b.S1/3 b.S1/4 a.S2/6 G/7 a.S2/7
    a.S2/8 SPLIT/6 b.S1/5 a.S2/9 U/7 b.S1/6 b.S1/7 G/8 b.S1/8 a.S2/10 a.HS a.S2/11 U/8 SPLIT/7 a.PV/1
    G/9 b.S1/9 b.S1/10 b.S1/11 U/9 b.HS a.PV/2 b.MT SPLIT/8 G/10 b.S2/0 a.OT/0 a.OT/1 SPLIT/9 b.S2/1
    U/10 a.LN2S b.S2/2 b.S2/3 b.S2/4 G/11 b.S2/5 b.PV/0 SPLIT/10 U/11 b.S2/6 b.S2/7 b.S2/8 G/12 SPLIT/11
    a.LN2A U/12 b.PV/1 b.S2/9 b.S2/10 G/13 b.S2/11 SPLIT/12 U/13 HL b.PV/2 b.OT/0 b.OT/1 SPLIT/13 a.XT2
    a.KV/0 a.KV/1 b.LN2S a.LQ a.KVT DN/0/1 DN/0/2 b.LN2A DN/0/3 a.GW a.Y b.XT2 DN/1/0 b.KV/0 b.KV/1 b.LQ
    a.LN3S b.KVT a.LN3A DN/1/1 b.GW
"""


def schedule():
    steps = []
    for token in ORDER_OF_STEPS.split():
        image, _, name = token.rpartition(".")
        stage, *numbers = name.split("/")
        numbers = [int(n) for n in numbers]
        if image:
            numbers = ["ab".index(image), *numbers]
        elif stage in ("RT", "ROUTE", "CT"):
            numbers = [None, *numbers]
        steps.append((stage, *(numbers + [0, 0])[:2]))
    return steps


def step_before(step):
    stage, a, k = step
    image = ["EM", "EM_END", "MEAN", "VAR", "N1", "XT", "Q", "K", "V", "S1", "MT", "S2", "OT", "LN2S", "LN2A",
             "XT2", "KV", "LQ", "KVT", "GW", "Y", "LN3S", "LN3A", "XT3", "HS"]
    if stage == "EM":
        return None
    if stage == "PV":
        return ("S2", a, 4 * k + 3)
    if stage in ("OT", "DN", "ROUTE") and k > 0 or stage in image and k > 0:
        return (stage, a, k - 1)
    if stage == "OT":
        return ("PV", a, 2)
    if stage in image:
        before = image[image.index(stage) - 1]
        return (before, a, PE_STAGES.get(before, 1) - 1)
    return {"RT": ("XT3", 1, 0), "ROUTE": ("RT", None, 0), "CT": ("ROUTE", None, 3), "U": ("G", a, 0),
            "G": ("U", a - 1, 0) if stage == "G" and a else ("XT3", 1, 0), "HL": ("U", UNITS - 1, 0),
            "SPLIT": ("G", a + 1, 0) if stage == "SPLIT" and a < UNITS - 1 else ("HL", 0, 0),
            "DN": ("DN", a - 1, 3) if stage == "DN" and a else ("U", 4, 0)}[stage]


def pairs_back(steps):
    at = {s: n for n, s in enumerate(steps)}
    assert len(at) == len(steps)
    back = {}

    def find(step):
        if step not in back:
            before = step_before(step)
            back[step] = 0 if before is None else find(before) + (at[step] < at[before])
        return back[step]

    for step in steps:
        find(step)
    return back


def vit_tower(nc, x, w_patch, pos, tok_add, ln_w, ln_b, w_split, bq, bk, bv, w_proj, b_proj,
              router_b, corr_b, w_down, down_b, shared_b, gate_bias, up_bias, select,
              consts32, consts16, out):
    pairs = x.shape[0]
    steps = schedule()
    back = pairs_back(steps)
    most_back = max(back.values())
    ring = [s for s in steps if s[0] in PE_STAGES or s[0] in ("RT", "CT")]
    assert len(ring) % 4 == 0
    place = {s: n for n, s in enumerate(ring)}

    ctx = ExitStack()
    with ctx:
        def sb(name, shape, dt=F32):
            return ctx.enter_context(nc.sbuf_tensor(name, shape, dt))

        def two(name, shape, dt=F32):
            return [sb(f"{name}{a}", shape, dt) for a in range(2)]

        w_high, w_low = sb("w_high", [128, SPLIT], F16), sb("w_low", [128, SPLIT], F16)
        wp_sb = sb("wp_sb", [128, CIN, C])
        wd_high, wd_low = sb("wd_high", [128, UNITS, C], F16), sb("wd_low", [128, UNITS, C], F16)
        wproj_sb = sb("wproj_sb", [128, 2, C])
        table = sb("table", [TR, 2, C])
        lnw_sb, lnb_sb = sb("lnw_sb", [TR, 2, C]), sb("lnb_sb", [TR, 2, C])
        bq_sb, bk_sb = sb("bq_sb", [96, 6]), sb("bk_sb", [96, 6])
        bv_sb, bproj_sb, sbd_sb = sb("bv_sb", [TR, C]), sb("bproj_sb", [TR, C]), sb("sbd_sb", [TR, C])
        rb_sb, corr_sb = sb("rb_sb", [TR, EXPERTS]), sb("corr_sb", [TR, EXPERTS])
        gbd_sb = sb("gbd_sb", [32, C])
        gbd_high, gbd_low = sb("gbd_high", [32, C], F16), sb("gbd_low", [32, C], F16)
        gbias, ubias, half_gbias = sb("gbias", [128, UNITS]), sb("ubias", [128, UNITS]), sb("half_gbias", [128, UNITS])
        select_sb = sb("select_sb", [32, ROUTED, 128], F16)
        c32 = sb("c32", [128, consts32.shape[1]])
        ident32, bd_mask = c32[:, 0:128], c32[:, 128:320]
        head_mask, mean_w, before = c32[:, 320:322], c32[:, 322:422], c32[:, 422:438]
        c16 = sb("c16", [128, 128], F16)
        ident16 = c16[:, :]

        xin = sb("xin", [128, CIN, 2, TC])
        tok, h1 = two("tok", [TR, 2, C]), two("h1", [TR, 2, C])
        xa, xb = two("xa", [TR, 2, C]), two("xb", [TR, 2, C])
        tok_add_sb = h1[0]
        ms, h1b = xa, xa
        rsum, nmean, sq, rstd, var = two("rsum", [TR, 2]), two("nmean", [TR, 1]), two("sq", [TR, 2]), two("rstd", [TR, 1]), two("var", [TR, 1])
        x3 = two("x3", [TR, 2, 6, 64], F16)
        xt = two("xt", [128, 3, TC], F16)
        qf = two("qf", [128, 6, TC])
        kf = qf
        qs, kh = two("qs", [128, 6, TC], F16), two("kh", [96, 6, TC], F16)
        ks = two("ks", [128, HEADS, TC], F16)
        vp = two("vp", [TR, 2, HEADS, 32])
        mx = two("mx", [TR, 2, HEADS], F16)
        probs = sb("probs", [128, HEADS, 2, TC])
        ots = [b[:, 0:3, :] for b in qf]
        rec = two("rec", [TR, 2, HEADS])
        bns, bna, rs2 = two("bns", [TR, 2, 6]), two("bna", [TR, 2, 2]), two("rs2", [TR, 2])
        xn = xb
        xs = [b[:, :, :, :].rearrange("p t j c -> p t (j c)") for b in x3]
        xt2 = xt
        eps = sb("eps", [TR, 2])
        work = two("work", [TR, 2, 2])
        kv, gkv, gw = two("kv", [TR, 2, 2 * C]), two("gkv", [128, C]), two("gw", [128, 2, C])
        h2 = [b[:, :, 0:C] for b in kv]
        gq, gkvm = [b[:, 3:5, :] for b in qf], gkv

        xp = sb("xp", [128, 3, PT], F16)
        ct = sb("ct", [32, PT], F16)
        hs = sb("hs", [TR, 2, 2, C])
        res = sb("res", [TR, 2, 2, C])
        z, ez, s1, score, sf = (sb(n, [TR, 4, EXPERTS]) for n in ("z", "ez", "s1", "score", "sf"))
        psum2 = sb("psum2", [TR, 16, 6])
        gs, rank, keep = (sb(n, [TR, 16]) for n in ("gs", "rank", "keep"))
        gt, eq, eql, beats = (sb(n, [TR, 4, 4, 4]) for n in ("gt", "eq", "eql", "beats"))
        sm, mr = sb("sm", [TR, 4, 20]), sb("mr", [TR, 4, 20])
        top8 = sb("top8", [TR, 4, 8])
        wsel, gates = sb("wsel", [TR, 4, EXPERTS]), sb("gates", [TR, 4, EXPERTS])
        den, den1, rden = (sb(n, [TR, 4]) for n in ("den", "den1", "rden"))
        gates_hl = sb("gates_hl", [TR, 4, 32], F16)
        cs, th, ga = (two(n, [128, PT]) for n in ("cs", "th", "ga"))
        ub = ga
        hid = sb("hid", [128, UNITS, 2, PT], F16)

        bank = [ctx.enter_context(nc.psum_tensor(f"ring{n}", [128, 512], F32)) for n in range(4)]
        bank_g, bank_u, bank_c, bank_d = (ctx.enter_context(nc.psum_tensor(n, [128, 512], F32))
                                          for n in ("bank_g", "bank_u", "bank_c", "bank_d"))

        sem = {n: [ctx.enter_context(nc.semaphore(f"{n}_{a}")) for a in range(2)]
              for n in (*PE_STAGES, *MADE)}
        pair_sem = {n: ctx.enter_context(nc.semaphore(n)) for n in PAIR}
        per = {**PE_STAGES, **MADE, **PAIR}
        consts_in = ctx.enter_context(nc.semaphore("consts_in"))
        stage_in = [ctx.enter_context(nc.semaphore(f"stage_in{n}")) for n in range(5)]
        init_done = ctx.enter_context(nc.semaphore("init_done"))
        pool_init = ctx.enter_context(nc.semaphore("pool_init"))
        init_chain = ctx.enter_context(nc.semaphore("init_chain"))

        def nth(name, i, k=0):
            return per[name] * i + k + 1

        def later(i):
            return not isinstance(i, int) or i > 0

        def ring_bank(step):
            return bank[place[step] % 4]

        def last_tenant(step, i):
            n, behind = place[step] - 4, 0
            while True:
                if n < 0:
                    n, behind = n + len(ring), behind + 1
                pairs_behind = behind + back[ring[n]] - back[step]
                if not isinstance(i, int) or 0 <= i - pairs_behind < pairs:
                    return ring[n], pairs_behind, True
                if i + back[step] - behind < 0:
                    return ring[n], pairs_behind, False
                n -= 4

        def ring_wait(step, i):
            (stage, a, k), behind, exists = last_tenant(step, i)
            name, part = ("probs", 4 * step[2] + 3) if step[0] == "PV" else COVERED.get(step[0], (None, 0))
            covered = (READ_BY[stage] == name and (a == step[1] or name == "x3_turned")
                       and (behind > 0 or behind == 0 and LAST_READ.get(stage, k) <= part))
            return exists and not covered

        def ring_reader(step, i):
            (stage, a, _), _, _ = last_tenant(step, i)
            return pair_sem[READ_BY[stage]] if a is None else sem[READ_BY[stage]][a]

        def ring_count(step, i):
            (stage, _, k), behind, _ = last_tenant(step, i)
            return nth(READ_BY[stage], i - behind, LAST_READ.get(stage, k))

        def walk(eng, parts, stop=pairs):
            def iteration(it):
                for step in steps:
                    pair = it - back[step]
                    if step[0] in parts and (not isinstance(it, int) or 0 <= pair < pairs):
                        parts[step[0]](pair, *step[1:])
            for it in range(most_back + 1):
                iteration(it)
            with eng.Fori(most_back + 1, stop) as it:
                iteration(it)
            for it in range(stop, pairs + most_back):
                iteration(it)

        probs_flat = probs[:, :, :, :].rearrange("p h t n -> p (h t n)")
        hid_flat = hid[:, :, :, :].rearrange("p m x n -> p (m x n)").bitcast(F32)
        qf_tiles = [b[:, :, :].rearrange("p j n -> p (j n)")[:, 0:6 * C].rearrange("p (m c) -> p m c", m=6) for b in qf]
        rest = SPLIT - SPLIT_A
        staged = [(probs_flat[:, 0:SPLIT_A], w_high[:, 0:SPLIT_A], w_low[:, 0:SPLIT_A], w_split[:, 0:SPLIT_A]),
                  (hid_flat[:, 0:rest], w_high[:, SPLIT_A:SPLIT], w_low[:, SPLIT_A:SPLIT], w_split[:, SPLIT_A:SPLIT]),
                  (qf_tiles[0], wd_high[:, 0:6, :], wd_low[:, 0:6, :], w_down[:, 0:6, :]),
                  (qf_tiles[1], wd_high[:, 6:12, :], wd_low[:, 6:12, :], w_down[:, 6:12, :]),
                  (hid_flat[:, rest:rest + 2 * C].rearrange("p (m c) -> p m c", m=2), wd_high[:, 12:14, :],
                   wd_low[:, 12:14, :], w_down[:, 12:14, :])]
        block = ctx.enter_context(nc.Block())

        @block.sync
        def _(sp):
            for n, (full, _, _, src) in enumerate(staged):
                sp.dma_start(full, src).then_inc(stage_in[n], 16)
            sp.dma_start(xin[:, :, :, :], x[0]).then_inc(pair_sem["loaded"], 16)
            for dst, src in ((wp_sb[:, :, :], w_patch), (wproj_sb[:, :, :], w_proj),
                             (table[:, :, :], pos), (tok_add_sb[:, :, :], tok_add), (lnw_sb[:, :, :], ln_w),
                             (lnb_sb[:, :, :], ln_b), (bq_sb[:, :], bq), (bk_sb[:, :], bk), (bv_sb[:, :], bv),
                             (bproj_sb[:, :], b_proj), (sbd_sb[:, :], shared_b), (rb_sb[:, :], router_b),
                             (corr_sb[:, :], corr_b), (gbd_sb[:, :], down_b), (gbias[:, :], gate_bias),
                             (ubias[:, :], up_bias), (select_sb[:, :, :], select), (c32[:, :], consts32),
                             (c16[:, :], consts16[:, 0:128]),
                             ):
                sp.dma_start(dst, src).then_inc(consts_in, 16)
            sp.wait_ge(pool_init, 4)
            for a in range(2):
                sp.dma_start(ks[a][96:128, :, :],
                             consts16[96:128, 128:128 + HEADS * TC].rearrange("p (h n) -> p h n", h=HEADS)
                             ).then_inc(consts_in, 16)

            def load_next(i, a, k):
                if a == 0 or (isinstance(i, int) and i == pairs - 1):
                    return
                sp.wait_ge(sem["EM"][0], nth("EM", i))
                sp.wait_ge(sem["EM"][1], nth("EM", i))
                if isinstance(i, int):
                    src = x[i + 1]
                else:
                    src = x[bass.ds(i + 1, 1)].rearrange("o p c a n -> p (o c) a n")
                sp.dma_start(xin[:, :, :, :], src).then_inc(pair_sem["loaded"], 16)

            def store(j, q, part):
                if (q, part) != (3, 3):
                    return
                sp.wait_ge(pair_sem["result"], nth("result", j, 1))
                if isinstance(j, int):
                    dst = out[j]
                else:
                    dst = out[bass.ds(j, 1)].rearrange("o p a t c -> p (o a) t c")
                sp.dma_start(dst, res[:, :, :, :]).then_inc(pair_sem["stored"], 16)

            walk(sp, dict(EM_END=load_next, DN=store), stop=pairs - 1)
            sp.wait_ge(pair_sem["stored"], 16 * pairs)

        CONSTS = 16 * 21

        @block.gpsimd
        def _(pool):
            for a in range(2):
                pool.memset(vp[a][:, :, :, 16:32], 1.0).then_inc(pool_init, 1)
                pool.wait_ge(pool_init, 2 * a + 1)
                pool.memset(qs[a][96:128, :, :], 0.0).then_inc(pool_init, 1)
                pool.wait_ge(pool_init, 2 * a + 2)
            pool.memset(sm[:, :, 16:20], SENTINEL).then_inc(pool_init, 1)
            pool.memset(eps[:, :], EPS).then_inc(pool_init, 1)
            pool.wait_ge(pool_init, 6)
            pool.wait_ge(consts_in, CONSTS)
            pool.wait_ge(init_done, 1)

            def rsqrt(i, a, y, variance, tmp, name):
                v, t = tmp[:, 0, :], tmp[:, 1, :]
                steps_done = [0]

                def step(ins):
                    ins.then_inc(sem[name][a], 1)
                    pool.drain()
                    steps_done[0] += 1

                step(nc.gpsimd.tensor_tensor(v, variance, eps[:, 0:variance.shape[1]], ALU.add))
                step(nc.gpsimd.tensor_scalar(y[:, :].bitcast(I32), v.bitcast(I32), -0.5, RSQRT_GUESS, ALU.mult, ALU.add))
                for _ in range(RSQRT_ROUNDS):
                    step(nc.gpsimd.tensor_tensor(t, y[:, :], y[:, :], ALU.mult))
                    step(nc.gpsimd.tensor_tensor(t, t, v, ALU.mult))
                    step(nc.gpsimd.tensor_scalar(t, t, -0.5, 1.5, ALU.mult, ALU.add))
                    step(nc.gpsimd.tensor_tensor(y[:, :], y[:, :], t, ALU.mult))
                assert steps_done[0] == RSQRT_STEPS

            def rsqrt_x(i, a, k):
                pool.drain()
                pool.wait_ge(sem["variance"][a], nth("variance", i))
                rsqrt(i, a, rstd[a], var[a][:, :], work[a][:, :, 0:1], "rstd")

            def low_of_x(i, a, k):
                pool.drain()
                pool.wait_ge(sem["x_high"][a], nth("x_high", i))
                pool.wait_ge(sem["normed"][a], nth("normed", i))
                nc.gpsimd.tensor_tensor(x3[a][:, :, :, 32:64], xb[a][:, :, :].rearrange("p t (j c) -> p t j c", c=32),
                                        x3[a][:, :, :, 0:32], ALU.subtract).then_inc(sem["x_low"][a], 1)

            def low_of_q(i, a, k):
                pool.drain()
                pool.wait_ge(sem["q_high"][a], nth("q_high", i, k))
                pool.wait_ge(sem["q_full"][a], nth("q_full", i, k))
                nc.gpsimd.tensor_tensor(qs[a][32:64, 2 * k:2 * k + 2, :], qf[a][32:64, 2 * k:2 * k + 2, :],
                                        qs[a][32:64, 2 * k:2 * k + 2, :], ALU.subtract).then_inc(sem["q_low"][a], 1)

            def low_of_k(i, a, k):
                pool.drain()
                pool.wait_ge(sem["k_high"][a], nth("k_high", i, k))
                pool.wait_ge(sem["k_full"][a], nth("k_full", i, k))
                nc.gpsimd.tensor_tensor(kh[a][64:96, 2 * k:2 * k + 2, :], kf[a][64:96, 2 * k:2 * k + 2, :],
                                        kh[a][64:96, 2 * k:2 * k + 2, :], ALU.subtract).then_inc(sem["k_low"][a], 1)

            def residual(i, a, t):
                pool.drain()
                pool.wait_ge(sem["heads"][a], nth("heads", i, t))
                pool.wait_ge(sem["tokens"][a], nth("tokens", i))
                nc.gpsimd.tensor_tensor(h1[a][:, t, :], tok[a][:, t, :], ms[a][:, t, :], ALU.add
                                        ).then_inc(sem["h1"][a], 1)

            def rsqrt_norm(i, a, name):
                pool.drain()
                pool.wait_ge(sem[name][a], nth(name, i, 3))
                rsqrt(i, a, rs2[a], bna[a][:, :, 1], work[a], name + "_rstd")

            def lows_of_norm(i, a, name):
                pool.drain()
                pool.wait_ge(sem[name + "_high"][a], nth(name + "_high", i))
                pool.wait_ge(sem[name][a], nth(name, i, 5))
                nc.gpsimd.tensor_tensor(xs[a][:, :, 256:384], xn[a][:, :, 0:128], xs[a][:, :, 0:128],
                                        ALU.subtract).then_inc(sem[name + "_low"][a], 1)
                nc.gpsimd.tensor_tensor(xs[a][:, :, C:256], xn[a][:, :, 128:C], xs[a][:, :, 128:C],
                                        ALU.subtract).then_inc(sem[name + "_low"][a], 1)

            def norm2(i, a, k):
                lows_of_norm(i, a, "ln2")
                nc.gpsimd.tensor_tensor(h1b[a][:, :, :], h1[a][:, :, :],
                                        bproj_sb[:, :].unsqueeze(1).to_broadcast([TR, 2, C]), ALU.add
                                        ).then_inc(sem["h1_biased"][a], 1)

            def mask_kv(i, a, k):
                pool.drain()
                pool.wait_ge(sem["gelu_kv"][a], nth("gelu_kv", i, 1))
                nc.gpsimd.tensor_tensor(gkvm[a][:, 0:128], gkv[a][:, 0:128], bd_mask[:, 0:128], ALU.mult
                                        ).then_inc(sem["gelu_kv_masked"][a], 1)
                nc.gpsimd.tensor_tensor(gkvm[a][0:64, 128:192], gkv[a][0:64, 128:192], bd_mask[0:64, 128:192],
                                        ALU.mult).then_inc(sem["gelu_kv_masked"][a], 1)

            def residual2(i, a, k):
                pool.drain()
                if later(i):
                    pool.wait_ge(pair_sem["result"], nth("result", i - 1, 1))
                nc.gpsimd.tensor_tensor(hs[:, a, :, :], h2[a][:, :, :],
                                        sbd_sb[:, :].unsqueeze(1).to_broadcast([TR, 2, C]), ALU.add
                                        ).then_inc(sem["h2_biased"][a], 1)

            def low_of_hidden(j, u, k):
                m = ORDER[u]
                n = UNIT_ROWS[m]
                pool.drain()
                pool.wait_ge(pair_sem["hidden_high"], nth("hidden_high", j, u))
                pool.wait_ge(pair_sem["hidden"], nth("hidden", j, u))
                nc.gpsimd.tensor_tensor(hid[0:n, m, 1, :], ub[u % 2][0:n, :], hid[0:n, m, 0, :], ALU.subtract
                                        ).then_inc(pair_sem["hidden_low"], 1)

            walk(pool, dict(VAR=rsqrt_x, N1=low_of_x, Q=low_of_q, K=low_of_k, OT=residual,
                          LN2S=lambda i, a, k: rsqrt_norm(i, a, "ln2"), LN2A=norm2, KVT=mask_kv,
                          LN3S=lambda i, a, k: rsqrt_norm(i, a, "ln3"),
                          LN3A=lambda i, a, k: lows_of_norm(i, a, "ln3"), HS=residual2,
                            SPLIT=low_of_hidden))

        @block.scalar
        def _(act):
            act.wait_ge(init_done, 1)
            act.wait_ge(consts_in, CONSTS)

            def moments(i, a, k):
                act.wait_ge(sem["MEAN"][a], nth("MEAN", i))
                nc.scalar.activation(nmean[a][:, :], ring_bank(("MEAN", a, 0))[0:TR, 0:1], ACT.Copy, scale=-1.0
                                     ).then_inc(sem["neg_mean"][a], 1)
                act.wait_ge(sem["neg_mean"][a], nth("neg_mean", i))
                for t in range(2):
                    n = LIVE[t]
                    nc.scalar.activation(xa[a][0:n, t, :], tok[a][0:n, t, :], ACT.Square,
                                         bias=nmean[a][0:n, :], accum_out=sq[a][0:n, t:t + 1]
                                         ).then_inc(sem["squares"][a], 1)

            def high_of_x(i, a, k):
                act.wait_ge(sem["normed"][a], nth("normed", i))
                nc.scalar.activation(x3[a][:, :, :, 0:32], xb[a][:, :, :].rearrange("p t (j c) -> p t j c", c=32),
                                     ACT.Copy).then_inc(sem["x_high"][a], 1)

            def x_out(i, a, k):
                act.wait_ge(sem["XT"][a], nth("XT", i))
                nc.scalar.activation(xt[a][:, :, :], turned(("XT", a, 0)), ACT.Copy).then_inc(sem["x_turned"][a], 1)

            def turned(step):
                return ring_bank(step)[:, 0:300].bitcast(F16).rearrange("p (b n) -> p b n", b=3)

            def high_of_q(i, a, k):
                act.wait_ge(sem["q_full"][a], nth("q_full", i, k))
                nc.scalar.activation(qs[a][0:96, 2 * k:2 * k + 2, :], qf[a][0:96, 2 * k:2 * k + 2, :], ACT.Copy
                                     ).then_inc(sem["q_high"][a], 1)

            def high_of_k(i, a, k):
                act.wait_ge(sem["k_full"][a], nth("k_full", i, k))
                nc.scalar.activation(kh[a][:, 2 * k:2 * k + 2, :], kf[a][0:96, 2 * k:2 * k + 2, :], ACT.Copy
                                     ).then_inc(sem["k_high"][a], 1)

            def exponents(i, a, h):
                act.wait_ge(sem["S2"][a], nth("S2", i, h))
                if a == 1:
                    act.wait_ge(sem["PV"][0], nth("PV", i, h // 4))
                else:
                    if later(i):
                        act.wait_ge(sem["PV"][1], nth("PV", i - 1, h // 4))
                nc.scalar.activation(probs[0:TR, h, :, :],
                                     ring_bank(("S2", a, h))[0:TR, 0:2 * TC].rearrange("p (t n) -> p t n", t=2),
                                     ACT.Exp, scale=DH ** -0.5).then_inc(sem["probs"][a], 1)

            def heads_out(i, a, g):
                act.wait_ge(sem["PV"][a], nth("PV", i, g))
                nc.scalar.activation(ots[a][:, g, :], ring_bank(("PV", a, g))[:, 0:TC], ACT.Copy
                                     ).then_inc(sem["heads_out"][a], 1)

            def highs_of_norm(i, a, name):
                act.wait_ge(sem[name][a], nth(name, i, 5))
                nc.scalar.activation(xs[a][:, :, 0:C], xn[a][:, :, :], ACT.Copy
                                     ).then_inc(sem[name + "_high"][a], 1)

            def x2_out(i, a, k):
                act.wait_ge(sem["XT2"][a], nth("XT2", i))
                nc.scalar.activation(xt2[a][:, :, :], turned(("XT2", a, 0)), ACT.Copy
                                     ).then_inc(sem["x2_turned"][a], 1)

            def kv_out(i, a, t):
                act.wait_ge(sem["KV"][a], nth("KV", i, t))
                nc.scalar.activation(kv[a][:, t, :], ring_bank(("KV", a, t))[0:TR, 0:2 * C], ACT.Copy
                                     ).then_inc(sem["kv"][a], 1)

            def gelu_q(i, a, k):
                b = ring_bank(("LQ", a, 0))
                act.wait_ge(sem["LQ"][a], nth("LQ", i))
                nc.scalar.activation(gq[a][:, 0, :], b[:, 0:TC], ACT.Gelu).then_inc(sem["gelu_q"][a], 1)
                nc.scalar.activation(gq[a][0:64, 1, :], b[0:64, TC:2 * TC], ACT.Gelu).then_inc(sem["gelu_q"][a], 1)

            def gelu_kv(i, a, k):
                b = ring_bank(("KVT", a, 0))
                act.wait_ge(sem["KVT"][a], nth("KVT", i))
                nc.scalar.activation(gkv[a][:, 0:128], b[:, 0:128], ACT.Gelu, scale=DH ** -0.5
                                     ).then_inc(sem["gelu_kv"][a], 1)
                nc.scalar.activation(gkv[a][0:64, 128:192], b[0:64, 128:192], ACT.Gelu, scale=DH ** -0.5
                                     ).then_inc(sem["gelu_kv"][a], 1)

            def x3_out(i, a, k):
                act.wait_ge(sem["XT3"][a], nth("XT3", i))
                if later(i):
                    act.wait_ge(pair_sem["U"], nth("U", i - 1, UNITS - 1))
                nc.scalar.activation(xp[:, :, a * TC:(a + 1) * TC], turned(("XT3", a, 0)), ACT.Copy
                                     ).then_inc(sem["x3_turned"][a], 1)

            def router_exp(i, a, k):
                if k > 0:
                    return
                act.wait_ge(pair_sem["router"], nth("router", i, 0))
                nc.scalar.activation(ez[:, :, :], z[:, :, :], ACT.Exp, scale=-1.0).then_inc(pair_sem["router_exp"], 1)

            def gate(j, u, k):
                m = ORDER[u]
                n = UNIT_ROWS[m]
                if u >= SHARED_UNITS:
                    act.wait_ge(pair_sem["CB"], nth("CB", j, u - SHARED_UNITS))
                    if u >= SHARED_UNITS + 2:
                        act.wait_ge(pair_sem["gated"], nth("gated", j, u - 2))
                    nc.scalar.activation(cs[u % 2][:, :], bank_c[:, 0:PT], ACT.Copy, scale=0.5
                                         ).then_inc(pair_sem["gate_copied"], 1)
                act.wait_ge(pair_sem["G"], nth("G", j, u))
                if u >= 2:
                    act.wait_ge(pair_sem["hidden"], nth("hidden", j, u - 2))
                nc.scalar.activation(th[u % 2][0:n, :], bank_g[0:n, 0:PT], ACT.Tanh, scale=0.5,
                                     bias=half_gbias[0:n, m:m + 1]).then_inc(pair_sem["tanh"], 1)

            def high_of_hidden(j, u, k):
                m = ORDER[u]
                n = UNIT_ROWS[m]
                act.wait_ge(pair_sem["hidden"], nth("hidden", j, u))
                if later(j):
                    act.wait_ge(pair_sem["DN"], nth("DN", j - 1, 3))
                nc.scalar.activation(hid[0:n, m, 0, :], ub[u % 2][0:n, :], ACT.Copy
                                     ).then_inc(pair_sem["hidden_high"], 1)

            walk(act, dict(MEAN=moments, N1=high_of_x, XT=x_out, Q=high_of_q, K=high_of_k, S2=exponents,
                          PV=heads_out, LN2A=lambda i, a, k: highs_of_norm(i, a, "ln2"), XT2=x2_out,
                          KV=kv_out, LQ=gelu_q, KVT=gelu_kv, LN3A=lambda i, a, k: highs_of_norm(i, a, "ln3"),
                          XT3=x3_out, ROUTE=router_exp, G=gate, SPLIT=high_of_hidden))

        @block.vector
        def _(dve):
            chain = [0]

            def link(ins):
                chain[0] += 1
                ins.then_inc(init_chain, 1)
                dve.wait_ge(init_chain, chain[0])

            for n, (full, high, low, _) in enumerate(staged):
                dve.wait_ge(stage_in[n], 16)
                link(nc.vector.tensor_copy(high, full))
                link(nc.vector.tensor_tensor(low, full, high, ALU.subtract))
            dve.wait_ge(consts_in, CONSTS)
            dve.wait_ge(pool_init, 5)
            link(nc.vector.tensor_copy(gbd_high[:, :], gbd_sb[:, :]))
            link(nc.vector.tensor_tensor(gbd_low[:, :], gbd_sb[:, :], gbd_high[:, :], ALU.subtract))
            link(nc.vector.tensor_scalar(half_gbias[:, :], gbias[:, :], 0.5, None, ALU.mult))
            nc.vector.tensor_tensor(table[:, :, :], table[:, :, :], tok_add_sb[:, :, :], ALU.add
                                    ).then_inc(init_done, 1)
            dve.wait_ge(init_done, 1)

            def tokens(i, a, k):
                dve.wait_ge(sem["EM"][a], nth("EM", i))
                nc.vector.tensor_tensor(tok[a][:, :, :], ring_bank(("EM", a, 0))[0:TR, 0:2 * C].rearrange(
                    "p (t c) -> p t c", t=2), table[:, :, :], ALU.add).then_inc(sem["tokens"][a], 1)
                dve.wait_ge(sem["tokens"][a], nth("tokens", i))
                nc.vector.tensor_reduce(rsum[a][:, :], tok[a][:, :, :], AX.X, ALU.add
                                        ).then_inc(sem["row_sums"][a], 1)

            def centre(i, a, k):
                dve.wait_ge(sem["VAR"][a], nth("VAR", i))
                nc.vector.tensor_copy(var[a][:, :], ring_bank(("VAR", a, 0))[0:TR, 0:1]).then_inc(sem["variance"][a], 1)
                dve.wait_ge(sem["neg_mean"][a], nth("neg_mean", i))
                nc.vector.scalar_tensor_tensor(out=xa[a][:, :, :], in0=tok[a][:, :, :], scalar=nmean[a][:, 0:1],
                                               in1=lnw_sb[:, :, :], op0=ALU.add, op1=ALU.mult
                                               ).then_inc(sem["centred"][a], 1)

            def normalise(i, a, k):
                dve.wait_ge(sem["centred"][a], nth("centred", i))
                dve.wait_ge(sem["rstd"][a], nth("rstd", i, RSQRT_STEPS - 1))
                nc.vector.scalar_tensor_tensor(out=xb[a][:, :, :], in0=xa[a][:, :, :], scalar=rstd[a][:, 0:1],
                                               in1=lnb_sb[:, :, :], op0=ALU.mult, op1=ALU.add
                                               ).then_inc(sem["normed"][a], 1)

            def biased(full, bias, stage, name):
                def part(i, a, k):
                    dve.wait_ge(sem[stage][a], nth(stage, i, k))
                    nc.vector.tensor_tensor(full[a][0:96, 2 * k:2 * k + 2, :],
                                            ring_bank((stage, a, k))[0:96, 0:2 * TC].rearrange("p (j n) -> p j n", j=2),
                                            bias[:, 2 * k:2 * k + 2].unsqueeze(2).to_broadcast([96, 2, TC]), ALU.add
                                            ).then_inc(sem[name][a], 1)
                return part

            def keys(i, a, k):
                dve.wait_ge(sem["q_low"][a], nth("q_low", i, k))
                dve.wait_ge(sem["q_high"][a], nth("q_high", i, k))
                biased(kf, bk_sb, "K", "k_full")(i, a, k)
                if k >= 1:
                    mask_keys(i, a, k - 1)

            def mask_keys(i, a, k):
                dve.wait_ge(sem["k_low"][a], nth("k_low", i, k))
                dve.wait_ge(sem["k_high"][a], nth("k_high", i, k))
                for odd in range(2):
                    nc.vector.tensor_scalar(ks[a][0:96, 4 * k + odd:4 * k + 4:2, :], kh[a][:, 2 * k:2 * k + 2, :],
                                            head_mask[0:96, odd:odd + 1], None, ALU.mult
                                            ).then_inc(sem["k_masked"][a], 1)

            def values(i, a, k):
                mask_keys(i, a, 2)
                dve.wait_ge(sem["V"][a], nth("V", i))
                nc.vector.tensor_tensor(vp[a][:, :, :, 0:16],
                                        ring_bank(("V", a, 0))[0:TR, 0:2 * C].rearrange("p (t h d) -> p t h d", t=2, d=DH),
                                        bv_sb[:, :].rearrange("p (h d) -> p h d", d=DH).unsqueeze(1)
                                        .to_broadcast([TR, 2, HEADS, DH]), ALU.add).then_inc(sem["v_made"][a], 1)

            def row_max(i, a, k):
                t, hp = divmod(k, 6)
                dve.wait_ge(sem["S1"][a], nth("S1", i, k))
                nc.vector.tensor_reduce(mx[a][:, t, 2 * hp:2 * hp + 2],
                                        ring_bank(("S1", a, k))[0:TR, 0:2 * TC].rearrange("p (x n) -> p x n", x=2)[:, :, 0:SEQ],
                                        AX.X, ALU.max).then_inc(sem["row_max"][a], 1)

            def max_out(i, a, k):
                dve.wait_ge(sem["MT"][a], nth("MT", i))
                nc.vector.tensor_copy(qs[a][96:96 + HEADS, :, :],
                                      ring_bank(("MT", a, 0))[0:HEADS, 0:TR].bitcast(F16).unsqueeze(1)
                                      .to_broadcast([HEADS, 6, TC])).then_inc(sem["max_turned"][a], 1)

            def divide(i, a, t):
                b = ring_bank(("OT", a, t))[0:TR, 0:384].rearrange("p (h d) -> p h d", d=32)
                dve.wait_ge(sem["OT"][a], nth("OT", i, t))
                nc.vector.reciprocal(rec[a][:, t, :], b[:, :, 16]).then_inc(sem["recip"][a], 1)
                dve.wait_ge(sem["recip"][a], nth("recip", i, t))
                nc.vector.tensor_tensor(ms[a][:, t, :].rearrange("p (h d) -> p h d", d=DH), b[:, :, 0:16],
                                        rec[a][:, t, :].unsqueeze(2).to_broadcast([TR, HEADS, DH]), ALU.mult
                                        ).then_inc(sem["heads"][a], 1)

            def statistics(i, a, src, name):
                for t in range(2):
                    nc.vector.bn_stats(bns[a][:, t, :], src[a][:, t, :]).then_inc(sem[name][a], 1)
                dve.drain()
                for t in range(2):
                    nc.vector.bn_aggr(bna[a][:, t, :], bns[a][:, t, :]).then_inc(sem[name][a], 1)

            def standardise(i, a, src, name):
                dve.wait_ge(sem[name + "_rstd"][a], nth(name + "_rstd", i, RSQRT_STEPS - 1))
                for t in range(2):
                    nc.vector.tensor_scalar(xn[a][:, t, :], src[a][:, t, :], bna[a][:, t, 0:1], rs2[a][:, t:t + 1],
                                            ALU.subtract, ALU.mult).then_inc(sem[name][a], 1)

            def statistics2(i, a, k):
                dve.wait_ge(sem["h1"][a], nth("h1", i, 1))
                statistics(i, a, h1, "ln2")

            def standardise2(i, a, k):
                standardise(i, a, h1, "ln2")

            def proj_out(i, a, k):
                b = ring_bank(("GW", a, 0))
                dve.wait_ge(sem["GW"][a], nth("GW", i))
                nc.vector.tensor_copy(gw[a][:, 0, :], b[:, 0:C]).then_inc(sem["kv_proj"][a], 1)
                nc.vector.tensor_copy(gw[a][0:64, 1, :], b[0:64, C:2 * C]).then_inc(sem["kv_proj"][a], 1)

            def y_out(i, a, k):
                dve.wait_ge(sem["Y"][a], nth("Y", i))
                dve.wait_ge(sem["h1_biased"][a], nth("h1_biased", i))
                nc.vector.tensor_tensor(h2[a][:, :, :], ring_bank(("Y", a, 0))[0:TR, 0:2 * C].rearrange(
                    "p (t c) -> p t c", t=2), h1b[a][:, :, :], ALU.add).then_inc(sem["h2"][a], 1)

            def statistics3(i, a, k):
                dve.wait_ge(sem["h2"][a], nth("h2", i))
                statistics(i, a, h2, "ln3")

            def standardise3(i, a, k):
                standardise(i, a, h2, "ln3")

            def all4(ap):
                return ap.unsqueeze(1).to_broadcast([TR, 4, EXPERTS])

            def router_logits(i, a, k):
                dve.wait_ge(pair_sem["RT"], nth("RT", i))
                nc.vector.tensor_tensor(z[:, :, :], ring_bank(("RT", None, 0))[0:TR, 0:4 * EXPERTS].rearrange(
                    "p (q e) -> p q e", q=4), all4(rb_sb[:, :]), ALU.add).then_inc(pair_sem["router"], 1)

            def step(ins):
                ins.then_inc(pair_sem["router"], 1)
                dve.drain()

            def route(i, a, k):
                (route_scores, rank_groups, pick_experts, weigh_experts)[k](i)

            def route_scores(i):
                dve.wait_ge(pair_sem["router_exp"], nth("router_exp", i))
                step(nc.vector.tensor_scalar(s1[:, :, :], ez[:, :, :], 1.0, None, ALU.add))
                step(nc.vector.reciprocal(score[:, :, :], s1[:, :, :]))
                step(nc.vector.tensor_tensor(sf[:, :, :], score[:, :, :], all4(corr_sb[:, :]), ALU.add))
                g4 = sf[:, :, :].rearrange("p q (g e) -> p (q g) e", e=4)
                step(nc.vector.tensor_tensor(psum2[:, :, 0:3], g4[:, :, 0:3], g4[:, :, 1:4], ALU.add))
                step(nc.vector.tensor_tensor(psum2[:, :, 3:5], g4[:, :, 0:2], g4[:, :, 2:4], ALU.add))
                step(nc.vector.tensor_tensor(psum2[:, :, 5:6], g4[:, :, 0:1], g4[:, :, 3:4], ALU.add))
                step(nc.vector.tensor_reduce(gs[:, :], psum2[:, :, :], AX.X, ALU.max))

            def rank_groups(i):
                other = gs[:, :].rearrange("p (q g) -> p q g", g=4).unsqueeze(2).to_broadcast([TR, 4, 4, 4])
                own = gs[:, :].rearrange("p (q g) -> p q g", g=4).unsqueeze(3).to_broadcast([TR, 4, 4, 4])
                step(nc.vector.tensor_tensor(gt[:, :, :, :], other, own, ALU.is_gt))
                step(nc.vector.tensor_tensor(eq[:, :, :, :], other, own, ALU.is_equal))
                step(nc.vector.tensor_tensor(eql[:, :, :, :].rearrange("p q g h -> p q (g h)"),
                                             eq[:, :, :, :].rearrange("p q g h -> p q (g h)"),
                                             all4(before[0:TR, :]), ALU.mult))
                step(nc.vector.tensor_tensor(beats[:, :, :, :], gt[:, :, :, :], eql[:, :, :, :], ALU.add))
                step(nc.vector.tensor_reduce(rank[:, :], beats[:, :, :, :].rearrange("p q g h -> p (q g) h"),
                                             AX.X, ALU.add))
                step(nc.vector.tensor_scalar(keep[:, :], rank[:, :], 1.5, None, ALU.is_lt))
                step(nc.vector.tensor_tensor(sm[:, :, 0:16].rearrange("p q (g e) -> p q g e", e=4),
                                             sf[:, :, :].rearrange("p q (g e) -> p q g e", e=4),
                                             keep[:, :].rearrange("p (q g) -> p q g", g=4).unsqueeze(3)
                                             .to_broadcast([TR, 4, 4, 4]), ALU.mult))

            def pick_experts(i):
                for q in range(4):
                    step(nc.vector.max(top8[:, q, :], sm[:, q, :]))
                step(nc.vector.memset(top8[:, :, 4:8], SENTINEL))
                for q in range(4):
                    step(nc.vector.match_replace(mr[:, q, :], top8[:, q, :], sm[:, q, :], TAKEN))

            def weigh_experts(i):
                step(nc.vector.scalar_tensor_tensor(out=wsel[:, :, :], in0=mr[:, :, 0:16], scalar=-2.0e38,
                                                    in1=score[:, :, :], op0=ALU.is_lt, op1=ALU.mult))
                step(nc.vector.tensor_reduce(den[:, :], wsel[:, :, :], AX.X, ALU.add))
                step(nc.vector.tensor_scalar(den1[:, :], den[:, :], 1e-20, None, ALU.add))
                step(nc.vector.reciprocal(rden[:, :], den1[:, :]))
                step(nc.vector.tensor_tensor(gates[:, :, :], wsel[:, :, :],
                                             rden[:, :].unsqueeze(2).to_broadcast([TR, 4, EXPERTS]), ALU.mult))
                step(nc.vector.tensor_scalar(gates_hl[:, :, 0:16], gates[:, :, :], 2.5, None, ALU.mult))
                step(nc.vector.scalar_tensor_tensor(out=gates_hl[:, :, 16:32], in0=gates[:, :, :], scalar=2.5,
                                                    in1=gates_hl[:, :, 0:16], op0=ALU.mult, op1=ALU.subtract))

            def gates_out(i, a, k):
                dve.wait_ge(pair_sem["CT"], nth("CT", i))
                if later(i):
                    dve.wait_ge(pair_sem["DN"], nth("DN", i - 1, 3))
                nc.vector.tensor_copy(ct[:, :], ring_bank(("CT", None, 0))[0:32, 0:TC].bitcast(F16)
                                      ).then_inc(pair_sem["gates_turned"], 1)

            def gated(j, u, k):
                m = ORDER[u]
                n = UNIT_ROWS[m]
                dve.wait_ge(pair_sem["tanh"], nth("tanh", j, u))
                if u >= 2:
                    dve.wait_ge(pair_sem["hidden_low"], nth("hidden_low", j, u - 2))
                elif later(j):
                    dve.wait_ge(pair_sem["hidden_low"], nth("hidden_low", j - 1, UNITS - 2 + u))
                if u >= SHARED_UNITS:
                    dve.wait_ge(pair_sem["gate_copied"], nth("gate_copied", j, u - SHARED_UNITS))
                    nc.vector.scalar_tensor_tensor(out=ga[u % 2][0:n, :], in0=bank_g[0:n, 0:PT],
                                                   scalar=gbias[0:n, m:m + 1], in1=cs[u % 2][0:n, :],
                                                   op0=ALU.add, op1=ALU.mult).then_inc(pair_sem["gated"], 1)
                else:
                    nc.vector.tensor_scalar(ga[u % 2][0:n, :], bank_g[0:n, 0:PT], gbias[0:n, m:m + 1], 0.5,
                                            ALU.add, ALU.mult).then_inc(pair_sem["gated"], 1)

            def hidden_before(j, u, k):
                if u >= 1:
                    hidden(j, u - 1)

            def hidden_last(j, a, k):
                hidden(j, UNITS - 1)

            def hidden(j, u):
                m = ORDER[u]
                n = UNIT_ROWS[m]
                dve.wait_ge(pair_sem["U"], nth("U", j, u))
                dve.wait_ge(pair_sem["gated"], nth("gated", j, u))
                nc.vector.scalar_tensor_tensor(out=ub[u % 2][0:n, :], in0=bank_u[0:n, 0:PT],
                                               scalar=ubias[0:n, m:m + 1], in1=ga[u % 2][0:n, :],
                                               op0=ALU.add, op1=ALU.mult).then_inc(pair_sem["upped"], 1)
                dve.wait_ge(pair_sem["upped"], nth("upped", j, u))
                nc.vector.scalar_tensor_tensor(out=ub[u % 2][0:n, :], in0=th[u % 2][0:n, :], scalar=1.0,
                                               in1=ub[u % 2][0:n, :], op0=ALU.add, op1=ALU.mult
                                               ).then_inc(pair_sem["hidden"], 1)

            def result(j, q, part):
                a, t = divmod(q, 2)
                if t == 0 or part < 3:
                    return
                dve.wait_ge(pair_sem["DN"], nth("DN", j, q))
                if a == 0 and later(j):
                    dve.wait_ge(pair_sem["stored"], 16 * j)
                dve.wait_ge(sem["h2_biased"][a], nth("h2_biased", j))
                nc.vector.tensor_tensor(res[:, a, :, :], bank_d[0:TR, 0:2 * C].rearrange("p (t c) -> p t c", t=2),
                                        hs[:, a, :, :], ALU.add).then_inc(pair_sem["result"], 1)

            walk(dve, dict(EM_END=tokens, VAR=centre, N1=normalise, Q=biased(qf, bq_sb, "Q", "q_full"), K=keys, V=values,
                          S1=row_max, MT=max_out, OT=divide, LN2S=statistics2, LN2A=standardise2,
                          GW=proj_out, Y=y_out, LN3S=statistics3, LN3A=standardise3, RT=router_logits,
                          ROUTE=route, CT=gates_out, G=hidden_before, U=gated, HL=hidden_last, DN=result))

        @block.tensor
        def _(pe):
            mm = nc.tensor.matmul
            pe.wait_ge(init_done, 1)
            pe.wait_ge(consts_in, CONSTS)

            def dense(dst, stationary, moving, columns=None):
                for n, (blk, w, row) in enumerate(((0, w_high, 0), (1, w_high, 0), (0, w_low, 0),
                                                   (2, w_high, 1), (2, w_low, 1))):
                    last = mm(dst, stationary(blk, w, row), moving(blk, w, row), start=n == 0, stop=n == 4)
                return last

            def embed(i, a, t):
                step = ("EM", a, 0)
                if t == 0:
                    pe.wait_ge(pair_sem["loaded"], 16 * (i + 1))
                    if ring_wait(step, i):
                        pe.wait_ge(ring_reader(step, i), ring_count(step, i))
                for c in range(CIN):
                    last = mm(ring_bank(step)[0:TR, t * C:(t + 1) * C], xin[:, c, a, t * TR:(t + 1) * TR],
                              wp_sb[:, c, :], start=c == 0, stop=c == CIN - 1)
                if t == 1:
                    last.then_inc(sem["EM"][a], 1)

            def moment(stage, source, made, k_made):
                def part(i, a, k):
                    step = (stage, a, 0)
                    pe.wait_ge(sem[made][a], nth(made, i, k_made))
                    if ring_wait(step, i):
                        pe.wait_ge(ring_reader(step, i), ring_count(step, i))
                    for t in range(2):
                        n = LIVE[t]
                        last = mm(ring_bank(step)[0:TR, 0:1], mean_w[0:n, :], source[a][0:n, t:t + 1],
                                  start=t == 0, stop=t == 1)
                    last.then_inc(sem[stage][a], 1)
                return part

            def turn(dst, src, n_blocks):
                for t in range(2):
                    for b in range(n_blocks):
                        last = nc.tensor.transpose(dst[:, b, t * TR:(t + 1) * TR], src(t, b), ident16[0:TR, 0:TR])
                return last

            def turned(step):
                return ring_bank(step)[:, 0:300].bitcast(F16).rearrange("p (b n) -> p b n", b=3)

            def turn_x(i, a, k):
                pe.wait_ge(sem["x_low"][a], nth("x_low", i))
                if ring_wait(("XT", a, 0), i):
                    pe.wait_ge(ring_reader(("XT", a, 0), i), ring_count(("XT", a, 0), i))
                turn(turned(("XT", a, 0)),
                     lambda t, b: x3[a][:, t, 2 * b:2 * b + 2, :].rearrange("p j c -> p (j c)"), 3
                     ).then_inc(sem["XT"][a], 1)

            def project(stage, col):
                def part(i, a, k):
                    step = (stage, a, k)
                    pe.wait_ge(sem["x_turned"][a], nth("x_turned", i))
                    if ring_wait(step, i):
                        pe.wait_ge(ring_reader(step, i), ring_count(step, i))
                    for y in range(2):
                        j = 2 * k + y
                        for n, w in enumerate((w_high, w_low)):
                            last = mm(ring_bank(step)[0:96, y * TC:(y + 1) * TC],
                                      w[:, col + 96 * j:col + 96 * j + 96], xt[a][:, j // 2, :],
                                      start=n == 0, stop=n == 1)
                    last.then_inc(sem[stage][a], 1)
                return part

            def project_v(i, a, k):
                step = ("V", a, 0)
                pe.wait_ge(sem["x_turned"][a], nth("x_turned", i))
                if ring_wait(step, i):
                    pe.wait_ge(ring_reader(step, i), ring_count(step, i))
                for t in range(2):
                    for b in range(3):
                        for n, w in enumerate((w_high, w_low)):
                            last = mm(ring_bank(step)[0:TR, t * C + 64 * b:t * C + 64 * b + 64],
                                      xt[a][:, b, t * TR:(t + 1) * TR], w[:, VW + 64 * b:VW + 64 * b + 64],
                                      start=n == 0, stop=n == 1)
                last.then_inc(sem["V"][a], 1)

            def scores(i, a, k):
                step = ("S1", a, k)
                t, hp = divmod(k, 6)
                pe.wait_ge(sem["q_low"][a], nth("q_low", i, hp // 2))
                pe.wait_ge(sem["q_high"][a], nth("q_high", i, hp // 2))
                pe.wait_ge(sem["k_masked"][a], nth("k_masked", i, 2 * (hp // 2) + 1))
                if ring_wait(step, i):
                    pe.wait_ge(ring_reader(step, i), ring_count(step, i))
                for odd in range(2):
                    last = mm(ring_bank(step)[0:TR, odd * TC:odd * TC + SEQ], qs[a][0:96, hp, t * TR:(t + 1) * TR],
                              ks[a][0:96, 2 * hp + odd, 0:SEQ], start=True, stop=True)
                last.then_inc(sem["S1"][a], 1)

            def turn_max(i, a, k):
                step = ("MT", a, 0)
                pe.wait_ge(sem["row_max"][a], nth("row_max", i, 11))
                if ring_wait(step, i):
                    pe.wait_ge(ring_reader(step, i), ring_count(step, i))
                for t in range(2):
                    last = nc.tensor.transpose(ring_bank(step)[0:HEADS, 0:TR].bitcast(F16)[:, t * TR:(t + 1) * TR],
                                               mx[a][:, t, :], ident16[0:TR, 0:TR])
                last.then_inc(sem["MT"][a], 1)

            def scores_less_max(i, a, h):
                step = ("S2", a, h)
                pe.wait_ge(sem["max_turned"][a], nth("max_turned", i))
                if ring_wait(step, i):
                    pe.wait_ge(ring_reader(step, i), ring_count(step, i))
                for t in range(2):
                    last = mm(ring_bank(step)[0:TR, t * TC:(t + 1) * TC], ks[a][:, h, t * TR:(t + 1) * TR],
                              qs[a][:, h // 2, :], start=True, stop=True)
                last.then_inc(sem["S2"][a], 1)

            def attend(i, a, g):
                step = ("PV", a, g)
                pe.wait_ge(sem["v_made"][a], nth("v_made", i))
                if ring_wait(step, i):
                    pe.wait_ge(ring_reader(step, i), ring_count(step, i))
                pe.wait_ge(sem["probs"][a], nth("probs", i, 4 * g + 3))
                for t in range(2):
                    n = LIVE[t]
                    for y in range(4):
                        h = 4 * g + y
                        last = mm(ring_bank(step)[32 * y:32 * y + 32, 0:TC], vp[a][0:n, t, h, :],
                                  probs[0:n, h, t, :], start=t == 0, stop=t == 1,
                                  tile_position=(0, 32 * y))
                last.then_inc(sem["PV"][a], 1)

            def turn_heads(i, a, t):
                step = ("OT", a, t)
                pe.wait_ge(sem["heads_out"][a], nth("heads_out", i, 2))
                if ring_wait(step, i):
                    pe.wait_ge(ring_reader(step, i), ring_count(step, i))
                for g in range(3):
                    last = nc.tensor.transpose(ring_bank(step)[0:TR, 128 * g:128 * g + 128],
                                               ots[a][:, g, t * TR:(t + 1) * TR], ident32)
                last.then_inc(sem["OT"][a], 1)

            def turn_norm(stage, name):
                def part(i, a, k):
                    pe.wait_ge(sem[name + "_low"][a], nth(name + "_low", i, 1))
                    if ring_wait((stage, a, 0), i):
                        pe.wait_ge(ring_reader((stage, a, 0), i), ring_count((stage, a, 0), i))
                    turn(turned((stage, a, 0)), lambda t, b: xs[a][:, t, (0, 256, 128)[b]:(128, 384, 256)[b]], 3
                         ).then_inc(sem[stage][a], 1)
                return part

            def linear_kv(i, a, t):
                step = ("KV", a, t)
                pe.wait_ge(sem["x2_turned"][a], nth("x2_turned", i))
                if ring_wait(step, i):
                    pe.wait_ge(ring_reader(step, i), ring_count(step, i))
                dense(ring_bank(step)[0:TR, 0:2 * C],
                      lambda blk, w, row: xt2[a][:, blk, t * TR:(t + 1) * TR],
                      lambda blk, w, row: w[:, (L0, L1)[row] + C:(L0, L1)[row] + 3 * C]
                      ).then_inc(sem["KV"][a], 1)

            def linear_q(i, a, k):
                step = ("LQ", a, 0)
                pe.wait_ge(sem["x2_turned"][a], nth("x2_turned", i))
                if ring_wait(step, i):
                    pe.wait_ge(ring_reader(step, i), ring_count(step, i))
                for n, (lo, m) in enumerate(((0, 128), (128, 64))):
                    last = dense(ring_bank(step)[0:m, n * TC:(n + 1) * TC],
                                 lambda blk, w, row: w[:, (L0, L1)[row] + lo:(L0, L1)[row] + lo + m],
                                 lambda blk, w, row: xt2[a][:, blk, :])
                last.then_inc(sem["LQ"][a], 1)

            def linear_kv_product(i, a, k):
                step = ("KVT", a, 0)
                pe.wait_ge(sem["kv"][a], nth("kv", i, 1))
                if ring_wait(step, i):
                    pe.wait_ge(ring_reader(step, i), ring_count(step, i))
                for lo, m in ((0, 128), (128, 64)):
                    for t in range(2):
                        n = LIVE[t]
                        last = mm(ring_bank(step)[0:m, lo:lo + m], kv[a][0:n, t, C + lo:C + lo + m],
                                  kv[a][0:n, t, lo:lo + m], start=t == 0, stop=t == 1)
                last.then_inc(sem["KVT"][a], 1)

            def fold_projection(i, a, k):
                step = ("GW", a, 0)
                pe.wait_ge(sem["gelu_kv_masked"][a], nth("gelu_kv_masked", i, 1))
                if ring_wait(step, i):
                    pe.wait_ge(ring_reader(step, i), ring_count(step, i))
                mm(ring_bank(step)[0:128, 0:C], gkvm[a][:, 0:128], wproj_sb[:, 0, :], start=True, stop=True)
                mm(ring_bank(step)[0:64, C:2 * C], gkvm[a][0:64, 128:192], wproj_sb[0:64, 1, :],
                   start=True, stop=True).then_inc(sem["GW"][a], 1)

            def linear_out(i, a, k):
                step = ("Y", a, 0)
                pe.wait_ge(sem["kv_proj"][a], nth("kv_proj", i, 1))
                pe.wait_ge(sem["gelu_q"][a], nth("gelu_q", i, 1))
                if ring_wait(step, i):
                    pe.wait_ge(ring_reader(step, i), ring_count(step, i))
                for t in range(2):
                    mm(ring_bank(step)[0:TR, t * C:(t + 1) * C], gq[a][:, 0, t * TR:(t + 1) * TR], gw[a][:, 0, :],
                       start=True, stop=False)
                    last = mm(ring_bank(step)[0:TR, t * C:(t + 1) * C], gq[a][0:64, 1, t * TR:(t + 1) * TR],
                              gw[a][0:64, 1, :], start=False, stop=True)
                last.then_inc(sem["Y"][a], 1)

            def router(i, a, k):
                step = ("RT", None, 0)
                pe.wait_ge(sem["x3_turned"][0], nth("x3_turned", i))
                pe.wait_ge(sem["x3_turned"][1], nth("x3_turned", i))
                if ring_wait(step, i):
                    pe.wait_ge(ring_reader(step, i), ring_count(step, i))
                for q in range(4):
                    last = dense(ring_bank(step)[0:TR, EXPERTS * q:EXPERTS * (q + 1)],
                                 lambda blk, w, row: xp[:, blk, q * TR:(q + 1) * TR],
                                 lambda blk, w, row: w[:, (R0, R1)[row]:(R0, R1)[row] + EXPERTS])
                last.then_inc(pair_sem["RT"], 1)

            def turn_gates(i, a, k):
                step = ("CT", None, 0)
                pe.wait_ge(pair_sem["router"], nth("router", i, ROUTER_STEPS - 1))
                if ring_wait(step, i):
                    pe.wait_ge(ring_reader(step, i), ring_count(step, i))
                for q in range(4):
                    last = nc.tensor.transpose(ring_bank(step)[0:32, 0:TC].bitcast(F16)[:, q * TR:(q + 1) * TR],
                                               gates_hl[:, q, :], ident16[0:TR, 0:TR])
                last.then_inc(pair_sem["CT"], 1)

            def ffn_up(dst, m, col):
                n = UNIT_ROWS[m]
                lo = col + 128 * m
                return dense(dst[0:n, 0:PT],
                             lambda blk, w, row: w[:, (UP0, UP1)[row] + lo:(UP0, UP1)[row] + lo + n],
                             lambda blk, w, row: xp[:, blk, :])

            def ffn_gate(j, u, k):
                m = ORDER[u]
                if u == 0:
                    pe.wait_ge(sem["x3_turned"][0], nth("x3_turned", j))
                    pe.wait_ge(sem["x3_turned"][1], nth("x3_turned", j))
                    if later(j):
                        pe.wait_ge(pair_sem["gated"], nth("gated", j - 1, UNITS - 1))
                if u >= SHARED_UNITS:
                    if u == SHARED_UNITS:
                        pe.wait_ge(pair_sem["gates_turned"], nth("gates_turned", j))
                    else:
                        pe.wait_ge(pair_sem["gate_copied"], nth("gate_copied", j, u - SHARED_UNITS - 1))
                    mm(bank_c[:, 0:PT], select_sb[:, m, :], ct[:, :], start=True, stop=True).then_inc(pair_sem["CB"], 1)
                if u >= 1:
                    pe.wait_ge(pair_sem["gated"], nth("gated", j, u - 1))
                ffn_up(bank_g, m, 0).then_inc(pair_sem["G"], 1)

            def ffn_value(j, u, k):
                if u >= 1:
                    pe.wait_ge(pair_sem["upped"], nth("upped", j, u - 1))
                elif later(j):
                    pe.wait_ge(pair_sem["upped"], nth("upped", j - 1, UNITS - 1))
                ffn_up(bank_u, ORDER[u], HID).then_inc(pair_sem["U"], 1)

            def ffn_down(j, q, part):
                a, t = divmod(q, 2)
                lo, hi = DOWN_PARTS[part]
                dst = bank_d[0:TR, t * C:(t + 1) * C]
                pe.wait_ge(pair_sem["hidden_low"], nth("hidden_low", j, hi - 1))
                if part == 0:
                    if a == 1:
                        pe.wait_ge(pair_sem["result"], nth("result", j, 0))
                    elif later(j):
                        pe.wait_ge(pair_sem["result"], nth("result", j - 1, 1))
                    mm(dst, ct[:, q * TR:(q + 1) * TR], gbd_high[:, :], start=True, stop=False)
                    mm(dst, ct[:, q * TR:(q + 1) * TR], gbd_low[:, :], start=False, stop=False)
                for u in range(lo, hi):
                    m = ORDER[u]
                    n = UNIT_ROWS[m]
                    high, low = (hid[0:n, m, x, q * TR:(q + 1) * TR] for x in range(2))
                    mm(dst, high, wd_high[0:n, m, :], start=False, stop=False)
                    mm(dst, high, wd_low[0:n, m, :], start=False, stop=False)
                    last = mm(dst, low, wd_high[0:n, m, :], start=False, stop=u == UNITS - 1)
                if part == 3:
                    last.then_inc(pair_sem["DN"], 1)

            walk(pe, dict(EM=lambda i, a, k: embed(i, a, 0), EM_END=lambda i, a, k: embed(i, a, 1), MEAN=moment("MEAN", rsum, "row_sums", 0), VAR=moment("VAR", sq, "squares", 1),
                          XT=turn_x, Q=project("Q", QW), K=project("K", KW), V=project_v, S1=scores, MT=turn_max,
                          S2=scores_less_max, PV=attend, OT=turn_heads, XT2=turn_norm("XT2", "ln2"),
                          KV=linear_kv, LQ=linear_q, KVT=linear_kv_product, GW=fold_projection, Y=linear_out,
                          XT3=turn_norm("XT3", "ln3"), RT=router, CT=turn_gates,
                          G=ffn_gate, U=ffn_value, DN=ffn_down))


def layout(np, pairs, x, L0_tok_W_map, L0_tok_b_map, L0_tok_class_token, L0_tok_ln_w, L0_tok_ln_b, L0_tok_Wq, L0_tok_bq,
           L0_tok_Wk, L0_tok_bk, L0_tok_Wv, L0_tok_bv, L0_attn_w_qkv, L0_attn_w_proj, L0_attn_b_proj,
           L0_ffn_router_w, L0_ffn_router_b, L0_ffn_corr_bias, L0_ffn_gWg, L0_ffn_gbg, L0_ffn_gWu, L0_ffn_gbu,
           L0_ffn_gWd, L0_ffn_gbd, L0_ffn_sWg, L0_ffn_sbg, L0_ffn_sWu, L0_ffn_sbu, L0_ffn_sWd, L0_ffn_sbd):
    f = np.float32
    A = {}
    xt = np.zeros((pairs, 128, CIN, 2, TC), f)
    xt[..., 0:PATCHES] = x.reshape(pairs, 2, PATCHES, CIN, 128).transpose(0, 4, 3, 1, 2)
    A["x"] = xt
    A["w_patch"] = L0_tok_W_map.T.reshape(CIN, 128, C).transpose(1, 0, 2)

    def tokens(rows_of_patches, row_of_class):
        t = np.zeros((TC, C), f)
        t[0:PATCHES] = rows_of_patches
        t[PATCHES] = row_of_class
        return t.reshape(2, TR, C).transpose(1, 0, 2)

    s = np.arange(SEQ, dtype=f)[:, None]
    d = np.arange(C, dtype=f)[None, :]
    even = (np.arange(C) % 2 == 0)[None, :]
    pos = np.where(even, np.sin(s / np.power(f(10000.0), d / f(C))),
                   np.cos(s / np.power(f(10000.0), (d - f(1.0)) / f(C)))).astype(f)
    A["pos"] = tokens(pos[1:], pos[0])
    A["tok_add"] = tokens(L0_tok_b_map, L0_tok_class_token[0])
    A["ln_w"] = tokens(L0_tok_ln_w[1:], L0_tok_ln_w[0])
    A["ln_b"] = tokens(L0_tok_ln_b[1:], L0_tok_ln_b[0])

    W = np.zeros((128, SPLIT), f)

    def twice(w):
        return np.concatenate([w[128:C], w[128:C]], 0)

    def hidden_columns(of_experts, shared):
        return np.concatenate([of_experts.transpose(1, 0, 2).reshape(C, EXPERTS * INNER), shared], 1)

    up = np.concatenate([hidden_columns(L0_ffn_gWg, L0_ffn_sWg), hidden_columns(L0_ffn_gWu, L0_ffn_sWu)], 1)
    W[:, UP0:UP0 + 2 * HID] = up[0:128]
    W[:, UP1:UP1 + 2 * HID] = twice(up)
    for col, w in ((QW, L0_tok_Wq), (KW, L0_tok_Wk)):
        for j in range(6):
            r = 64 * (j % 2)
            for y in range(2):
                for copy in range(3):
                    c0 = col + 96 * j + 32 * copy + 16 * y
                    for half in range(2):
                        r0 = r + 32 * half + 16 * y
                        W[r0:r0 + 16, c0:c0 + 16] = w[2 * j + y].T
    for b in range(3):
        for y in range(4):
            for half in range(2):
                r0 = 64 * (y // 2) + 32 * half + 16 * (y % 2)
                c0 = VW + 64 * b + 16 * y
                W[r0:r0 + 16, c0:c0 + 16] = L0_tok_Wv[4 * b + y].T
    W[:, L0:L0 + 3 * C] = L0_attn_w_qkv[0:128]
    W[:, L1:L1 + 3 * C] = twice(L0_attn_w_qkv)
    W[:, R0:R0 + EXPERTS] = L0_ffn_router_w.T[0:128]
    W[:, R1:R1 + EXPERTS] = twice(L0_ffn_router_w.T)
    A["w_split"] = W
    for name, b in (("bq", L0_tok_bq), ("bk", L0_tok_bk)):
        A[name] = np.concatenate([b.reshape(6, 32).T] * 3, 0)

    def rows(v, n=TR):
        return np.broadcast_to(v.reshape(1, -1), (n, v.size))

    A["bv"] = rows(L0_tok_bv)
    wproj = np.zeros((128, 2, C), f)
    wproj[:, 0] = L0_attn_w_proj[0:128]
    wproj[0:64, 1] = L0_attn_w_proj[128:C]
    A["w_proj"] = wproj
    A["b_proj"] = rows(L0_attn_b_proj)
    A["router_b"] = rows(L0_ffn_router_b)
    A["corr_b"] = rows(L0_ffn_corr_bias)
    wd = np.zeros((UNITS * 128, C), f)
    wd[0:HID] = np.concatenate([L0_ffn_gWd.reshape(EXPERTS * INNER, C), L0_ffn_sWd], 0)
    A["w_down"] = wd.reshape(UNITS, 128, C).transpose(1, 0, 2)
    A["down_b"] = np.concatenate([L0_ffn_gbd, L0_ffn_gbd], 0)
    A["shared_b"] = rows(L0_ffn_sbd)
    for name, of_experts, shared in (("gate_bias", L0_ffn_gbg, L0_ffn_sbg), ("up_bias", L0_ffn_gbu, L0_ffn_sbu)):
        b = np.zeros((UNITS * 128,), f)
        b[0:HID] = np.concatenate([of_experts.reshape(-1), shared], 0)
        A[name] = b.reshape(UNITS, 128).T
    expert = np.arange(ROUTED * 128) // INNER
    sel = (np.arange(EXPERTS)[:, None] == expert[None, :]).astype(np.float16)
    A["select"] = np.concatenate([sel, sel], 0).reshape(32, ROUTED, 128)
    c32 = np.zeros((128, 438), f)
    c32[:, 0:128] = np.eye(128, dtype=f)
    p = np.arange(128)
    c32[:, 128:256] = p[:, None] // DH == p[None, :] // DH
    c32[:, 256:320] = p[:, None] // DH == p[None, 0:64] // DH
    for odd in range(2):
        c32[:, 320 + odd] = (p // DH) % 2 == odd
    c32[:, 322:422] = 1.0 / (SEQ * C)
    g = np.arange(GROUPS)
    c32[:, 422:438] = (g[None, :] < g[:, None]).astype(f).reshape(1, 16)
    A["consts32"] = c32
    c16 = np.zeros((128, 128 + HEADS * TC), np.float16)
    c16[:, 0:128] = np.eye(128, dtype=np.float16)
    for h in range(HEADS):
        c16[96 + h, 128 + TC * h:128 + TC * (h + 1)] = -1.0
    A["consts16"] = c16
    return A


NAMES = ["x", "w_patch", "pos", "tok_add", "ln_w", "ln_b", "w_split", "bq", "bk", "bv", "w_proj", "b_proj",
         "router_b", "corr_b", "w_down", "down_b", "shared_b", "gate_bias", "up_bias", "select",
         "consts32", "consts16"]


def kernel(**inputs):
    import numpy as np
    import concourse.bacc as bacc
    from concourse.bass_utils import run_bass_kernel_spmd

    pairs = inputs["x"].shape[0] // 2
    arrays = {k: np.ascontiguousarray(v) for k, v in
              layout(np, pairs, **{k: np.asarray(v) for k, v in inputs.items()}).items()}
    nc = bacc.Bacc("TRN2", target_bir_lowering=False, num_devices=1)
    args = [nc.dram_tensor(f"in_{n}", arrays[n].shape, mybir.dt.from_np(arrays[n].dtype), kind="ExternalInput").ap()
            for n in NAMES]
    args.append(nc.dram_tensor("out_0", (pairs, TR, 2, 2, C), F32, kind="ExternalOutput").ap())
    vit_tower(nc, *args)
    r = run_bass_kernel_spmd(nc, [{f"in_{n}": arrays[n] for n in NAMES}], core_ids=[0])
    got = np.asarray(r.results[0]["out_0"]).transpose(0, 2, 3, 1, 4).reshape(2 * pairs, TC, C)
    return np.concatenate([got[:, PATCHES:SEQ], got[:, 0:PATCHES]], 1)
```
